# Optimizing a Trainium2 kernel written in Bass

```python
import numpy as np
import jax
import jax.numpy as jnp

def _softmax(x, axis=-1):
    return jax.nn.softmax(x, axis=axis)

def _gelu(x):
    return jax.nn.gelu(x, approximate=True)

def _silu(x):
    return jax.nn.silu(x)

def _sigmoid(x):
    return jax.nn.sigmoid(x)

def _layernorm(x, axis=-1, eps=1e-05):
    m = jnp.mean(x, axis=axis, keepdims=True)
    v = jnp.var(x, axis=axis, keepdims=True)
    return (x - m) / jnp.sqrt(v + eps)

def _scatter_add(tgt, idx, src, axis=0):
    return tgt.at[idx].add(src)

def _segment_sum(src, seg, n):
    return jax.ops.segment_sum(src, seg, n)
kernel_name = 'mk_adaln_d2_jaxref_r8_e407d8'

def setup_inputs(seed: int=0):
    np.random.seed(seed)
    _w = jnp.asarray

    def _L0_attn_setup():
        import jax, jax.numpy as jnp
        import numpy as np
        D_ATTN = 256
        D_STATE = 64
        SHIFT_FRAC = 0.5
        LN_EPS = 1e-05

        def _reference_tuple_inner(x, W_key, W_value, W_output, W_shift, gate, time_decay, time_first, ln_gamma, ln_beta):
            B, T, D = x.shape
            shift_len = max(1, int(T * SHIFT_FRAC))
            x_cat = jnp.roll(x, -shift_len, axis=1)
            g = jax.nn.sigmoid(gate)
            x_shift = jnp.einsum('btd,ed->bte', x_cat, W_shift) * g + x * (1.0 - g)
            mu = jnp.mean(x_shift, axis=-1, keepdims=True)
            var = jnp.var(x_shift, axis=-1, keepdims=True)
            x_norm = (x_shift - mu) * jax.lax.rsqrt(var + LN_EPS) * ln_gamma + ln_beta
            k = jnp.einsum('btd,sd->bts', x_norm, W_key)
            v = jnp.einsum('btd,sd->bts', x_norm, W_value)
            w = jnp.exp(time_decay)
            u = jnp.exp(time_first)
            wkv = jnp.exp(-u * jax.nn.sigmoid(k)) * v

            def step(state, wkv_t):
                state = state * w + wkv_t
                return (state, state)
            init = jnp.zeros((B, k.shape[-1]), x.dtype)
            last_state, states = jax.lax.scan(step, init, jnp.swapaxes(wkv, 0, 1))
            states = jnp.swapaxes(states, 0, 1)
            output = jnp.einsum('bts,ds->btd', states, W_output)
            return (output, jax.lax.stop_gradient(last_state))
        key = jax.random.key(seed)
        ks = jax.random.split(key, 8)
        B, T = (8, 256)
        s_attn = 1.0 / np.sqrt(D_ATTN)
        s_state = 1.0 / np.sqrt(D_STATE)
        x = jax.random.normal(ks[0], (B, T, D_ATTN), jnp.float32)
        W_key = jax.random.normal(ks[1], (D_STATE, D_ATTN), jnp.float32) * s_attn
        W_value = jax.random.normal(ks[2], (D_STATE, D_ATTN), jnp.float32) * s_attn
        W_output = jax.random.normal(ks[3], (D_ATTN, D_STATE), jnp.float32) * s_state
        W_shift = jax.random.normal(ks[4], (D_ATTN, D_ATTN), jnp.float32) * s_attn
        gate = jnp.ones((D_ATTN,), jnp.float32)
        time_decay = -jax.random.uniform(ks[5], (D_STATE,), jnp.float32, 0.05, 1.0)
        time_first = jax.random.normal(ks[6], (D_STATE,), jnp.float32) * 0.1
        ln_gamma = jnp.ones((D_ATTN,), jnp.float32)
        ln_beta = jnp.zeros((D_ATTN,), jnp.float32)
        return dict(x=x, W_key=W_key, W_value=W_value, W_output=W_output, W_shift=W_shift, gate=gate, time_decay=time_decay, time_first=time_first, ln_gamma=ln_gamma, ln_beta=ln_beta)
    _L0_attn_in = _L0_attn_setup()

    def _L0_ffn_setup():
        import jax, jax.numpy as jnp
        import numpy as np
        B, T, D, F, E, K = (2, 128, 256, 96, 16, 2)
        key = jax.random.key(seed)
        k0, k1, k2, k3, k4 = jax.random.split(key, 5)
        scale = 0.02
        return {'x': jax.random.normal(k0, (B, T, D), dtype=jnp.float32), 'router_w': jax.random.normal(k1, (D, E), dtype=jnp.float32) * scale, 'gate_w': jax.random.normal(k2, (E, D, F), dtype=jnp.float32) * scale, 'up_w': jax.random.normal(k3, (E, D, F), dtype=jnp.float32) * scale, 'down_w': jax.random.normal(k4, (E, F, D), dtype=jnp.float32) * scale}
    _L0_ffn_in = _L0_ffn_setup()
    _L0_c = _w((lambda *s: np.random.randn(*s).astype(np.float32) * 0.05)(2, 256))
    _L0_wmod = _w((lambda *s: np.random.randn(*s).astype(np.float32) * 0.05)(256, 6 * 256) * 256 ** (-0.5))

    def _L1_attn_setup():
        import jax, jax.numpy as jnp
        import numpy as np
        D_MODEL = 256
        N_HEADS = 8
        EXPAND_K = 1
        EXPAND_V = 2
        DK = D_MODEL * EXPAND_K // N_HEADS
        DV = D_MODEL * EXPAND_V // N_HEADS
        INTER = 704
        EPS = 1e-06
        CHUNK = 64

        def rmsnorm(x, w, eps=EPS):
            return x * jax.lax.rsqrt(jnp.mean(x * x, axis=-1, keepdims=True) + eps) * w

        def rope(x):
            T, D = (x.shape[1], x.shape[-1])
            inv_freq = 1.0 / 10000.0 ** (jnp.arange(0, D, 2, dtype=jnp.float32) / D)
            ang = jnp.arange(T, dtype=jnp.float32)[:, None] * inv_freq
            cos = jnp.cos(ang)[None, :, None, :]
            sin = jnp.sin(ang)[None, :, None, :]
            x1, x2 = jnp.split(x, 2, axis=-1)
            return jnp.concatenate([x1 * cos - x2 * sin, x2 * cos + x1 * sin], axis=-1)

        def chunk_retention(q, k, v):
            B, T, H, Dk = q.shape
            Dv = v.shape[-1]
            C = CHUNK
            N = T // C
            gamma = 1.0 - jnp.exp2(-5.0 - jnp.arange(H, dtype=jnp.float32))
            i = jnp.arange(C, dtype=jnp.float32)
            diff = i[:, None] - i[None, :]
            Dmask = jnp.where(diff >= 0, gamma[:, None, None] ** diff, 0.0)
            cross_decay = gamma[:, None] ** (i[None, :] + 1.0)
            k_decay = gamma[:, None] ** (C - 1.0 - i[None, :])
            chunk_decay = gamma ** C
            to_chunks = lambda x: jnp.moveaxis(x.reshape(B, N, C, H, x.shape[-1]).transpose(0, 1, 3, 2, 4), 1, 0)
            qc, kc, vc = (to_chunks(q), to_chunks(k), to_chunks(v))

            def body(S, inp):
                qb, kb, vb = inp
                attn = jnp.einsum('bhid,bhjd->bhij', qb, kb) * Dmask
                o_intra = jnp.einsum('bhij,bhje->bhie', attn, vb)
                o_cross = jnp.einsum('bhid,bhde->bhie', qb * cross_decay[None, :, :, None], S)
                S = chunk_decay[None, :, None, None] * S + jnp.einsum('bhid,bhie->bhde', kb * k_decay[None, :, :, None], vb)
                return (S, o_intra + o_cross)
            S0 = jnp.zeros((B, H, Dk, Dv), q.dtype)
            _, o = jax.lax.scan(body, S0, (qc, kc, vc))
            return jnp.moveaxis(o, 0, 1).transpose(0, 1, 3, 2, 4).reshape(B, T, H, Dv)
        key = jax.random.key(seed)
        ks = jax.random.split(key, 12)
        d = D_MODEL
        s = lambda fan_in: 1.0 / np.sqrt(fan_in)
        return {'hidden_states': jax.random.normal(ks[0], (2, 256, d), jnp.float32), 'attn_norm_w': jnp.ones((d,), jnp.float32), 'q_w': jax.random.normal(ks[1], (d, d * EXPAND_K), jnp.float32) * s(d), 'k_w': jax.random.normal(ks[2], (d, d * EXPAND_K), jnp.float32) * s(d), 'v_w': jax.random.normal(ks[3], (d, d * EXPAND_V), jnp.float32) * s(d), 'g_w': jax.random.normal(ks[4], (d, d * EXPAND_V), jnp.float32) * s(d), 'o_w': jax.random.normal(ks[5], (d * EXPAND_V, d), jnp.float32) * s(d * EXPAND_V), 'gnorm_w': jnp.ones((DV,), jnp.float32), 'mlp_norm_w': jnp.ones((d,), jnp.float32), 'gate_w': jax.random.normal(ks[6], (d, INTER * 2), jnp.float32) * s(d), 'down_w': jax.random.normal(ks[7], (INTER, d), jnp.float32) * s(INTER)}
    _L1_attn_in = _L1_attn_setup()

    def _L1_ffn_setup():
        import jax, jax.numpy as jnp
        import numpy as np
        DIM = 256
        HID = 704
        ZERO_POINT = 128.0

        def _qlinear(x, wq, scale):
            W = (wq.astype(jnp.float32) - ZERO_POINT) * scale[:, None]
            return jnp.einsum('bsd,hd->bsh', x, W)
        key = jax.random.key(seed)
        ks = jax.random.split(key, 7)
        B, S = (4, 256)
        sg = jax.random.uniform(ks[1], (HID,)) * (0.02 / np.sqrt(DIM)) + 0.0001
        su = jax.random.uniform(ks[3], (HID,)) * (0.02 / np.sqrt(DIM)) + 0.0001
        sd = jax.random.uniform(ks[5], (DIM,)) * (0.02 / np.sqrt(HID)) + 0.0001
        return {'x': jax.random.normal(ks[0], (B, S, DIM), dtype=jnp.float32), 'wq_gate': jax.random.randint(ks[2], (HID, DIM), 0, 32, dtype=jnp.int32), 's_gate': sg, 'wq_up': jax.random.randint(ks[4], (HID, DIM), 0, 32, dtype=jnp.int32), 's_up': su, 'wq_down': jax.random.randint(ks[6], (DIM, HID), 0, 32, dtype=jnp.int32), 's_down': sd}
    _L1_ffn_in = _L1_ffn_setup()
    _L1_c = _w((lambda *s: np.random.randn(*s).astype(np.float32) * 0.05)(2, 256))
    _L1_wmod = _w((lambda *s: np.random.randn(*s).astype(np.float32) * 0.05)(256, 6 * 256) * 256 ** (-0.5))
    _d = {'L0_attn_x': _L0_attn_in['x'], 'L0_attn_W_key': _L0_attn_in['W_key'], 'L0_attn_W_value': _L0_attn_in['W_value'], 'L0_attn_W_output': _L0_attn_in['W_output'], 'L0_attn_W_shift': _L0_attn_in['W_shift'], 'L0_attn_gate': _L0_attn_in['gate'], 'L0_attn_time_decay': _L0_attn_in['time_decay'], 'L0_attn_time_first': _L0_attn_in['time_first'], 'L0_attn_ln_gamma': _L0_attn_in['ln_gamma'], 'L0_attn_ln_beta': _L0_attn_in['ln_beta'], 'L0_ffn_router_w': _L0_ffn_in['router_w'], 'L0_ffn_gate_w': _L0_ffn_in['gate_w'], 'L0_ffn_up_w': _L0_ffn_in['up_w'], 'L0_ffn_down_w': _L0_ffn_in['down_w'], 'L0_c': _L0_c, 'L0_wmod': _L0_wmod, 'L1_attn_attn_norm_w': _L1_attn_in['attn_norm_w'], 'L1_attn_q_w': _L1_attn_in['q_w'], 'L1_attn_k_w': _L1_attn_in['k_w'], 'L1_attn_v_w': _L1_attn_in['v_w'], 'L1_attn_g_w': _L1_attn_in['g_w'], 'L1_attn_o_w': _L1_attn_in['o_w'], 'L1_attn_gnorm_w': _L1_attn_in['gnorm_w'], 'L1_attn_mlp_norm_w': _L1_attn_in['mlp_norm_w'], 'L1_attn_gate_w': _L1_attn_in['gate_w'], 'L1_attn_down_w': _L1_attn_in['down_w'], 'L1_ffn_wq_gate': _L1_ffn_in['wq_gate'], 'L1_ffn_s_gate': _L1_ffn_in['s_gate'], 'L1_ffn_wq_up': _L1_ffn_in['wq_up'], 'L1_ffn_s_up': _L1_ffn_in['s_up'], 'L1_ffn_wq_down': _L1_ffn_in['wq_down'], 'L1_ffn_s_down': _L1_ffn_in['s_down'], 'L1_c': _L1_c, 'L1_wmod': _L1_wmod}
    _x0 = _d['L0_attn_x']
    _d['L0_attn_x'] = jax.random.normal(jax.random.fold_in(jax.random.key(seed), 1), (2, 1024, 256), dtype=_x0.dtype)
    del _x0
    return _d

def reference(L0_attn_x, L0_attn_W_key, L0_attn_W_value, L0_attn_W_output, L0_attn_W_shift, L0_attn_gate, L0_attn_time_decay, L0_attn_time_first, L0_attn_ln_gamma, L0_attn_ln_beta, L0_ffn_router_w, L0_ffn_gate_w, L0_ffn_up_w, L0_ffn_down_w, L0_c, L0_wmod, L1_attn_attn_norm_w, L1_attn_q_w, L1_attn_k_w, L1_attn_v_w, L1_attn_g_w, L1_attn_o_w, L1_attn_gnorm_w, L1_attn_mlp_norm_w, L1_attn_gate_w, L1_attn_down_w, L1_ffn_wq_gate, L1_ffn_s_gate, L1_ffn_wq_up, L1_ffn_s_up, L1_ffn_wq_down, L1_ffn_s_down, L1_c, L1_wmod):

    def _L0_attn_ref(x, W_key, W_value, W_output, W_shift, gate, time_decay, time_first, ln_gamma, ln_beta):
        import jax, jax.numpy as jnp
        import numpy as np
        D_ATTN = 256
        D_STATE = 64
        SHIFT_FRAC = 0.5
        LN_EPS = 1e-05

        def _reference_tuple_inner(x, W_key, W_value, W_output, W_shift, gate, time_decay, time_first, ln_gamma, ln_beta):
            B, T, D = x.shape
            shift_len = max(1, int(T * SHIFT_FRAC))
            x_cat = jnp.roll(x, -shift_len, axis=1)
            g = jax.nn.sigmoid(gate)
            x_shift = jnp.einsum('btd,ed->bte', x_cat, W_shift) * g + x * (1.0 - g)
            mu = jnp.mean(x_shift, axis=-1, keepdims=True)
            var = jnp.var(x_shift, axis=-1, keepdims=True)
            x_norm = (x_shift - mu) * jax.lax.rsqrt(var + LN_EPS) * ln_gamma + ln_beta
            k = jnp.einsum('btd,sd->bts', x_norm, W_key)
            v = jnp.einsum('btd,sd->bts', x_norm, W_value)
            w = jnp.exp(time_decay)
            u = jnp.exp(time_first)
            wkv = jnp.exp(-u * jax.nn.sigmoid(k)) * v

            def step(state, wkv_t):
                state = state * w + wkv_t
                return (state, state)
            init = jnp.zeros((B, k.shape[-1]), x.dtype)
            last_state, states = jax.lax.scan(step, init, jnp.swapaxes(wkv, 0, 1))
            states = jnp.swapaxes(states, 0, 1)
            output = jnp.einsum('bts,ds->btd', states, W_output)
            return (output, jax.lax.stop_gradient(last_state))
        return _reference_tuple_inner(x, W_key, W_value, W_output, W_shift, gate, time_decay, time_first, ln_gamma, ln_beta)[0]

    def _L0_ffn_ref(x, router_w, gate_w, up_w, down_w):
        import jax, jax.numpy as jnp
        import numpy as np
        B, T, D, F, E, K = (2, 128, 256, 96, 16, 2)
        scores = jnp.einsum('btd,de->bte', x, router_w).astype(jnp.float32)
        probs = jax.nn.softmax(scores, axis=-1)
        routing_weights, routing_idx = jax.lax.top_k(probs, K)
        routing_weights = routing_weights / jnp.sum(routing_weights, axis=-1, keepdims=True)
        routing_weights = routing_weights.astype(x.dtype)
        one_hot = jax.nn.one_hot(routing_idx, E, dtype=x.dtype)
        combine = jnp.einsum('btk,btke->bte', routing_weights, one_hot)
        g = jnp.einsum('btd,edf->ebtf', x, gate_w)
        u = jnp.einsum('btd,edf->ebtf', x, up_w)
        h = jax.nn.silu(g) * u
        expert_out = jnp.einsum('ebtf,efd->ebtd', h, down_w)
        out = jnp.einsum('ebtd,bte->btd', expert_out, combine)
        return out

    def _L1_attn_ref(hidden_states, attn_norm_w, q_w, k_w, v_w, g_w, o_w, gnorm_w, mlp_norm_w, gate_w, down_w):
        import jax, jax.numpy as jnp
        import numpy as np
        D_MODEL = 256
        N_HEADS = 8
        EXPAND_K = 1
        EXPAND_V = 2
        DK = D_MODEL * EXPAND_K // N_HEADS
        DV = D_MODEL * EXPAND_V // N_HEADS
        INTER = 704
        EPS = 1e-06
        CHUNK = 64

        def rmsnorm(x, w, eps=EPS):
            return x * jax.lax.rsqrt(jnp.mean(x * x, axis=-1, keepdims=True) + eps) * w

        def rope(x):
            T, D = (x.shape[1], x.shape[-1])
            inv_freq = 1.0 / 10000.0 ** (jnp.arange(0, D, 2, dtype=jnp.float32) / D)
            ang = jnp.arange(T, dtype=jnp.float32)[:, None] * inv_freq
            cos = jnp.cos(ang)[None, :, None, :]
            sin = jnp.sin(ang)[None, :, None, :]
            x1, x2 = jnp.split(x, 2, axis=-1)
            return jnp.concatenate([x1 * cos - x2 * sin, x2 * cos + x1 * sin], axis=-1)

        def chunk_retention(q, k, v):
            B, T, H, Dk = q.shape
            Dv = v.shape[-1]
            C = CHUNK
            N = T // C
            gamma = 1.0 - jnp.exp2(-5.0 - jnp.arange(H, dtype=jnp.float32))
            i = jnp.arange(C, dtype=jnp.float32)
            diff = i[:, None] - i[None, :]
            Dmask = jnp.where(diff >= 0, gamma[:, None, None] ** diff, 0.0)
            cross_decay = gamma[:, None] ** (i[None, :] + 1.0)
            k_decay = gamma[:, None] ** (C - 1.0 - i[None, :])
            chunk_decay = gamma ** C
            to_chunks = lambda x: jnp.moveaxis(x.reshape(B, N, C, H, x.shape[-1]).transpose(0, 1, 3, 2, 4), 1, 0)
            qc, kc, vc = (to_chunks(q), to_chunks(k), to_chunks(v))

            def body(S, inp):
                qb, kb, vb = inp
                attn = jnp.einsum('bhid,bhjd->bhij', qb, kb) * Dmask
                o_intra = jnp.einsum('bhij,bhje->bhie', attn, vb)
                o_cross = jnp.einsum('bhid,bhde->bhie', qb * cross_decay[None, :, :, None], S)
                S = chunk_decay[None, :, None, None] * S + jnp.einsum('bhid,bhie->bhde', kb * k_decay[None, :, :, None], vb)
                return (S, o_intra + o_cross)
            S0 = jnp.zeros((B, H, Dk, Dv), q.dtype)
            _, o = jax.lax.scan(body, S0, (qc, kc, vc))
            return jnp.moveaxis(o, 0, 1).transpose(0, 1, 3, 2, 4).reshape(B, T, H, Dv)
        B, T, d = hidden_states.shape
        residual = hidden_states
        h = rmsnorm(hidden_states, attn_norm_w)
        q = (h @ q_w).reshape(B, T, N_HEADS, DK)
        k = (h @ k_w).reshape(B, T, N_HEADS, DK)
        v = (h @ v_w).reshape(B, T, N_HEADS, DV)
        g = (h @ g_w).reshape(B, T, N_HEADS, DV)
        q, k = (rope(q), rope(k))
        q = q * DK ** (-0.5)
        o = chunk_retention(q, k, v)
        o = rmsnorm(o, gnorm_w) * (g * jax.nn.sigmoid(g))
        h = o.reshape(B, T, N_HEADS * DV) @ o_w
        residual = h + residual
        h = rmsnorm(residual, mlp_norm_w)
        y = h @ gate_w
        gate, y = jnp.split(y, 2, axis=-1)
        h = gate * jax.nn.sigmoid(gate) * y @ down_w
        return residual + h

    def _L1_ffn_ref(x, wq_gate, s_gate, wq_up, s_up, wq_down, s_down):
        import jax, jax.numpy as jnp
        import numpy as np
        DIM = 256
        HID = 704
        ZERO_POINT = 128.0

        def _qlinear(x, wq, scale):
            W = (wq.astype(jnp.float32) - ZERO_POINT) * scale[:, None]
            return jnp.einsum('bsd,hd->bsh', x, W)
        gate = _qlinear(x, wq_gate, s_gate)
        gate = jax.nn.silu(gate)
        up = _qlinear(x, wq_up, s_up)
        return _qlinear(gate * up, wq_down, s_down)
    x = L0_attn_x
    mod = (_silu(L0_c) @ L0_wmod).reshape(L0_c.shape[0], 6, 1, -1)
    sa, ca, ga, sb, cb, gb = (mod[:, 0], mod[:, 1], mod[:, 2], mod[:, 3], mod[:, 4], mod[:, 5])
    ga = (2 * (ga >= 0) - 1) * jnp.maximum(jnp.abs(ga), 0.25)
    gb = (2 * (gb >= 0) - 1) * jnp.maximum(jnp.abs(gb), 0.25)
    h = _layernorm(x, axis=-1) * (1 + ca) + sa
    x = x + ga * _L0_attn_ref(h, L0_attn_W_key, L0_attn_W_value, L0_attn_W_output, L0_attn_W_shift, L0_attn_gate, L0_attn_time_decay, L0_attn_time_first, L0_attn_ln_gamma, L0_attn_ln_beta)
    h = _layernorm(x, axis=-1) * (1 + cb) + sb
    x = x + gb * _L0_ffn_ref(h, L0_ffn_router_w, L0_ffn_gate_w, L0_ffn_up_w, L0_ffn_down_w)
    mod = (_silu(L1_c) @ L1_wmod).reshape(L1_c.shape[0], 6, 1, -1)
    sa, ca, ga, sb, cb, gb = (mod[:, 0], mod[:, 1], mod[:, 2], mod[:, 3], mod[:, 4], mod[:, 5])
    ga = (2 * (ga >= 0) - 1) * jnp.maximum(jnp.abs(ga), 0.25)
    gb = (2 * (gb >= 0) - 1) * jnp.maximum(jnp.abs(gb), 0.25)
    h = _layernorm(x, axis=-1) * (1 + ca) + sa
    x = x + ga * _L1_attn_ref(h, L1_attn_attn_norm_w, L1_attn_q_w, L1_attn_k_w, L1_attn_v_w, L1_attn_g_w, L1_attn_o_w, L1_attn_gnorm_w, L1_attn_mlp_norm_w, L1_attn_gate_w, L1_attn_down_w)
    h = _layernorm(x, axis=-1) * (1 + cb) + sb
    x = x + gb * _L1_ffn_ref(h, L1_ffn_wq_gate, L1_ffn_s_gate, L1_ffn_wq_up, L1_ffn_s_up, L1_ffn_wq_down, L1_ffn_s_down)
    return x

_drawn_inputs = setup_inputs


def setup_inputs(seed=0):
    import zlib

    import numpy as np

    out = dict(_drawn_inputs(seed))
    spreads = {'L0_attn_gate': (1.0, 0.6),
     'L0_attn_ln_gamma': (1.0, 0.2),
     'L0_attn_ln_beta': (0.0, 0.1),
     'L1_attn_attn_norm_w': (1.0, 0.2),
     'L1_attn_gnorm_w': (1.0, 0.59),
     'L1_attn_mlp_norm_w': (1.0, 0.2)}
    factors = {'L0_attn_time_first': 4.253,
     'L0_ffn_router_w': 8.0,
     'L0_ffn_gate_w': 8.0,
     'L0_ffn_up_w': 8.0,
     'L0_ffn_down_w': 8.0,
     'L1_ffn_s_gate': 8.0,
     'L1_ffn_s_up': 8.0,
     'L1_ffn_s_down': 8.0}
    for name, (base, spread) in spreads.items():
        noise = np.random.default_rng([zlib.crc32(name.encode()), seed]).standard_normal(out[name].shape)
        drawn = base * np.exp(spread * noise) if base else spread * noise
        out[name] = jnp.asarray(drawn.astype(out[name].dtype))
    for name, factor in factors.items():
        out[name] = (out[name] * factor).astype(out[name].dtype)
    return out
```

```python
from contextlib import ExitStack

import numpy as np
import concourse.bass as bass
from concourse import mybir

F32 = mybir.dt.float32
F32R = mybir.dt.float32r
I32 = mybir.dt.int32
U32 = mybir.dt.uint32
ALU = mybir.AluOpType
ACT = mybir.ActivationFunctionType
AX = mybir.AxisListType

P = 128
B, T, D = 2, 1024, 256
J = T // P
KC = D // P
S = 64
E, FE = 16, 96
EG = 4
GW = E * FE // EG
H, DK, DV = 8, 32, 64
HV = H * DV
INTER = 704
IG = 2
IW = INTER // IG
MODS = 6
LN_EPS = 1e-5
RMS_EPS = 1e-6
MIN_GATE = 0.25
ZERO_POINT = 128.0


class Signal:

    def __init__(self, sem, per_turn, ahead=False):
        self.sem, self.per_turn, self.ahead = sem, per_turn, ahead
        self.base = per_turn if ahead else 0

    def now(self, turn, k=0):
        return turn * self.per_turn + (self.base + k + 1)

    def before(self, turn, k=0):
        assert self.ahead
        return turn * self.per_turn + (self.base + k + 1 - self.per_turn)

    def pass_turns(self, turns):
        self.base += turns * self.per_turn

    def again(self, per_turn):
        self.per_turn = per_turn
        return self


class Steps:

    def __init__(self, eng, counts, turn=None):
        self.eng, self.counts, self.turn, self.k = eng, counts, turn, 0

    def __call__(self, instruction):
        instruction.then_inc(self.counts.sem, 1)
        self.eng.wait_ge(self.counts.sem, self.counts.now(0 if self.turn is None else self.turn, self.k))
        self.k += 1

    def end(self, turns=1):
        assert self.turn is None or self.k == self.counts.per_turn, (self.k, self.counts.per_turn)
        self.counts.base += turns * self.k


def f32(ap):
    return ap.bitcast(F32)


def product3(nc, out, terms, first=True, last=True):
    n = len(terms)
    for i, (lhs, rhs) in enumerate(terms):
        for k, (x, y) in enumerate(((0, 0), (0, 1), (1, 0))):
            done = nc.tensor.matmul(out, lhs[x], rhs[y], start=(first and i == 0 and k == 0),
                                    stop=(last and i == n - 1 and k == 2), skip_group_check=True)
    return done


class Memory(dict):

    def __init__(self, nc, stack, phase=""):
        self.nc, self.stack, self.phase = nc, stack, phase

    def add(self, name, shape, dt=F32):
        tile = self.stack.enter_context(self.nc.sbuf_tensor(self.phase + name, [P] + list(shape), dt))
        self[name] = tile
        return tile

    def pair(self, name, shape):
        both = [self.stack.enter_context(self.nc.sbuf_tensor(f"{self.phase}{name}_{x}", [P] + list(shape), F32R)) for x in ("hi", "lo")]
        self[name] = both
        return both

    def slots(self, names, shape, n, dt=F32):
        for name in names:
            self[name] = [self.stack.enter_context(self.nc.sbuf_tensor(f"{self.phase}{name}{s}", [P] + list(shape), dt))
                                   for s in range(n)]

    def pair_slots(self, names, shape, n):
        for name in names:
            self[name] = [[self.stack.enter_context(self.nc.sbuf_tensor(f"{self.phase}{name}{s}_{x}", [P] + list(shape), F32R))
                                    for x in ("hi", "lo")] for s in range(n)]


def flat(ap):
    return ap.rearrange("p a b -> p (a b)")


def row(tile, *index):
    *first, last = index
    ap = tile
    for i in first:
        ap = ap[:, i]
    return ap[:, bass.ds(last, 1), :].rearrange("p a d -> p (a d)")


MIX, DIAG = 0, KC * D
KV = DIAG + KC * P
OUT0 = KV + KC * P
ROUT = OUT0 + B * D
W0N = ROUT + KC * E


def build(nc, a, out):
    with ExitStack() as ctx:
        bank = [ctx.enter_context(nc.psum_tensor(f"bank{i}", [P, 512], F32)) for i in range(8)]

        def sem(name):
            return ctx.enter_context(nc.semaphore(name))

        keep = Memory(nc, ctx)
        keep.add("x", [B, J, D])
        keep.add("ident", [P])
        keep.add("neg_half", [H])
        keep.add("ln_eps", [1])
        keep.add("rms_eps", [1])
        keep.add("head_eps", [H])
        keep.add("norm_cols", [2, KC])
        keep.add("norm16", [2, KC])
        keep.add("gnorm_col", [1])
        keep.add("gnorm4", [1])
        keep.add("spare", [1])
        for l in range(2):
            keep.add(f"mod_col{l}", [MODS * KC, B])
            keep.add(f"gate_row{l}", [B, 2, D])
        keep.add("shift_scale", [B, 2, D])
        keep.pair("w_qkvg", [KC, 2 * D + 2 * HV])
        keep.pair("w_o", [HV // P, D])
        x_loaded = sem("x_loaded")
        with ExitStack() as early:
            lay0 = Memory(nc, early)
            lay0.pair("w0", [W0N])
            lay0.add("wkv_tok", [J, B, S])
            lay0.add("states", [T])
            lay0.add("decay", [1])
            lay0.add("ln_col", [2, KC])
            lay0.add("neg_u", [S])
            lay0.pair("w_gate", [KC, E * FE])
            lay0.pair("w_up", [KC, E * FE])
            lay0.pair("w_down", [E * FE // P, D])
            with ExitStack() as tmp:
                setup(nc, sem, a, bank, keep, lay0, Memory(nc, tmp, "setup_"), x_loaded)
            with ExitStack() as tmp:
                mix_and_key_value(nc, sem, a, bank, keep, lay0, Memory(nc, tmp, "mix_"), x_loaded)
            recurrence(nc, sem, bank, keep, lay0)
            signals = {}
            with ExitStack() as tmp:
                gated_mlp(nc, sem, a, bank, keep, Memory(nc, tmp, "experts_"), "experts", lay0, None, signals)
        keep.pair("w_mlp", [KC, IG * 2 * IW])
        keep.pair("w_mlp_down", [IG * 3, D])
        keep.add("r2", [B, J, D])
        with ExitStack() as tmp:
            retention(nc, sem, a, bank, keep, Memory(nc, tmp, "ret_"))
        keep.pair("w_ffn", [KC, IG * 2 * IW])
        keep.pair("w_ffn_down", [IG * 3, D])
        with ExitStack() as tmp:
            gated_mlp(nc, sem, a, bank, keep, Memory(nc, tmp, "mlp_"), "mlp", None, None, signals)
        with ExitStack() as tmp:
            gated_mlp(nc, sem, a, bank, keep, Memory(nc, tmp, "ffn_"), "ffn", None, out, signals)


def moments(nc, v, step, spare, tiles, gone, arrive=None):
    for s, (stats, mv, x) in enumerate(tiles):
        if arrive:
            arrive(s)
        else:
            nc.vector.memset(spare[:], 0.0)
        statistics = nc.vector.bn_stats(stats, x)
        if s:
            nc.vector.bn_aggr(tiles[s - 1][1], tiles[s - 1][0]).then_inc(gone.sem, 1)
        step(statistics)
    nc.vector.memset(spare[:], 0.0)
    nc.vector.bn_aggr(tiles[-1][1], tiles[-1][0]).then_inc(gone.sem, 1)


def setup(nc, sem, a, bank, keep, lay0, m, x_loaded):
    m.add("w_raw", [W0N])
    m.slots(["wmod"], [KC, MODS * D], 2)
    for name in ("c_col", "c_th", "c_sum", "c_silu"):
        m.add(name, [2, KC, B])
    m.add("c_wide", [2 * KC * B, P])
    for name in ("gate_bc", "gate_th", "mix_gain", "keep_gain"):
        m.add(name, [D])
    m.add("u_bc", [S])
    m.add("u_exp", [S])
    m.add("dec_raw", [1])
    m.slots(["sign", "size"], [512], 2)
    small, loaded, zeroed, c_tanh, gate_tanh, exps, silu, products, raw_ready, hi_ready, steps = (
        sem(n) for n in ("small_loaded", "weights_loaded", "padding_zeroed", "c_tanh_done", "gate_tanh_done",
                         "exps_done", "silu_ready", "mod_products", "w0_raw_ready", "w0_hi_ready", "setup_steps"))

    with nc.Block() as block:
        @block.sync
        def _(sp):
            sp.dma_start(m["c_col"][:], a["c"]).then_inc(small, 16)
            sp.dma_start(m["gate_bc"][:], a["gate"].partition_broadcast(P)).then_inc(small, 16)
            sp.dma_start(m["u_bc"][:], a["time_first"].partition_broadcast(P)).then_inc(small, 16)
            sp.dma_start(lay0["ln_col"][:], a["ln_cols"]).then_inc(small, 16)
            sp.dma_start(keep["norm_cols"][:], a["norm_cols"]).then_inc(small, 16)
            sp.dma_start(keep["gnorm_col"][:], a["gnorm_col"]).then_inc(small, 16)
            for b in range(B):
                sp.dma_start(m["dec_raw"][S * b:S * b + S, :], a["time_decay"]).then_inc(small, 16)
            for l in range(2):
                sp.dma_start(m["wmod"][l][:], a["wmod"][l]).then_inc(loaded, 16)
            sp.dma_start(keep["ident"][:], a["ident"]).then_inc(loaded, 16)
            sp.dma_start(m["w_raw"][:, MIX:DIAG], a["w_mix"]).then_inc(loaded, 16)
            sp.dma_start(m["w_raw"][:, KV:OUT0], a["w_kv"]).then_inc(loaded, 16)
            sp.dma_start(m["w_raw"][:, ROUT:W0N], a["router"]).then_inc(loaded, 16)
            sp.wait_ge(zeroed, 2)
            for b in range(B):
                sp.dma_start(m["w_raw"][S * b:S * b + S, OUT0 + b * D:OUT0 + (b + 1) * D], a["w_out0"]).then_inc(loaded, 16)
            sp.dma_start(keep["x"][:], a["x"].rearrange("b (j p) d -> p b j d", p=P)).then_inc(x_loaded, 16)

        @block.gpsimd
        def _(pool):
            nc.gpsimd.memset(m["w_raw"][:, OUT0:ROUT], 0.0).then_inc(zeroed, 1)
            nc.gpsimd.memset(keep["neg_half"][:], -0.5).then_inc(zeroed, 1)
            nc.gpsimd.memset(keep["ln_eps"][:], LN_EPS)
            nc.gpsimd.memset(keep["rms_eps"][:], RMS_EPS * D)
            nc.gpsimd.memset(keep["head_eps"][:], RMS_EPS * DV)

        @block.scalar
        def _(act):
            act.wait_ge(small, 16 * 8)
            nc.scalar.activation(m["c_th"][:], m["c_col"][:], ACT.Tanh, scale=0.5).then_inc(c_tanh, 1)
            nc.scalar.activation(m["gate_th"][:], m["gate_bc"][:], ACT.Tanh, scale=0.5).then_inc(gate_tanh, 1)
            nc.scalar.activation(m["u_exp"][:], m["u_bc"][:], ACT.Exp).then_inc(exps, 1)
            nc.scalar.activation(lay0["decay"][:], m["dec_raw"][:], ACT.Exp).then_inc(exps, 1)
            act.wait_ge(raw_ready, 1)
            nc.scalar.copy(lay0["w0"][0][:], m["w_raw"][:]).then_inc(hi_ready, 1)

        @block.vector
        def _(v):
            step = Steps(v, Signal(steps, 0))
            v.wait_ge(c_tanh, 1)
            step(nc.vector.scalar_tensor_tensor(m["c_sum"][:], m["c_th"][:], 1.0, m["c_col"][:], ALU.add, ALU.mult))
            step(nc.vector.tensor_scalar(m["c_silu"][:], m["c_sum"][:], 0.5, None, ALU.mult))
            nc.vector.tensor_copy(m["c_wide"][:], m["c_silu"][:].rearrange("p l k b -> p (l k b)").unsqueeze(2)
                                  .to_broadcast([P, 2 * KC * B, P])).then_inc(silu, 1)
            v.wait_ge(gate_tanh, 1)
            step(nc.vector.tensor_scalar(m["mix_gain"][:], m["gate_th"][:], 0.5, 0.5, ALU.mult, ALU.add))
            step(nc.vector.tensor_scalar(m["keep_gain"][:], m["gate_th"][:], -0.5, 0.5, ALU.mult, ALU.add))
            v.wait_ge(exps, 1)
            nc.vector.tensor_scalar(lay0["neg_u"][:], m["u_exp"][:], -0.5, None, ALU.mult)
            nc.vector.tensor_scalar(keep["norm16"][:], keep["norm_cols"][:], float(D) ** 0.5, None, ALU.mult)
            nc.vector.tensor_scalar(keep["gnorm4"][:], keep["gnorm_col"][:], float(DV) ** 0.5 / 2, None, ALU.mult)
            v.wait_ge(loaded, 16 * 8)
            for k in range(KC):
                w = m["w_raw"][:, MIX + k * D:MIX + (k + 1) * D]
                step(nc.vector.tensor_tensor(w, w, m["mix_gain"][:], ALU.mult))
                step(nc.vector.tensor_tensor(m["w_raw"][:, DIAG + k * P:DIAG + (k + 1) * P], keep["ident"][:],
                                             m["keep_gain"][:, k * P:(k + 1) * P], ALU.mult))
            v.sem_inc(raw_ready, 1)
            v.wait_ge(hi_ready, 1)
            nc.vector.tensor_tensor(lay0["w0"][1][:], m["w_raw"][:], f32(lay0["w0"][0][:]), ALU.subtract)
            v.wait_ge(products, 1)
            for l, (col, gates) in enumerate(((keep["mod_col0"], keep["gate_row0"]), (keep["mod_col1"], keep["gate_row1"]))):
                step(nc.vector.tensor_copy(col[:].rearrange("p m b -> p (m b)"), bank[l][:, 0:MODS * KC * B]))
                for i in (1, 4):
                    w = col[:, i * KC:(i + 1) * KC, :]
                    step(nc.vector.tensor_scalar(w, w, 1.0, None, ALU.add))
                for b in range(B):
                    ps = bank[2 + 2 * l + b]
                    step(nc.vector.tensor_scalar(m["sign"][b][:], ps[:], 0.0, 2.0, ALU.is_ge, ALU.mult))
                    step(nc.vector.tensor_scalar(m["sign"][b][:], m["sign"][b][:], 1.0, None, ALU.subtract))
                    step(nc.vector.tensor_tensor(m["size"][b][:], ps[:], m["sign"][b][:], ALU.mult))
                    step(nc.vector.scalar_tensor_tensor(flat(gates[:, b]), m["size"][b][:], MIN_GATE, m["sign"][b][:],
                                                        ALU.max, ALU.mult))
            for b in range(B):
                nc.vector.tensor_copy(keep["shift_scale"][:, b, 0, :], bank[6 + b][:, 0:D])
                nc.vector.tensor_scalar(keep["shift_scale"][:, b, 1, :], bank[6 + b][:, D:2 * D], 1.0, None, ALU.add)

        @block.tensor
        def _(pe):
            pe.wait_ge(silu, 1)
            pe.wait_ge(loaded, 16 * 8)
            for l in range(2):
                for i in range(MODS * KC):
                    for k in range(KC):
                        nc.tensor.matmul(bank[l][:, i * B:(i + 1) * B], m["wmod"][l][:, k, i * P:(i + 1) * P],
                                         m["c_silu"][:, l, k, :], start=(k == 0), stop=(k == KC - 1))

            def on_every_row(ps, l, b, first, n):
                for k in range(KC):
                    last = nc.tensor.matmul(ps, m["c_wide"][:, (l * KC + k) * B + b, :], m["wmod"][l][:, k, first:first + n],
                                            start=(k == 0), stop=(k == KC - 1))
                return last
            for b in range(B):
                for l in range(2):
                    for i, which in enumerate((2, 5)):
                        on_every_row(bank[2 + 2 * l + b][:, i * D:(i + 1) * D], l, b, which * D, D)
                last = on_every_row(bank[6 + b][:], 1, b, 0, 2 * D)
            last.then_inc(products, 1)


def mix_and_key_value(nc, sem, a, bank, keep, lay0, m, x_loaded):
    NS, TURNS = 2 * B, J // 2
    PIECE = KC * E * FE // TURNS
    slots = [(s, s // 2, s % 2) for s in range(NS)]
    m.slots(["xn", "mn"], [D], NS)
    m.slots(["feat", "mfeat"], [KC, P], NS)
    m.pair_slots(["f", "mf"], [KC, P], NS)
    m.slots(["stats"], [2, 6], NS)
    m.slots(["mv"], [2, 2], NS)
    m.slots(["ve", "rstd"], [2], NS)
    m.slots(["kth", "karg", "kexp"], [S], NS)
    m.slots(["raw"], [PIECE], 3)
    experts = ((lay0["w_gate"], "w_gate"), (lay0["w_up"], "w_up"), (lay0["w_down"], "w_down"))

    def signal(name, per_turn=NS, ahead=False):
        return Signal(sem("mix_" + name), per_turn, ahead)
    var, rstd, xn, xT, f_hi, f_lo = (signal(n) for n in ("var", "rstd", "xn", "xT", "f_hi", "f_lo"))
    mixed, mvar, mrstd, mn, mT, mf_hi, mf_lo = (signal(n) for n in ("mixed", "mvar", "mrstd", "mn", "mT", "mf_hi", "mf_lo"))
    kv, kth, karg, kexp = (signal(n) for n in ("kv", "ktanh", "karg", "kexp"))
    wkv = signal("wkv", ahead=True)
    raw_in = [sem(f"mix_raw_in{i}") for i in range(3)]
    raw_hi, raw_lo = signal("raw_hi", 3), signal("raw_lo", 3, True)
    v_steps, p_steps = signal("v_steps", 2 * NS), signal("p_steps", 2 * NS)

    def tile_of_x(t, b, h):
        return row(keep["x"], b, t + h * TURNS)

    def piece(w, t):
        return flat(flat(w[:]).rearrange("p (t n) -> p t n", t=TURNS)[:, bass.ds(t, 1), :])

    with nc.Block() as block:
        @block.sync
        def _(sp):
            for sig in (wkv, raw_lo):
                sp.sem_inc(sig.sem, sig.per_turn)
            sp.wait_ge(x_loaded, 16)
            with nc.sync.Fori(0, TURNS) as t:
                for i, (_, name) in enumerate(experts):
                    sp.wait_ge(raw_lo.sem, raw_lo.before(t, i))
                    sp.dma_start(m["raw"][i][:], a[name][bass.ds(t, 1)].rearrange("a p n -> p (a n)")).then_inc(raw_in[i], 16)

        @block.gpsimd
        def _(pool):
            with nc.gpsimd.Fori(0, TURNS) as t:
                step = Steps(pool, p_steps, t)

                def rsqrt(k, got, gone):
                    for s, _, _ in slots:
                        pool.wait_ge(got.sem, got.now(t, s))
                        step(nc.gpsimd.tensor_tensor(m["ve"][s][:, k:k + 1], m["mv"][s][:, k, 1:2], keep["ln_eps"][:], ALU.add))
                        nc.gpsimd.tensor_tensor(m["rstd"][s][:, k:k + 1], m["ve"][s][:, k:k + 1], keep["neg_half"][:, 0:1],
                                                ALU.pow).then_inc(gone.sem, 1)

                def low(full, pair, got, gone):
                    for s, _, _ in slots:
                        pool.wait_ge(got.sem, got.now(t, s))
                        nc.gpsimd.tensor_tensor(pair[s][1][:], full[s][:], f32(pair[s][0][:]), ALU.subtract).then_inc(gone.sem, 1)
                rsqrt(0, var, rstd)
                low(m["feat"], m["f"], f_hi, f_lo)
                rsqrt(1, mvar, mrstd)
                low(m["mfeat"], m["mf"], mf_hi, mf_lo)
                step.end(TURNS)

        @block.vector
        def _(v):
            v.wait_ge(x_loaded, 16)
            with nc.vector.Fori(0, TURNS) as t:
                step = Steps(v, v_steps, t)
                moments(nc, v, step, keep["spare"], [(m["stats"][s][:, 0, :], m["mv"][s][:, 0, :], tile_of_x(t, b, h))
                                                  for s, b, h in slots], var)
                for s, b, h in slots:
                    v.wait_ge(rstd.sem, rstd.now(t, s))
                    nc.vector.tensor_scalar(m["xn"][s][:], tile_of_x(t, b, h), m["mv"][s][:, 0, 0:1], m["rstd"][s][:, 0:1],
                                            ALU.subtract, ALU.mult).then_inc(xn.sem, 1)
                moments(nc, v, step, keep["spare"], [(m["stats"][s][:, 1, :], m["mv"][s][:, 1, :], bank[4 + s][:, 0:D])
                                                  for s, b, h in slots], mvar, lambda s: v.wait_ge(mixed.sem, mixed.now(t, s)))
                for s, b, h in slots:
                    v.wait_ge(mrstd.sem, mrstd.now(t, s))
                    nc.vector.tensor_scalar(m["mn"][s][:], bank[4 + s][:, 0:D], m["mv"][s][:, 1, 0:1], m["rstd"][s][:, 1:2],
                                            ALU.subtract, ALU.mult).then_inc(mn.sem, 1)
                for i, (w, _) in enumerate(experts):
                    v.wait_ge(raw_hi.sem, raw_hi.now(t, i))
                    nc.vector.tensor_tensor(piece(w[1], t), m["raw"][i][:], f32(piece(w[0], t)), ALU.subtract).then_inc(raw_lo.sem, 1)
                for s, b, h in slots:
                    v.wait_ge(kth.sem, kth.now(t, s))
                    nc.vector.scalar_tensor_tensor(m["karg"][s][:], m["kth"][s][:], 1.0, lay0["neg_u"][:], ALU.add,
                                                   ALU.mult).then_inc(karg.sem, 1)
                for s, b, h in slots:
                    v.wait_ge(kexp.sem, kexp.now(t, s))
                    o = lay0["wkv_tok"][:, bass.ds(t + h * TURNS, 1), b, :].rearrange("p a s -> p (a s)")
                    nc.vector.tensor_tensor(o, bank[4 + s][:, S:2 * S], m["kexp"][s][:], ALU.mult).then_inc(wkv.sem, 1)
                step.end(TURNS)

        @block.scalar
        def _(act):
            with nc.scalar.Fori(0, TURNS) as t:
                def affine(full, pair, got, gone, columns):
                    for s, b, h in slots:
                        act.wait_ge(got.sem, got.now(t, s))
                        for c in range(KC):
                            scale, shift = columns(b, c)
                            ps = bank[s][:, c * P:(c + 1) * P]
                            nc.scalar.activation(full[s][:, c, :], ps, ACT.Identity, bias=shift, scale=scale)
                            last = nc.scalar.activation(pair[s][0][:, c, :], ps, ACT.Identity, bias=shift, scale=scale)
                        last.then_inc(gone.sem, 1)
                affine(m["feat"], m["f"], xT, f_hi, lambda b, c: (keep["mod_col0"][:, KC + c, b:b + 1], keep["mod_col0"][:, c, b:b + 1]))
                for i, (w, _) in enumerate(experts):
                    act.wait_ge(raw_in[i], t * 16 + 16)
                    nc.scalar.copy(piece(w[0], t), m["raw"][i][:]).then_inc(raw_hi.sem, 1)
                affine(m["mfeat"], m["mf"], mT, mf_hi, lambda b, c: (lay0["ln_col"][:, 0, c:c + 1], lay0["ln_col"][:, 1, c:c + 1]))
                for s, _, _ in slots:
                    act.wait_ge(kv.sem, kv.now(t, s))
                    nc.scalar.activation(m["kth"][s][:], bank[4 + s][:, 0:S], ACT.Tanh, scale=0.5).then_inc(kth.sem, 1)
                for s, _, _ in slots:
                    act.wait_ge(karg.sem, karg.now(t, s))
                    nc.scalar.activation(m["kexp"][s][:], m["karg"][s][:], ACT.Exp).then_inc(kexp.sem, 1)

        @block.tensor
        def _(pe):
            def w0(first, n):
                return [w[:, first:first + n] for w in lay0["w0"]]

            def chunk(pair, c):
                return [x[:, c, :] for x in pair]
            with nc.tensor.Fori(0, TURNS) as t:
                def transposes(src, got, gone):
                    for s, _, _ in slots:
                        pe.wait_ge(got.sem, got.now(t, s))
                        for c in range(KC):
                            last = nc.tensor.transpose(bank[s][:, c * P:(c + 1) * P], src[s][:, c * P:(c + 1) * P], keep["ident"][:])
                        last.then_inc(gone.sem, 1)
                transposes(m["xn"], xn, xT)
                pe.wait_ge(f_lo.sem, f_lo.now(t, NS - 1))
                for s, b, h in slots:
                    partner = 2 * b + 1 - h
                    pe.wait_ge(wkv.sem, wkv.before(t, s))
                    product3(nc, bank[4 + s][:, 0:D], [(chunk(m["f"][partner], c), w0(MIX + c * D, D)) for c in range(KC)],
                             last=False)
                    for c in range(KC):
                        last = product3(nc, bank[4 + s][:, c * P:(c + 1) * P], [(chunk(m["f"][s], c), w0(DIAG + c * P, P))],
                                        first=False)
                    last.then_inc(mixed.sem, 1)
                transposes(m["mn"], mn, mT)
                for s, _, _ in slots:
                    pe.wait_ge(mf_lo.sem, mf_lo.now(t, s))
                    product3(nc, bank[4 + s][:, 0:2 * S], [(chunk(m["mf"][s], c), w0(KV + c * P, P)) for c in range(KC)]
                             ).then_inc(kv.sem, 1)


def recurrence(nc, sem, bank, keep, lay0):
    turned, scanned = sem("wkv_turned"), sem("scanned")
    with nc.Block() as block:
        @block.tensor
        def _(pe):
            for j in range(J):
                nc.tensor.transpose(bank[j // 4][:, (j % 4) * P:(j % 4 + 1) * P],
                                    flat(lay0["wkv_tok"][:, j]), keep["ident"][:]).then_inc(turned, 1)

        @block.vector
        def _(v):
            half = T // 2
            for k in range(2):
                v.wait_ge(turned, (k + 1) * J // 2)
                if k:
                    v.wait_ge(scanned, 1)
                nc.vector.tensor_tensor_scan(lay0["states"][:, k * half:(k + 1) * half], lay0["decay"][:].to_broadcast([P, half]),
                                             bank[k][:], lay0["states"][:, half - 1:half] if k else 0.0,
                                             ALU.mult, ALU.add).then_inc(scanned, 1)
            v.wait_ge(scanned, 2)


class Cut:

    def __init__(self, nc, sem, m, a, name, parts):
        self.nc, self.a, self.parts = nc, a, parts
        n = len(parts)
        self.loaded = [sem(f"{name}_loaded{i}") for i in range(n)]
        self.scaled = Signal(sem(f"{name}_scaled"), n, True)
        self.hi = Signal(sem(f"{name}_hi"), n)
        self.lo = Signal(sem(f"{name}_lo"), n)
        shapes = [[w[0].shape[1], w[0].shape[2] // J] for _, _, w, _ in parts]
        self.raw = [m.add(f"{name}_raw{i}", shape, parts[i][1]) for i, shape in enumerate(shapes)]
        self.full = [m.add(f"{name}_full{i}", shape) for i, shape in enumerate(shapes)]

    def piece(self, w, t):
        n = w.shape[2] // J
        return w[:, :, bass.ds(t * n, n)]

    def load(self, sp, t):
        for i, (name, _, _, _) in enumerate(self.parts):
            sp.wait_ge(self.scaled.sem, self.scaled.before(t, i))
            sp.dma_start(self.raw[i][:], self.a[name][bass.ds(t, 1)].rearrange("a p k n -> p (a k) n")).then_inc(self.loaded[i], 16)

    def scale(self, v, t):
        for i, (_, _, _, scaling) in enumerate(self.parts):
            v.wait_ge(self.loaded[i], t * 16 + 16)
            scaling(self.full[i], self.raw[i], t).then_inc(self.scaled.sem, 1)

    def take_hi(self, act, t):
        for i, (_, _, w, _) in enumerate(self.parts):
            act.wait_ge(self.scaled.sem, self.scaled.now(t, i))
            self.nc.scalar.copy(self.piece(w[0], t), self.full[i][:]).then_inc(self.hi.sem, 1)

    def take_lo(self, v, t):
        for i, (_, _, w, _) in enumerate(self.parts):
            v.wait_ge(self.hi.sem, self.hi.now(t, i))
            self.nc.vector.tensor_tensor(self.piece(w[1], t), self.full[i][:], f32(self.piece(w[0], t)),
                                         ALU.subtract).then_inc(self.lo.sem, 1)


def by_column(nc, columns):
    def scaling(out, raw, t):
        for k in range(out.shape[1]):
            last = nc.vector.tensor_scalar(out[:, k, :], raw[:, k, :], columns(k), None, ALU.mult)
        return last
    return scaling


def by_constant(nc, value):
    return lambda out, raw, t: nc.vector.tensor_scalar(out[:], raw[:], value, None, ALU.mult)


def from_codes(nc, scales):
    def scaling(out, raw, t):
        k, n = out.shape[1], out.shape[2]
        return nc.vector.scalar_tensor_tensor(out[:], raw[:], ZERO_POINT, scales[:, bass.ds(t * n, n)].unsqueeze(1)
                                              .to_broadcast([P, k, n]), ALU.subtract, ALU.mult)
    return scaling


def gated_mlp(nc, sem, a, bank, keep, m, kind, lay0, out, signals):
    experts, mlp, ffn = kind == "experts", kind == "mlp", kind == "ffn"
    NS = B
    G, W = (EG, GW) if experts else (IG, IW)
    mod_col, gate_row = (keep["mod_col0"], keep["gate_row0"]) if experts else (keep["mod_col1"], keep["gate_row1"])
    which_gate = 0 if mlp else 1
    if experts:
        w_down = lay0["w_down"]
    else:
        w_in, w_down = (keep["w_mlp"], keep["w_mlp_down"]) if mlp else (keep["w_ffn"], keep["w_ffn_down"])

    m.slots(["xn", "tmp"], [D], NS)
    m.slots(["feat"], [KC, P], NS)
    m.pair_slots(["f"], [KC, P], NS)
    m.slots(["th", "silu", "prod"], [W], NS)
    m.slots(["hid"], [3 * P], NS)
    m.pair_slots(["h"], [3, P], NS)
    m.slots(["stats"], [6], NS)
    m.slots(["mv"], [2], NS)
    m.slots(["ve", "rstd"], [1], NS)
    if experts:
        m.pair("st", [P])
        m.slots(["best"], [8], NS)
        m.slots(["first", "second", "share"], [E], NS)
        m.slots(["lead", "lead_th"], [1], NS)
        m.slots(["weight"], [2], NS)
        m.slots(["index"], [8], NS, U32)
        m.slots(["place"], [2], NS)
        m.add("iota", [E])
        cut = Cut(nc, sem, m, a, "cut1", [
            ("w_qkvg", F32, keep["w_qkvg"], by_column(nc, lambda k: keep["norm16"][:, 0, k:k + 1])),
            ("w_o", F32, keep["w_o"], by_column(nc, lambda k: keep["gnorm4"][:]))])
    elif mlp:
        m.add("s_in", [IG * 2 * IW])
        m.add("s_down", [D])
        m.add("s_down_half", [D])
        cut = Cut(nc, sem, m, a, "cut3", [("w_ffn", I32, keep["w_ffn"], from_codes(nc, m["s_in"])),
                                          ("w_ffn_down", I32, keep["w_ffn_down"], from_codes(nc, m["s_down_half"]))])
    else:
        cut = None

    def signal(name, per_turn=NS, ahead=False):
        if name in signals:
            return signals[name].again(per_turn)
        signals[name] = Signal(sem("gated_" + name), per_turn, ahead)
        return signals[name]
    moment, rstd, xn, xT, f_hi, f_lo = (signal(n) for n in ("moment", "rstd", "xn", "xT", "f_hi", "f_lo"))
    gu, th, hT, h_hi, h_lo = (signal(n, NS * G) for n in ("gate_up", "tanh", "hid_T", "h_hi", "h_lo"))
    prod = signal("prod", NS * G, True)
    down = signal("down")
    x_out = signal("x_out", NS, True)
    if experts:
        st_hi, st_lo = signal("st_hi", 1), signal("st_lo", 1)
        attn = signal("attn", NS, True)
        routed, lead, lead_tanh, share, attn_used = (signal(n) for n in ("routed", "lead", "lead_tanh", "share", "attn_used"))
        hid = signal("hid", NS * G)
    else:
        hid = prod
    v_steps = signal("v_steps", {"experts": 24, "mlp": 8, "ffn": 8}[kind])
    p_steps = signal("p_steps")
    if not ffn:
        ready = sem(f"{kind}_ready")
    if out is not None:
        stored = sem("stored")
    slots = range(NS)
    at = lambda gr, s: gr * NS + s

    def A(s): return bank[4 * s]
    def GATE(s): return bank[4 * s + 1]
    def UP(s): return bank[4 * s + 2]
    def TURN(s): return bank[4 * s + 3]

    with nc.Block() as block:
        @block.sync
        def _(sp):
            if experts:
                for sig in (x_out, prod, attn):
                    sp.sem_inc(sig.sem, sig.per_turn)
                sp.dma_start(m["iota"][:], a["iota"].partition_broadcast(P)).then_inc(ready, 16)
            if mlp:
                sp.dma_start(m["s_in"][:], a["s_ffn"].partition_broadcast(P)).then_inc(ready, 16)
                sp.dma_start(m["s_down"][:], a["s_ffn_down"].partition_broadcast(P)).then_inc(ready, 16)
            if cut:
                sp.sem_inc(cut.scaled.sem, cut.scaled.per_turn)
                with nc.sync.Fori(0, J) as t:
                    cut.load(sp, t)
            if out is not None:
                with nc.sync.Fori(0, J) as t:
                    for s in slots:
                        sp.wait_ge(x_out.sem, x_out.now(t, s))
                        sp.dma_start(out[s].rearrange("(j p) d -> j p d", p=P)[bass.ds(t, 1)].rearrange("a p d -> p (a d)"),
                                     row(keep["x"], s, t)).then_inc(stored, 16)
                sp.wait_ge(stored, 16 * NS * J)

        @block.gpsimd
        def _(pool):
            def front(t, step):
                if experts:
                    pool.wait_ge(st_hi.sem, st_hi.now(t))
                    nc.gpsimd.tensor_tensor(m["st"][1][:], lay0["states"][:, bass.ds(t * P, P)], f32(m["st"][0][:]),
                                            ALU.subtract).then_inc(st_lo.sem, 1)
                for s in slots:
                    pool.wait_ge(moment.sem, moment.now(t, s))
                    if mlp:
                        step(nc.gpsimd.tensor_tensor(m["ve"][s][:], m["mv"][s][:, 0:1], keep["rms_eps"][:], ALU.add))
                    else:
                        step(nc.gpsimd.tensor_tensor(m["ve"][s][:], m["mv"][s][:, 1:2], keep["ln_eps"][:], ALU.add))
                    nc.gpsimd.tensor_tensor(m["rstd"][s][:], m["ve"][s][:], keep["neg_half"][:, 0:1], ALU.pow).then_inc(rstd.sem, 1)

            def lows(t):
                if not mlp:
                    for s in slots:
                        pool.wait_ge(f_hi.sem, f_hi.now(t, s))
                        nc.gpsimd.tensor_tensor(m["f"][s][1][:], m["feat"][s][:], f32(m["f"][s][0][:]), ALU.subtract).then_inc(f_lo.sem, 1)

            def weigh(t, gr):
                for s in slots:
                    if gr == 0:
                        pool.wait_ge(share.sem, share.now(t, s))
                    pool.wait_ge(prod.sem, prod.now(t, at(gr, s)))
                    nc.gpsimd.tensor_tensor(
                        m["hid"][s][:].rearrange("p (e f) -> p e f", f=FE), m["prod"][s][:].rearrange("p (e f) -> p e f", f=FE),
                        m["share"][s][:, gr * (E // G):(gr + 1) * (E // G)].unsqueeze(2).to_broadcast([P, E // G, FE]),
                        ALU.mult).then_inc(hid.sem, 1)

            def body(t, step, ahead=True):
                for gr in range(G):
                    if gr == 1 and ahead:
                        front(t + 1, step)
                    if experts and gr:
                        weigh(t, gr)
                if ahead:
                    lows(t + 1)
                    if experts:
                        weigh(t + 1, 0)
            step = Steps(pool, p_steps)
            front(0, step)
            step.end()
            lows(0)
            if experts:
                weigh(0, 0)
            with nc.gpsimd.Fori(0, J - 1) as t:
                step = Steps(pool, p_steps, t)
                body(t, step)
            step.end(J - 1)
            body(J - 1, None, False)

        @block.vector
        def _(v):
            def front(t, step):
                if experts:
                    for s in slots:
                        v.wait_ge(attn.sem, attn.now(t, s))
                        nc.vector.tensor_tensor(m["tmp"][s][:], A(s)[:, 0:D], gate_row[:, s, 0, :], ALU.mult).then_inc(attn_used.sem, 1)
                        v.wait_ge(attn_used.sem, attn_used.now(t, s))
                        step(nc.vector.tensor_tensor(row(keep["x"], s, t), row(keep["x"], s, t), m["tmp"][s][:], ALU.add))
                if not mlp:
                    moments(nc, v, step, keep["spare"], [(m["stats"][s][:], m["mv"][s][:], row(keep["x"], s, t)) for s in slots], moment)

            def norm(t):
                for s in slots:
                    v.wait_ge(rstd.sem, rstd.now(t, s))
                    if mlp:
                        nc.vector.tensor_scalar(m["xn"][s][:], row(keep["r2"], s, t), m["rstd"][s][:], None, ALU.mult).then_inc(xn.sem, 1)
                    else:
                        nc.vector.tensor_scalar(m["xn"][s][:], row(keep["x"], s, t), m["mv"][s][:, 0:1], m["rstd"][s][:],
                                                ALU.subtract, ALU.mult).then_inc(xn.sem, 1)

            def mlp_low(t, s):
                if mlp:
                    v.wait_ge(f_hi.sem, f_hi.now(t, s))
                    nc.vector.tensor_tensor(flat(m["f"][s][1][:]), GATE(s)[:, 0:D], f32(flat(m["f"][s][0][:])),
                                            ALU.subtract).then_inc(f_lo.sem, 1)

            def routing(t, s, step):
                v.wait_ge(routed.sem, routed.now(t, s))
                nc.vector.memset(keep["spare"][:], 0.0)
                step(nc.vector.max(m["best"][s][:], TURN(s)[:, 0:E]))
                nc.vector.tensor_tensor(m["lead"][s][:], m["best"][s][:, 0:1], m["best"][s][:, 1:2], ALU.subtract).then_inc(lead.sem, 1)
                found = nc.vector.max_index(m["index"][s][:], m["best"][s][:], TURN(s)[:, 0:E])
                step(found)
                step(nc.vector.tensor_copy(m["place"][s][:], m["index"][s][:, 0:2]))
                v.wait_ge(lead_tanh.sem, lead_tanh.now(t, s))
                nc.vector.tensor_scalar(m["weight"][s][:, 0:1], m["lead_th"][s][:], 0.25, 0.25, ALU.mult, ALU.add)
                step(nc.vector.tensor_scalar(m["weight"][s][:, 1:2], m["lead_th"][s][:], -0.25, 0.25, ALU.mult, ALU.add))
                nc.vector.tensor_scalar(m["first"][s][:], m["iota"][:], m["place"][s][:, 0:1], m["weight"][s][:, 0:1], ALU.is_equal, ALU.mult)
                step(nc.vector.tensor_scalar(m["second"][s][:], m["iota"][:], m["place"][s][:, 1:2], m["weight"][s][:, 1:2], ALU.is_equal, ALU.mult))
                nc.vector.tensor_tensor(m["share"][s][:], m["first"][s][:], m["second"][s][:], ALU.add).then_inc(share.sem, 1)

            def product(t, gr, s, step):
                v.wait_ge(th.sem, th.now(t, at(gr, s)))
                step(nc.vector.scalar_tensor_tensor(m["silu"][s][:], m["th"][s][:], 1.0, GATE(s)[:, 0:W], ALU.add, ALU.mult))
                o = m["prod"][s][:] if experts else m["hid"][s][:, 0:W]
                nc.vector.tensor_tensor(o, m["silu"][s][:], UP(s)[:, 0:W], ALU.mult).then_inc(prod.sem, 1)

            def add_to_x(t, s, step):
                v.wait_ge(down.sem, down.now(t, s))
                gate = gate_row[:, s, which_gate, :]
                if mlp:
                    step(nc.vector.tensor_tensor(m["tmp"][s][:], A(s)[:, 0:D], row(keep["r2"], s, t), ALU.add))
                    step(nc.vector.tensor_tensor(m["tmp"][s][:], m["tmp"][s][:], gate, ALU.mult))
                else:
                    step(nc.vector.tensor_tensor(m["tmp"][s][:], A(s)[:, 0:D], gate, ALU.mult))
                nc.vector.tensor_tensor(row(keep["x"], s, t), row(keep["x"], s, t), m["tmp"][s][:], ALU.add).then_inc(x_out.sem, 1)

            def body(t, step, ahead=True):
                if ahead:
                    front(t + 1, step)
                if cut:
                    cut.scale(v, t)
                for gr in range(G):
                    if gr == G - 1 and ahead:
                        norm(t + 1)
                    for s in slots:
                        v.wait_ge(h_hi.sem, h_hi.now(t, at(gr, s)))
                        nc.vector.tensor_tensor(flat(m["h"][s][1][:]), TURN(s)[:, 0:3 * P], f32(flat(m["h"][s][0][:])),
                                                ALU.subtract).then_inc(h_lo.sem, 1)
                        if gr + 1 < G:
                            product(t, gr + 1, s, step)
                if cut:
                    cut.take_lo(v, t)
                for s in slots:
                    if ahead:
                        mlp_low(t + 1, s)
                    add_to_x(t, s, step)
                    if ahead:
                        if experts:
                            routing(t + 1, s, step)
                        product(t + 1, 0, s, step)
            if experts:
                v.wait_ge(ready, 16)
            if mlp:
                v.wait_ge(ready, 32)
                nc.vector.tensor_scalar(m["s_down_half"][:], m["s_down"][:], 0.5, None, ALU.mult)
            if not experts:
                for s in slots:
                    nc.vector.memset(m["hid"][s][:, W:3 * P], 0.0)
            step = Steps(v, v_steps)
            front(0, step)
            norm(0)
            for s in slots:
                mlp_low(0, s)
                if experts:
                    routing(0, s, step)
                product(0, 0, s, step)
            step.end()
            with nc.vector.Fori(0, J - 1) as t:
                step = Steps(v, v_steps, t)
                body(t, step)
            step.end(J - 1)
            step = Steps(v, v_steps)
            body(J - 1, step, False)
            step.end()

        @block.scalar
        def _(act):
            def front(t):
                if experts:
                    act.wait_ge(attn.sem, attn.before(t, NS - 1))
                    nc.scalar.copy(m["st"][0][:], lay0["states"][:, bass.ds(t * P, P)]).then_inc(st_hi.sem, 1)
                if mlp:
                    for s in slots:
                        nc.scalar.activation(m["feat"][s][:].rearrange("p k n -> p (k n)"), row(keep["r2"], s, t), ACT.Square,
                                             accum_out=m["mv"][s][:, 0:1]).then_inc(moment.sem, 1)

            def features(t, s):
                act.wait_ge(xT.sem, xT.now(t, s))
                if mlp:
                    nc.scalar.copy(flat(m["f"][s][0][:]), GATE(s)[:, 0:D]).then_inc(f_hi.sem, 1)
                    return
                for c in range(KC):
                    scale, shift = mod_col[:, 4 * KC + c, s:s + 1], mod_col[:, 3 * KC + c, s:s + 1]
                    ps = GATE(s)[:, c * P:(c + 1) * P]
                    nc.scalar.activation(m["feat"][s][:, c, :], ps, ACT.Identity, bias=shift, scale=scale)
                    last = nc.scalar.activation(m["f"][s][0][:, c, :], ps, ACT.Identity, bias=shift, scale=scale)
                last.then_inc(f_hi.sem, 1)

            def lead_of(t, s):
                act.wait_ge(lead.sem, lead.now(t, s))
                nc.scalar.activation(m["lead_th"][s][:], m["lead"][s][:], ACT.Tanh, scale=0.5).then_inc(lead_tanh.sem, 1)

            def tanh(t, gr, s):
                act.wait_ge(gu.sem, gu.now(t, at(gr, s)))
                nc.scalar.activation(m["th"][s][:], GATE(s)[:, 0:W], ACT.Tanh, scale=0.5).then_inc(th.sem, 1)

            def body(t, ahead=True):
                if ahead:
                    front(t + 1)
                if cut:
                    cut.take_hi(act, t)
                for gr in range(G):
                    if gr == G - 1 and ahead:
                        for s in slots:
                            features(t + 1, s)
                    for s in slots:
                        act.wait_ge(hT.sem, hT.now(t, at(gr, s)))
                        nc.scalar.copy(flat(m["h"][s][0][:]), TURN(s)[:, 0:3 * P]).then_inc(h_hi.sem, 1)
                        if gr + 1 < G:
                            tanh(t, gr + 1, s)
                if ahead:
                    for s in slots:
                        if experts:
                            lead_of(t + 1, s)
                        tanh(t + 1, 0, s)
            front(0)
            for s in slots:
                features(0, s)
            for s in slots:
                if experts:
                    lead_of(0, s)
                tanh(0, 0, s)
            with nc.scalar.Fori(0, J - 1) as t:
                body(t)
            body(J - 1, False)

        @block.tensor
        def _(pe):
            def attention(t, used):
                pe.wait_ge(st_lo.sem, st_lo.now(t))
                for s in slots:
                    pe.wait_ge(x_out.sem, used(s))
                    product3(nc, A(s)[:, 0:D], [([w[:] for w in m["st"]], [w[:, OUT0 + s * D:OUT0 + (s + 1) * D] for w in lay0["w0"]])]
                             ).then_inc(attn.sem, 1)

            def normed(t):
                for s in slots:
                    pe.wait_ge(xn.sem, xn.now(t, s))
                    pe.wait_ge(prod.sem, prod.before(t, at(G - 1, s)))
                    for c in range(KC):
                        last = nc.tensor.transpose(GATE(s)[:, c * P:(c + 1) * P], m["xn"][s][:, c * P:(c + 1) * P], keep["ident"][:])
                    last.then_inc(xT.sem, 1)

            def gate_up(t, gr, s):
                if gr == 0:
                    pe.wait_ge(f_lo.sem, f_lo.now(t, s))
                for which, ps in enumerate((GATE(s), UP(s))):
                    terms = []
                    for c in range(KC):
                        if experts:
                            w = [x[:, c, gr * W:(gr + 1) * W] for x in (lay0["w_up"] if which else lay0["w_gate"])]
                        else:
                            w = [x[:, c, (2 * gr + which) * W:(2 * gr + which + 1) * W] for x in w_in]
                        terms.append(([x[:, c, :] for x in m["f"][s]], w))
                    last = product3(nc, ps[:, 0:W], terms)
                last.then_inc(gu.sem, 1)

            def turn(t, gr, s):
                pe.wait_ge(hid.sem, hid.now(t, at(gr, s)))
                for c in range(3):
                    last = nc.tensor.transpose(TURN(s)[:, c * P:(c + 1) * P], m["hid"][s][:, c * P:(c + 1) * P], keep["ident"][:])
                last.then_inc(hT.sem, 1)

            def route(t, s):
                pe.wait_ge(f_lo.sem, f_lo.now(t, s))
                product3(nc, TURN(s)[:, 0:E], [([x[:, c, :] for x in m["f"][s]], [w[:, ROUT + c * E:ROUT + (c + 1) * E] for w in lay0["w0"]])
                                               for c in range(KC)]).then_inc(routed.sem, 1)

            def body(t, ahead=True):
                if experts and ahead:
                    attention(t + 1, lambda s: x_out.before(t, s))
                for gr in range(G):
                    if gr == G - 1 and ahead:
                        normed(t + 1)
                    for s in slots:
                        turn(t, gr, s)
                        if gr + 1 < G:
                            gate_up(t, gr + 1, s)
                    for s in slots:
                        pe.wait_ge(h_lo.sem, h_lo.now(t, at(gr, s)))
                        if experts and gr == 0 and ahead:
                            pe.wait_ge(attn_used.sem, attn_used.now(t + 1, s))
                        last = product3(nc, A(s)[:, 0:D], [([x[:, c, :] for x in m["h"][s]], [w[:, gr * 3 + c, :] for w in w_down])
                                                           for c in range(3)], first=gr == 0, last=gr == G - 1)
                        if gr == G - 1:
                            last.then_inc(down.sem, 1)
                            if ahead:
                                if experts:
                                    route(t + 1, s)
                                gate_up(t + 1, 0, s)
            if experts:
                attention(0, lambda s: x_out.before(0, s))
            normed(0)
            for s in slots:
                if experts:
                    route(0, s)
                gate_up(0, 0, s)
            with nc.tensor.Fori(0, J - 1) as t:
                body(t)
            body(J - 1, False)
    for sig in signals.values():
        if sig is not v_steps and sig is not p_steps:
            sig.pass_turns(J)


def retention(nc, sem, a, bank, keep, m):
    NS, HG = B, H // 4
    QK = 2 * H * DK
    m.slots(["xn", "h", "hn"], [D], NS)
    m.pair_slots(["f"], [KC, P], NS)
    m.slots(["work"], [2, QK], NS)
    m.slots(["rot"], [QK], NS)
    m.slots(["sgate"], [HV], NS)
    m.pair_slots(["k"], [H * DK], NS)
    m.pair_slots(["v"], [HV], NS)
    m.pair_slots(["qkT"], [4, P], NS)
    m.pair_slots(["score"], [HG, 4, P], NS)
    m.slots(["state"], [HG, 4 * DV], NS)
    m.pair_slots(["S"], [HG, 4 * DV], NS)
    m.slots(["stats"], [6], NS)
    m.slots(["mv"], [2], NS)
    m.slots(["ve", "rstd", "sumsq", "hve", "hrstd"], [1], NS)
    m.slots(["hsum", "heps", "hrms"], [H], NS)
    m.add("rope", [2, QK])
    m.add("state_mask", [HG, 4 * DV])
    m.add("state_gain", [HG])
    m.add("pool_spare", [NS])
    cut = Cut(nc, sem, m, a, "cut2", [
        ("w_mlp", F32, keep["w_mlp"], by_column(nc, lambda k: keep["norm16"][:, 1, k:k + 1])),
        ("w_mlp_down", F32, keep["w_mlp_down"], by_constant(nc, 0.5))])

    def signal(name, per_turn=NS, ahead=False):
        return Signal(sem("ret_" + name), per_turn, ahead)
    (moment, rstd, xn, h_ready, sumsq, hrstd, hn, hT, f_hi, f_lo, qk, val, gate) = (signal(n) for n in (
        "moment", "rstd", "xn", "h", "sumsq", "hrstd", "hn", "hT", "f_hi", "f_lo", "qk", "val", "gate"))
    terms, rot, k_lo, v_hi, v_lo, tanh, sgate, qkT, qkT_hi, qkT_lo = (signal(n) for n in (
        "rope_terms", "rot", "k_lo", "v_hi", "v_lo", "tanh", "sgate", "qkT", "qkT_hi", "qkT_lo"))
    scores, copied_a, copied_v, masked, s_hi, s_lo = (signal(n) for n in (
        "scores", "copied_act", "copied_dve", "masked", "score_hi", "score_lo"))
    o_done, st_done, st_sum, S_hi = (signal(n) for n in ("o", "state_product", "state_sum", "S_hi"))
    S_lo = signal("S_lo", NS, True)
    square, hsum, hrms, on, oT, oT_hi, oT_lo, proj = (signal(n) for n in (
        "square", "head_sum", "head_rms", "out_norm", "oT", "oT_hi", "oT_lo", "proj"))
    r2_out = signal("r2")
    k_hi = signal("k_hi")
    rope_in, ready, zeroed = (sem(f"ret_{n}") for n in ("rope_in", "ready", "zeroed"))
    v_steps, p_steps = signal("v_steps", 10), signal("p_steps", 3 * NS)
    slots = range(NS)

    def bk(s, i): return bank[4 * s + i]

    with nc.Block() as block:
        @block.sync
        def _(sp):
            for sig in (S_lo, cut.scaled):
                sp.sem_inc(sig.sem, sig.per_turn)
            sp.dma_start(m["state_mask"][:], a["state_mask"]).then_inc(ready, 16)
            sp.dma_start(m["state_gain"][:], a["state_gain"]).then_inc(ready, 16)
            sp.dma_start(m["rope"][:], a["rope"][0]).then_inc(rope_in, 16)
            with nc.sync.Fori(0, J - 1) as t:
                cut.load(sp, t)
                sp.wait_ge(terms.sem, terms.now(t, NS - 1))
                sp.dma_start(m["rope"][:], a["rope"][bass.ds(t + 1, 1)].rearrange("a p c n -> p (a c) n")).then_inc(rope_in, 16)
            cut.load(sp, J - 1)

        @block.gpsimd
        def _(pool):
            for s in slots:
                for x in (*m["S"][s], m["state"][s]):
                    last = nc.gpsimd.memset(x[:] if x is m["state"][s] else f32(x[:]), 0.0).then_inc(zeroed, 1)
            with nc.gpsimd.Fori(0, J) as t:
                step = Steps(pool, p_steps, t)

                def rsqrt(got, out, tmp, x, eps, gone):
                    for s in slots:
                        pool.wait_ge(got.sem, got.now(t, s))
                        step(nc.gpsimd.tensor_tensor(tmp[s][:], x(s), eps[:], ALU.add))
                        nc.gpsimd.tensor_tensor(out[s][:], tmp[s][:], keep["neg_half"][:, 0:out[s].shape[1]],
                                                ALU.pow).then_inc(gone.sem, 1)
                rsqrt(moment, m["rstd"], m["ve"], lambda s: m["mv"][s][:, 1:2], keep["ln_eps"], rstd)
                rsqrt(sumsq, m["hrstd"], m["hve"], lambda s: m["sumsq"][s][:], keep["rms_eps"], hrstd)
                for s in slots:
                    pool.wait_ge(terms.sem, terms.now(t, s))
                    nc.gpsimd.tensor_tensor(m["rot"][s][:], m["work"][s][:, 0, :], m["work"][s][:, 1, :], ALU.add).then_inc(rot.sem, 1)
                for s in slots:
                    pool.wait_ge(k_hi.sem, k_hi.now(t, s))
                    nc.gpsimd.tensor_tensor(m["k"][s][1][:], m["rot"][s][:, H * DK:QK], f32(m["k"][s][0][:]), ALU.subtract).then_inc(k_lo.sem, 1)
                for s in slots:
                    pool.wait_ge(copied_a.sem, copied_a.now(t, s))
                    pool.wait_ge(copied_v.sem, copied_v.now(t, s))
                    nc.gpsimd.tensor_tensor(m["pool_spare"][:, s:s + 1], keep["ln_eps"][:], keep["ln_eps"][:], ALU.add)
                    w = m["work"][s][:].rearrange("p a n -> p (a n)").rearrange("p (h i) -> p h i", i=P)
                    nc.gpsimd.affine_select(out=w, in_=w, pattern=[[0, H], [1, P]], compare_op=ALU.is_ge, fill=0.0,
                                            base=0, channel_multiplier=-1).then_inc(masked.sem, 1)
                rsqrt(hsum, m["hrms"], m["heps"], lambda s: m["hsum"][s][:], keep["head_eps"], hrms)
                for s in slots:
                    pool.wait_ge(S_hi.sem, S_hi.now(t, s))
                    nc.gpsimd.tensor_tensor(flat(m["S"][s][1][:]), flat(m["state"][s][:]), f32(flat(m["S"][s][0][:])),
                                            ALU.subtract).then_inc(S_lo.sem, 1)
                step.end(J)

        @block.vector
        def _(v):
            v.wait_ge(ready, 32)
            v.wait_ge(zeroed, 3 * NS)
            with nc.vector.Fori(0, J) as t:
                step = Steps(v, v_steps, t)
                moments(nc, v, step, keep["spare"], [(m["stats"][s][:], m["mv"][s][:], row(keep["x"], s, t)) for s in slots], moment)
                for s in slots:
                    v.wait_ge(rstd.sem, rstd.now(t, s))
                    step(nc.vector.tensor_scalar(m["xn"][s][:], row(keep["x"], s, t), m["mv"][s][:, 0:1], m["rstd"][s][:],
                                                 ALU.subtract, ALU.mult))
                    step(nc.vector.tensor_tensor(m["xn"][s][:], m["xn"][s][:], keep["shift_scale"][:, s, 1, :], ALU.mult))
                    nc.vector.tensor_tensor(m["h"][s][:], m["xn"][s][:], keep["shift_scale"][:, s, 0, :], ALU.add).then_inc(h_ready.sem, 1)
                for s in slots:
                    v.wait_ge(hrstd.sem, hrstd.now(t, s))
                    nc.vector.tensor_scalar(m["hn"][s][:], m["h"][s][:], m["hrstd"][s][:], None, ALU.mult).then_inc(hn.sem, 1)

                def low(pair, ps, n, got, gone):
                    for s in slots:
                        v.wait_ge(got.sem, got.now(t, s))
                        lo, hi = [x[:] if len(x.shape) == 2 else flat(x[:]) for x in (pair[s][1], pair[s][0])]
                        nc.vector.tensor_tensor(lo, ps(s)[:, 0:n], f32(hi), ALU.subtract).then_inc(gone.sem, 1)
                low(m["f"], lambda s: bk(s, 0), D, f_hi, f_lo)
                v.wait_ge(rope_in, t * 16 + 16)
                for s in slots:
                    v.wait_ge(qk.sem, qk.now(t, s))
                    nc.vector.tensor_tensor(m["work"][s][:, 0, :], bk(s, 1)[:], m["rope"][:, 0, :], ALU.mult)
                    split = [x.rearrange("p (h c d) -> p h c d", c=2, d=DK // 2) for x in (m["work"][s][:, 1, :], bk(s, 1)[:], m["rope"][:, 1, :])]
                    for c in range(2):
                        last = nc.vector.tensor_tensor(split[0][:, :, c, :], split[1][:, :, 1 - c, :], split[2][:, :, c, :], ALU.mult)
                    last.then_inc(terms.sem, 1)
                for s in slots:
                    v.wait_ge(tanh.sem, tanh.now(t, s))
                    nc.vector.scalar_tensor_tensor(m["sgate"][s][:], m["sgate"][s][:], 1.0, bk(s, 3)[:], ALU.add,
                                                   ALU.mult).then_inc(sgate.sem, 1)
                low(m["v"], lambda s: bk(s, 2), HV, v_hi, v_lo)
                low(m["qkT"], lambda s: bk(s, 0), 4 * P, qkT_hi, qkT_lo)
                cut.scale(v, t)
                for s in slots:
                    v.wait_ge(scores.sem, scores.now(t, s))
                    for h in (2, 3):
                        last = nc.vector.tensor_copy(score_view(m["work"][s])[:, :, h, :], by_head(bk(s, h)))
                    last.then_inc(copied_v.sem, 1)
                for s in slots:
                    v.wait_ge(s_hi.sem, s_hi.now(t, s))
                    nc.vector.tensor_tensor(m["score"][s][1][:].rearrange("p g h i -> p (g h i)"), flat(m["work"][s][:]),
                                            f32(m["score"][s][0][:]).rearrange("p g h i -> p (g h i)"), ALU.subtract).then_inc(s_lo.sem, 1)
                for s in slots:
                    v.wait_ge(st_done.sem, st_done.now(t, s))
                    v.wait_ge(s_lo.sem, s_lo.now(t, s))
                    step(nc.vector.tensor_tensor(m["work"][s][:, 1, :], bk(s, 1)[:], flat(m["state_mask"][:]), ALU.mult))
                    for g in range(HG):
                        last = nc.vector.scalar_tensor_tensor(m["state"][s][:, g, :], m["state"][s][:, g, :], m["state_gain"][:, g:g + 1],
                                                              m["work"][s][:, 1, g * 4 * DV:(g + 1) * 4 * DV], ALU.mult, ALU.add)
                    last.then_inc(st_sum.sem, 1)
                cut.take_lo(v, t)
                for s in slots:
                    v.wait_ge(square.sem, square.now(t, s))
                    nc.vector.tensor_reduce(m["hsum"][s][:], m["work"][s][:, 0, :].rearrange("p (h d) -> p h d", d=DV), AX.X,
                                            ALU.add).then_inc(hsum.sem, 1)
                for s in slots:
                    v.wait_ge(hrms.sem, hrms.now(t, s))
                    heads = lambda x: x.rearrange("p (h d) -> p h d", d=DV)
                    step(nc.vector.tensor_tensor(heads(m["rot"][s][:]), heads(bk(s, 0)[:]),
                                                 m["hrms"][s][:].unsqueeze(2).to_broadcast([P, H, DV]), ALU.mult))
                    nc.vector.tensor_tensor(m["rot"][s][:], m["rot"][s][:], m["sgate"][s][:], ALU.mult).then_inc(on.sem, 1)
                low(m["qkT"], lambda s: bk(s, 2), 4 * P, oT_hi, oT_lo)
                for s in slots:
                    v.wait_ge(proj.sem, proj.now(t, s))
                    nc.vector.tensor_tensor(row(keep["r2"], s, t), bk(s, 3)[:, 0:D], m["h"][s][:], ALU.add).then_inc(r2_out.sem, 1)
                step.end(J)

        @block.scalar
        def _(act):
            with nc.scalar.Fori(0, J) as t:
                for s in slots:
                    act.wait_ge(h_ready.sem, h_ready.now(t, s))
                    nc.scalar.activation(m["hn"][s][:], m["h"][s][:], ACT.Square, accum_out=m["sumsq"][s][:]).then_inc(sumsq.sem, 1)

                def high(pair, src, got, gone):
                    for s in slots:
                        act.wait_ge(got.sem, got.now(t, s))
                        hi = pair[s][0]
                        nc.scalar.copy(hi[:] if len(hi.shape) == 2 else flat(hi[:]), src(s)).then_inc(gone.sem, 1)
                high(m["f"], lambda s: bk(s, 0)[:, 0:D], hT, f_hi)
                for s in slots:
                    act.wait_ge(gate.sem, gate.now(t, s))
                    nc.scalar.activation(m["sgate"][s][:], bk(s, 3)[:], ACT.Tanh, scale=0.5).then_inc(tanh.sem, 1)
                high(m["v"], lambda s: bk(s, 2)[:], val, v_hi)
                high(m["k"], lambda s: m["rot"][s][:, H * DK:QK], rot, k_hi)
                high(m["qkT"], lambda s: bk(s, 0)[:], qkT, qkT_hi)
                cut.take_hi(act, t)
                for s in slots:
                    act.wait_ge(scores.sem, scores.now(t, s))
                    for h in (0, 1):
                        last = nc.scalar.copy(score_view(m["work"][s])[:, :, h, :], by_head(bk(s, h)))
                    last.then_inc(copied_a.sem, 1)
                for s in slots:
                    act.wait_ge(masked.sem, masked.now(t, s))
                    nc.scalar.copy(m["score"][s][0][:].rearrange("p g h i -> p (g h i)"), flat(m["work"][s][:])).then_inc(s_hi.sem, 1)
                for s in slots:
                    act.wait_ge(o_done.sem, o_done.now(t, s))
                    nc.scalar.activation(m["work"][s][:, 0, :], bk(s, 0)[:], ACT.Square).then_inc(square.sem, 1)
                for s in slots:
                    act.wait_ge(st_sum.sem, st_sum.now(t, s))
                    nc.scalar.copy(flat(m["S"][s][0][:]), flat(m["state"][s][:])).then_inc(S_hi.sem, 1)
                high(m["qkT"], lambda s: bk(s, 2)[:], oT, oT_hi)

        @block.tensor
        def _(pe):
            pe.wait_ge(zeroed, 3 * NS)
            with nc.tensor.Fori(0, J) as t:
                def transposes(ps, src, n, got, gone):
                    for s in slots:
                        pe.wait_ge(got.sem, got.now(t, s))
                        for c in range(n):
                            last = nc.tensor.transpose(ps(s)[:, c * P:(c + 1) * P], src[s][:, c * P:(c + 1) * P], keep["ident"][:])
                        last.then_inc(gone.sem, 1)
                transposes(lambda s: bk(s, 0), m["hn"], KC, hn, hT)
                for s in slots:
                    pe.wait_ge(f_lo.sem, f_lo.now(t, s))
                    for i, sig in ((0, qk), (2, gate), (1, val)):
                        product3(nc, bk(s, 1 + i)[:], [([x[:, c, :] for x in m["f"][s]], [w[:, c, i * 512:(i + 1) * 512] for w in keep["w_qkvg"]])
                                                       for c in range(KC)]).then_inc(sig.sem, 1)
                transposes(lambda s: bk(s, 0), m["rot"], 4, rot, qkT)
                for s in slots:
                    pe.wait_ge(qkT_lo.sem, qkT_lo.now(t, s))
                    pe.wait_ge(v_lo.sem, v_lo.now(t, s))
                    pe.wait_ge(sgate.sem, sgate.now(t, s))
                    for g in range(HG):
                        for h in range(4):
                            part = slice(h * DK, (h + 1) * DK)
                            last = product3(nc, bk(s, h)[:, g * P:(g + 1) * P],
                                            [([x[part, 2 + g, :] for x in m["qkT"][s]], [x[part, g, :] for x in m["qkT"][s]])])
                    last.then_inc(scores.sem, 1)
                for s in slots:
                    pe.wait_ge(k_lo.sem, k_lo.now(t, s))
                    pe.wait_ge(copied_a.sem, copied_a.now(t, s))
                    for g in range(HG):
                        cols = slice(g * 4 * DV, (g + 1) * 4 * DV)
                        last = product3(nc, bk(s, 1)[:, cols], [([x[:, g * P:(g + 1) * P] for x in m["k"][s]], [x[:, cols] for x in m["v"][s]])])
                    last.then_inc(st_done.sem, 1)
                for s in slots:
                    pe.wait_ge(S_lo.sem, S_lo.before(t, s))
                    pe.wait_ge(s_lo.sem, s_lo.now(t, s))
                    for g in range(HG):
                        product3(nc, bk(s, 0)[:, g * 4 * DV:(g + 1) * 4 * DV], [([x[:, g, :] for x in m["qkT"][s]], [x[:, g, :] for x in m["S"][s]])],
                                 first=g == 0, last=False)
                    for n in range(H):
                        g, h = n // 4, n % 4
                        last = product3(nc, bk(s, 0)[:, n * DV:(n + 1) * DV],
                                        [([x[:, g, h, :] for x in m["score"][s]], [x[:, n * DV:(n + 1) * DV] for x in m["v"][s]])],
                                        first=False, last=n == H - 1)
                    last.then_inc(o_done.sem, 1)
                transposes(lambda s: bk(s, 2), m["rot"], 4, on, oT)
                for s in slots:
                    pe.wait_ge(oT_lo.sem, oT_lo.now(t, s))
                    product3(nc, bk(s, 3)[:, 0:D], [([x[:, c, :] for x in m["qkT"][s]], [w[:, c, :] for w in keep["w_o"]])
                                                    for c in range(HV // P)]).then_inc(proj.sem, 1)


def score_view(work):
    return work[:].rearrange("p a n -> p (a n)").rearrange("p (g h i) -> p g h i", g=H // 4, h=4)


def by_head(bank):
    return bank[:, 0:2 * P].rearrange("p (g i) -> p g i", i=P)




def kernel(**inputs):
    import concourse.bacc as _bacc
    from concourse.bass_utils import run_bass_kernel_spmd as _run

    def col(v):
        return np.asarray(v).reshape(KC, P).T

    def rows(w):
        w = np.asarray(w)
        return w.reshape(-1, P, w.shape[-1]).transpose(1, 0, 2)

    def pieces(w, n):
        return w.reshape(P, n, -1).transpose(1, 0, 2)

    def column_pieces(w, n):
        return w.reshape(P, w.shape[1], n, -1).transpose(2, 0, 1, 3)

    def by_group(gate, up):
        return np.concatenate([w[:, g * IW:(g + 1) * IW] for g in range(IG) for w in (gate, up)], axis=1)

    def down_rows(w):
        o = np.zeros((IG, 3 * P, w.shape[-1]), w.dtype)
        o[:, :IW] = w.reshape(IG, IW, -1)
        return rows(o.reshape(IG * 3 * P, -1))

    g = {k: np.asarray(v) for k, v in inputs.items()}
    a = {}
    a["x"] = g["L0_attn_x"]
    a["c"] = np.stack([rows(g[f"L{l}_c"].T) for l in range(2)], axis=1)
    a["wmod"] = np.stack([rows(g[f"L{l}_wmod"]) for l in range(2)])
    a["gate"], a["time_first"] = g["L0_attn_gate"], g["L0_attn_time_first"]
    a["time_decay"] = g["L0_attn_time_decay"].reshape(S, 1)
    a["ln_cols"] = np.stack([col(g["L0_attn_ln_gamma"]), col(g["L0_attn_ln_beta"])], axis=1)
    a["ident"] = np.eye(P, dtype=np.float32)
    a["w_mix"] = rows(g["L0_attn_W_shift"].T).reshape(P, -1)
    a["w_kv"] = rows(np.concatenate([g["L0_attn_W_key"], g["L0_attn_W_value"]], axis=0).T).reshape(P, -1)
    a["w_out0"] = g["L0_attn_W_output"].T
    a["router"] = rows(g["L0_ffn_router_w"]).reshape(P, -1)
    for name, key in (("w_gate", "gate_w"), ("w_up", "up_w")):
        a[name] = pieces(rows(g["L0_ffn_" + key].transpose(1, 0, 2).reshape(D, E * FE)), J // 2)
    a["w_down"] = pieces(rows(g["L0_ffn_down_w"].reshape(E * FE, D)), J // 2)

    qkvg = np.concatenate([g["L1_attn_" + n] for n in ("q_w", "k_w", "v_w", "g_w")], axis=1)
    a["w_qkvg"] = column_pieces(rows(qkvg), J)
    a["w_o"] = column_pieces(rows(g["L1_attn_o_w"]), J)
    a["norm_cols"] = np.stack([col(g["L1_attn_attn_norm_w"]), col(g["L1_attn_mlp_norm_w"])], axis=1)
    a["gnorm_col"] = np.tile(g["L1_attn_gnorm_w"], 2).reshape(P, 1)
    mlp = g["L1_attn_gate_w"]
    a["w_mlp"] = column_pieces(rows(by_group(mlp[:, :INTER], mlp[:, INTER:])), J)
    a["w_mlp_down"] = column_pieces(down_rows(g["L1_attn_down_w"]), J)
    a["w_ffn"] = column_pieces(rows(by_group(g["L1_ffn_wq_gate"].T, g["L1_ffn_wq_up"].T)), J)
    a["w_ffn_down"] = column_pieces(down_rows(g["L1_ffn_wq_down"].T), J)
    a["s_ffn"] = by_group(g["L1_ffn_s_gate"][None], g["L1_ffn_s_up"][None])[0]
    a["s_ffn_down"] = g["L1_ffn_s_down"]
    a.update(shape_tables())

    nc = _bacc.Bacc("TRN2", target_bir_lowering=False, num_devices=1)
    a = {k: np.ascontiguousarray(v) for k, v in a.items()}
    aps = {k: nc.dram_tensor("in_" + k, v.shape, mybir.dt.from_np(v.dtype), kind="ExternalInput").ap() for k, v in a.items()}
    out = nc.dram_tensor("out_0", (B, T, D), F32, kind="ExternalOutput").ap()
    build(nc, aps, out)
    r = _run(nc, [{"in_" + k: v for k, v in a.items()}], core_ids=[0])
    return r.results[0]["out_0"]


def shape_tables():
    gamma = 1.0 - np.exp2(-5.0 - np.arange(H, dtype=np.float64))
    i = np.arange(P, dtype=np.float64)[:, None]
    q_gain = gamma ** (i + 1) * DK ** -0.5
    k_gain = gamma ** -(i + 1)
    inv_freq = (np.float32(1.0) / np.float32(10000.0) ** (np.arange(0, DK, 2, dtype=np.float32) / np.float32(DK))).astype(np.float32)
    angle = np.arange(T, dtype=np.float32)[:, None] * inv_freq
    cos = np.cos(angle.astype(np.float64)).reshape(J, P, 1, DK // 2)
    sin = np.sin(angle.astype(np.float64)).reshape(J, P, 1, DK // 2)
    full_cos = np.concatenate([cos, cos], axis=-1)
    full_sin = np.concatenate([-sin, sin], axis=-1)
    table = np.stack([np.concatenate([f * q_gain[None, :, :, None], f * k_gain[None, :, :, None]], axis=2)
                      for f in (full_cos, full_sin)], axis=2)
    tile_decay = gamma ** P
    state_mask = np.zeros((4, DK, 2, 4, DV))
    state_gain = np.zeros((4, DK, 2))
    for grp in range(2):
        for h in range(4):
            state_mask[h, :, grp, h, :] = tile_decay[grp * 4 + h]
            state_gain[h, :, grp] = tile_decay[grp * 4 + h]
    return {"iota": np.arange(E, dtype=np.float32), "rope": table.reshape(J, P, 2, 2 * H * DK).astype(np.float32),
            "state_mask": state_mask.reshape(P, 2, 4 * DV).astype(np.float32),
            "state_gain": state_gain.reshape(P, 2).astype(np.float32)}
```

```python
from contextlib import ExitStack

import numpy as np
import concourse.bass as bass
from concourse import mybir

F32 = mybir.dt.float32
F32R = mybir.dt.float32r
I32 = mybir.dt.int32
U32 = mybir.dt.uint32
ALU = mybir.AluOpType
ACT = mybir.ActivationFunctionType
AX = mybir.AxisListType

P = 128
B, T, D = 2, 1024, 256
J = T // P
KC = D // P
S = 64
E, FE = 16, 96
EG = 4
GW = E * FE // EG
H, DK, DV = 8, 32, 64
HV = H * DV
INTER = 704
IG = 2
IW = INTER // IG
MODS = 6
LN_EPS = 1e-5
RMS_EPS = 1e-6
MIN_GATE = 0.25
ZERO_POINT = 128.0


class Signal:

    def __init__(self, sem, per_turn, ahead=False):
        self.sem, self.per_turn, self.ahead = sem, per_turn, ahead
        self.base = per_turn if ahead else 0

    def now(self, turn, k=0):
        return turn * self.per_turn + (self.base + k + 1)

    def before(self, turn, k=0):
        assert self.ahead
        return turn * self.per_turn + (self.base + k + 1 - self.per_turn)

    def pass_turns(self, turns):
        self.base += turns * self.per_turn

    def again(self, per_turn):
        self.per_turn = per_turn
        return self


class Steps:

    def __init__(self, eng, counts, turn=None):
        self.eng, self.counts, self.turn, self.k = eng, counts, turn, 0

    def __call__(self, instruction):
        instruction.then_inc(self.counts.sem, 1)
        self.eng.wait_ge(self.counts.sem, self.counts.now(0 if self.turn is None else self.turn, self.k))
        self.k += 1

    def end(self, turns=1):
        assert self.turn is None or self.k == self.counts.per_turn, (self.k, self.counts.per_turn)
        self.counts.base += turns * self.k


def f32(ap):
    return ap.bitcast(F32)


def product3(nc, out, terms, first=True, last=True):
    n = len(terms)
    for i, (lhs, rhs) in enumerate(terms):
        for k, (x, y) in enumerate(((0, 0), (0, 1), (1, 0))):
            done = nc.tensor.matmul(out, lhs[x], rhs[y], start=(first and i == 0 and k == 0),
                                    stop=(last and i == n - 1 and k == 2), skip_group_check=True)
    return done


class Memory(dict):

    def __init__(self, nc, stack, phase=""):
        self.nc, self.stack, self.phase = nc, stack, phase

    def add(self, name, shape, dt=F32):
        tile = self.stack.enter_context(self.nc.sbuf_tensor(self.phase + name, [P] + list(shape), dt))
        self[name] = tile
        return tile

    def pair(self, name, shape):
        both = [self.stack.enter_context(self.nc.sbuf_tensor(f"{self.phase}{name}_{x}", [P] + list(shape), F32R)) for x in ("hi", "lo")]
        self[name] = both
        return both

    def slots(self, names, shape, n, dt=F32):
        for name in names:
            self[name] = [self.stack.enter_context(self.nc.sbuf_tensor(f"{self.phase}{name}{s}", [P] + list(shape), dt))
                                   for s in range(n)]

    def pair_slots(self, names, shape, n):
        for name in names:
            self[name] = [[self.stack.enter_context(self.nc.sbuf_tensor(f"{self.phase}{name}{s}_{x}", [P] + list(shape), F32R))
                                    for x in ("hi", "lo")] for s in range(n)]


def flat(ap):
    return ap.rearrange("p a b -> p (a b)")


def row(tile, *index):
    *first, last = index
    ap = tile
    for i in first:
        ap = ap[:, i]
    return ap[:, bass.ds(last, 1), :].rearrange("p a d -> p (a d)")


MIX, DIAG = 0, KC * D
KV = DIAG + KC * P
OUT0 = KV + KC * P
ROUT = OUT0 + B * D
W0N = ROUT + KC * E


def build(nc, a, out):
    with ExitStack() as ctx:
        bank = [ctx.enter_context(nc.psum_tensor(f"bank{i}", [P, 512], F32)) for i in range(8)]

        def sem(name):
            return ctx.enter_context(nc.semaphore(name))

        keep = Memory(nc, ctx)
        keep.add("x", [B, J, D])
        keep.add("ident", [P])
        keep.add("neg_half", [H])
        keep.add("ln_eps", [1])
        keep.add("rms_eps", [1])
        keep.add("head_eps", [H])
        keep.add("norm_cols", [2, KC])
        keep.add("norm16", [2, KC])
        keep.add("gnorm_col", [1])
        keep.add("gnorm4", [1])
        keep.add("spare", [1])
        for l in range(2):
            keep.add(f"mod_col{l}", [MODS * KC, B])
            keep.add(f"gate_row{l}", [B, 2, D])
        keep.add("shift_scale", [B, 2, D])
        keep.pair("w_qkvg", [KC, 2 * D + 2 * HV])
        keep.pair("w_o", [HV // P, D])
        x_loaded = sem("x_loaded")
        with ExitStack() as early:
            lay0 = Memory(nc, early)
            lay0.pair("w0", [W0N])
            lay0.add("wkv_tok", [J, B, S])
            lay0.add("states", [T])
            lay0.add("decay", [1])
            lay0.add("ln_col", [2, KC])
            lay0.add("neg_u", [S])
            lay0.pair("w_gate", [KC, E * FE])
            lay0.pair("w_up", [KC, E * FE])
            lay0.pair("w_down", [E * FE // P, D])
            with ExitStack() as tmp:
                setup(nc, sem, a, bank, keep, lay0, Memory(nc, tmp, "setup_"), x_loaded)
            with ExitStack() as tmp:
                mix_and_key_value(nc, sem, a, bank, keep, lay0, Memory(nc, tmp, "mix_"), x_loaded)
            recurrence(nc, sem, bank, keep, lay0)
            signals = {}
            with ExitStack() as tmp:
                gated_mlp(nc, sem, a, bank, keep, Memory(nc, tmp, "experts_"), "experts", lay0, None, signals)
        keep.pair("w_mlp", [KC, IG * 2 * IW])
        keep.pair("w_mlp_down", [IG * 3, D])
        keep.add("r2", [B, J, D])
        with ExitStack() as tmp:
            retention(nc, sem, a, bank, keep, Memory(nc, tmp, "ret_"))
        keep.pair("w_ffn", [KC, IG * 2 * IW])
        keep.pair("w_ffn_down", [IG * 3, D])
        with ExitStack() as tmp:
            gated_mlp(nc, sem, a, bank, keep, Memory(nc, tmp, "mlp_"), "mlp", None, None, signals)
        with ExitStack() as tmp:
            gated_mlp(nc, sem, a, bank, keep, Memory(nc, tmp, "ffn_"), "ffn", None, out, signals)


def moments(nc, v, step, spare, tiles, gone, arrive=None):
    for s, (stats, mv, x) in enumerate(tiles):
        if arrive:
            arrive(s)
        else:
            nc.vector.memset(spare[:], 0.0)
        statistics = nc.vector.bn_stats(stats, x)
        if s:
            nc.vector.bn_aggr(tiles[s - 1][1], tiles[s - 1][0]).then_inc(gone.sem, 1)
        step(statistics)
    nc.vector.memset(spare[:], 0.0)
    nc.vector.bn_aggr(tiles[-1][1], tiles[-1][0]).then_inc(gone.sem, 1)


def setup(nc, sem, a, bank, keep, lay0, m, x_loaded):
    m.add("w_raw", [W0N])
    m.slots(["wmod"], [KC, MODS * D], 2)
    for name in ("c_col", "c_th", "c_sum", "c_silu"):
        m.add(name, [2, KC, B])
    m.add("c_wide", [2 * KC * B, P])
    for name in ("gate_bc", "gate_th", "mix_gain", "keep_gain"):
        m.add(name, [D])
    m.add("u_bc", [S])
    m.add("u_exp", [S])
    m.add("dec_raw", [1])
    m.slots(["sign", "size"], [512], 2)
    small, loaded, zeroed, c_tanh, gate_tanh, exps, silu, products, raw_ready, hi_ready, steps = (
        sem(n) for n in ("small_loaded", "weights_loaded", "padding_zeroed", "c_tanh_done", "gate_tanh_done",
                         "exps_done", "silu_ready", "mod_products", "w0_raw_ready", "w0_hi_ready", "setup_steps"))

    with nc.Block() as block:
        @block.sync
        def _(sp):
            sp.dma_start(m["c_col"][:], a["c"]).then_inc(small, 16)
            sp.dma_start(m["gate_bc"][:], a["gate"].partition_broadcast(P)).then_inc(small, 16)
            sp.dma_start(m["u_bc"][:], a["time_first"].partition_broadcast(P)).then_inc(small, 16)
            sp.dma_start(lay0["ln_col"][:], a["ln_cols"]).then_inc(small, 16)
            sp.dma_start(keep["norm_cols"][:], a["norm_cols"]).then_inc(small, 16)
            sp.dma_start(keep["gnorm_col"][:], a["gnorm_col"]).then_inc(small, 16)
            for b in range(B):
                sp.dma_start(m["dec_raw"][S * b:S * b + S, :], a["time_decay"]).then_inc(small, 16)
            for l in range(2):
                sp.dma_start(m["wmod"][l][:], a["wmod"][l]).then_inc(loaded, 16)
            sp.dma_start(keep["ident"][:], a["ident"]).then_inc(loaded, 16)
            sp.dma_start(m["w_raw"][:, MIX:DIAG], a["w_mix"]).then_inc(loaded, 16)
            sp.dma_start(m["w_raw"][:, KV:OUT0], a["w_kv"]).then_inc(loaded, 16)
            sp.dma_start(m["w_raw"][:, ROUT:W0N], a["router"]).then_inc(loaded, 16)
            sp.wait_ge(zeroed, 2)
            for b in range(B):
                sp.dma_start(m["w_raw"][S * b:S * b + S, OUT0 + b * D:OUT0 + (b + 1) * D], a["w_out0"]).then_inc(loaded, 16)
            sp.dma_start(keep["x"][:], a["x"].rearrange("b (j p) d -> p b j d", p=P)).then_inc(x_loaded, 16)

        @block.gpsimd
        def _(pool):
            nc.gpsimd.memset(m["w_raw"][:, OUT0:ROUT], 0.0).then_inc(zeroed, 1)
            nc.gpsimd.memset(keep["neg_half"][:], -0.5).then_inc(zeroed, 1)
            nc.gpsimd.memset(keep["ln_eps"][:], LN_EPS)
            nc.gpsimd.memset(keep["rms_eps"][:], RMS_EPS * D)
            nc.gpsimd.memset(keep["head_eps"][:], RMS_EPS * DV)

        @block.scalar
        def _(act):
            act.wait_ge(small, 16 * 8)
            nc.scalar.activation(m["c_th"][:], m["c_col"][:], ACT.Tanh, scale=0.5).then_inc(c_tanh, 1)
            nc.scalar.activation(m["gate_th"][:], m["gate_bc"][:], ACT.Tanh, scale=0.5).then_inc(gate_tanh, 1)
            nc.scalar.activation(m["u_exp"][:], m["u_bc"][:], ACT.Exp).then_inc(exps, 1)
            nc.scalar.activation(lay0["decay"][:], m["dec_raw"][:], ACT.Exp).then_inc(exps, 1)
            act.wait_ge(raw_ready, 1)
            nc.scalar.copy(lay0["w0"][0][:], m["w_raw"][:]).then_inc(hi_ready, 1)

        @block.vector
        def _(v):
            step = Steps(v, Signal(steps, 0))
            v.wait_ge(c_tanh, 1)
            step(nc.vector.scalar_tensor_tensor(m["c_sum"][:], m["c_th"][:], 1.0, m["c_col"][:], ALU.add, ALU.mult))
            step(nc.vector.tensor_scalar(m["c_silu"][:], m["c_sum"][:], 0.5, None, ALU.mult))
            nc.vector.tensor_copy(m["c_wide"][:], m["c_silu"][:].rearrange("p l k b -> p (l k b)").unsqueeze(2)
                                  .to_broadcast([P, 2 * KC * B, P])).then_inc(silu, 1)
            v.wait_ge(gate_tanh, 1)
            step(nc.vector.tensor_scalar(m["mix_gain"][:], m["gate_th"][:], 0.5, 0.5, ALU.mult, ALU.add))
            step(nc.vector.tensor_scalar(m["keep_gain"][:], m["gate_th"][:], -0.5, 0.5, ALU.mult, ALU.add))
            v.wait_ge(exps, 1)
            nc.vector.tensor_scalar(lay0["neg_u"][:], m["u_exp"][:], -0.5, None, ALU.mult)
            nc.vector.tensor_scalar(keep["norm16"][:], keep["norm_cols"][:], float(D) ** 0.5, None, ALU.mult)
            nc.vector.tensor_scalar(keep["gnorm4"][:], keep["gnorm_col"][:], float(DV) ** 0.5 / 2, None, ALU.mult)
            v.wait_ge(loaded, 16 * 8)
            for k in range(KC):
                w = m["w_raw"][:, MIX + k * D:MIX + (k + 1) * D]
                step(nc.vector.tensor_tensor(w, w, m["mix_gain"][:], ALU.mult))
                step(nc.vector.tensor_tensor(m["w_raw"][:, DIAG + k * P:DIAG + (k + 1) * P], keep["ident"][:],
                                             m["keep_gain"][:, k * P:(k + 1) * P], ALU.mult))
            v.sem_inc(raw_ready, 1)
            v.wait_ge(hi_ready, 1)
            nc.vector.tensor_tensor(lay0["w0"][1][:], m["w_raw"][:], f32(lay0["w0"][0][:]), ALU.subtract)
            v.wait_ge(products, 1)
            for l, (col, gates) in enumerate(((keep["mod_col0"], keep["gate_row0"]), (keep["mod_col1"], keep["gate_row1"]))):
                step(nc.vector.tensor_copy(col[:].rearrange("p m b -> p (m b)"), bank[l][:, 0:MODS * KC * B]))
                for i in (1, 4):
                    w = col[:, i * KC:(i + 1) * KC, :]
                    step(nc.vector.tensor_scalar(w, w, 1.0, None, ALU.add))
                for b in range(B):
                    ps = bank[2 + 2 * l + b]
                    step(nc.vector.tensor_scalar(m["sign"][b][:], ps[:], 0.0, 2.0, ALU.is_ge, ALU.mult))
                    step(nc.vector.tensor_scalar(m["sign"][b][:], m["sign"][b][:], 1.0, None, ALU.subtract))
                    step(nc.vector.tensor_tensor(m["size"][b][:], ps[:], m["sign"][b][:], ALU.mult))
                    step(nc.vector.scalar_tensor_tensor(flat(gates[:, b]), m["size"][b][:], MIN_GATE, m["sign"][b][:],
                                                        ALU.max, ALU.mult))
            for b in range(B):
                nc.vector.tensor_copy(keep["shift_scale"][:, b, 0, :], bank[6 + b][:, 0:D])
                nc.vector.tensor_scalar(keep["shift_scale"][:, b, 1, :], bank[6 + b][:, D:2 * D], 1.0, None, ALU.add)

        @block.tensor
        def _(pe):
            pe.wait_ge(silu, 1)
            pe.wait_ge(loaded, 16 * 8)
            for l in range(2):
                for i in range(MODS * KC):
                    for k in range(KC):
                        nc.tensor.matmul(bank[l][:, i * B:(i + 1) * B], m["wmod"][l][:, k, i * P:(i + 1) * P],
                                         m["c_silu"][:, l, k, :], start=(k == 0), stop=(k == KC - 1))

            def on_every_row(ps, l, b, first, n):
                for k in range(KC):
                    last = nc.tensor.matmul(ps, m["c_wide"][:, (l * KC + k) * B + b, :], m["wmod"][l][:, k, first:first + n],
                                            start=(k == 0), stop=(k == KC - 1))
                return last
            for b in range(B):
                for l in range(2):
                    for i, which in enumerate((2, 5)):
                        on_every_row(bank[2 + 2 * l + b][:, i * D:(i + 1) * D], l, b, which * D, D)
                last = on_every_row(bank[6 + b][:], 1, b, 0, 2 * D)
            last.then_inc(products, 1)


def mix_and_key_value(nc, sem, a, bank, keep, lay0, m, x_loaded):
    NS, TURNS = 2 * B, J // 2
    PIECE = KC * E * FE // TURNS
    slots = [(s, s // 2, s % 2) for s in range(NS)]
    m.slots(["xn", "mn"], [D], NS)
    m.slots(["feat", "mfeat"], [KC, P], NS)
    m.pair_slots(["f", "mf"], [KC, P], NS)
    m.slots(["stats", "mstats"], [6], NS)
    m.add("mv", [NS, 2])
    m.add("ve", [NS])
    m.add("rstd", [NS])
    m.slots(["mmv"], [2], NS)
    m.slots(["mve", "mrstd"], [1], NS)
    m.slots(["kth", "karg", "kexp"], [S], NS)
    m.slots(["raw"], [PIECE], 3)
    experts = ((lay0["w_gate"], "w_gate"), (lay0["w_up"], "w_up"), (lay0["w_down"], "w_down"))

    def signal(name, per_turn=NS, ahead=False):
        return Signal(sem("mix_" + name), per_turn, ahead)
    var, xn, xT, feat, f_hi, f_lo = (signal(n) for n in ("var", "xn", "xT", "feat", "f_hi", "f_lo"))
    rstd = signal("rstd", 1)
    mixed, mvar, mrstd, mn, mT, mfeat, mf_hi, mf_lo = (signal(n) for n in (
        "mixed", "mvar", "mrstd", "mn", "mT", "mfeat", "mf_hi", "mf_lo"))
    kv, kth, karg, kexp = (signal(n) for n in ("kv", "ktanh", "karg", "kexp"))
    wkv = signal("wkv", ahead=True)
    raw_in = [sem(f"mix_raw_in{i}") for i in range(3)]
    raw_hi, raw_lo = signal("raw_hi", 3), signal("raw_lo", 3, True)
    v_steps, p_steps = signal("v_steps", 2 * NS), signal("p_steps", 1 + NS)

    def tile_of_x(t, b, h):
        return row(keep["x"], b, t + h * TURNS)

    def piece(w, t):
        return flat(flat(w[:]).rearrange("p (t n) -> p t n", t=TURNS)[:, bass.ds(t, 1), :])

    with nc.Block() as block:
        @block.sync
        def _(sp):
            for sig in (wkv, raw_lo):
                sp.sem_inc(sig.sem, sig.per_turn)
            sp.wait_ge(x_loaded, 16)
            with nc.sync.Fori(0, TURNS) as t:
                for i, (_, name) in enumerate(experts):
                    sp.wait_ge(raw_lo.sem, raw_lo.before(t, i))
                    sp.dma_start(m["raw"][i][:], a[name][bass.ds(t, 1)].rearrange("a p n -> p (a n)")).then_inc(raw_in[i], 16)

        @block.gpsimd
        def _(pool):
            def first_rsqrt(t, step):
                pool.wait_ge(var.sem, var.now(t, NS - 1))
                step(nc.gpsimd.tensor_tensor(m["ve"][:], m["mv"][:, :, 1:2].rearrange("p s a -> p (s a)"),
                                             keep["ln_eps"][:].to_broadcast([P, NS]), ALU.add))
                nc.gpsimd.tensor_tensor(m["rstd"][:], m["ve"][:], keep["neg_half"][:, 0:NS], ALU.pow).then_inc(rstd.sem, 1)

            def low(t, full, pair, got, gone):
                for s, _, _ in slots:
                    pool.wait_ge(got.sem, got.now(t, s))
                    nc.gpsimd.tensor_tensor(pair[s][1][:], full[s][:], f32(pair[s][0][:]), ALU.subtract).then_inc(gone.sem, 1)

            def body(t, step, ahead=True):
                if ahead:
                    first_rsqrt(t + 1, step)
                for s, _, _ in slots:
                    pool.wait_ge(mvar.sem, mvar.now(t, s))
                    step(nc.gpsimd.tensor_tensor(m["mve"][s][:], m["mmv"][s][:, 1:2], keep["ln_eps"][:], ALU.add))
                    nc.gpsimd.tensor_tensor(m["mrstd"][s][:], m["mve"][s][:], keep["neg_half"][:, 0:1], ALU.pow).then_inc(mrstd.sem, 1)
                low(t, m["mfeat"], m["mf"], mf_hi, mf_lo)
                if ahead:
                    low(t + 1, m["feat"], m["f"], f_hi, f_lo)
            step = Steps(pool, p_steps)
            first_rsqrt(0, step)
            step.end()
            low(0, m["feat"], m["f"], f_hi, f_lo)
            with nc.gpsimd.Fori(0, TURNS - 1) as t:
                step = Steps(pool, p_steps, t)
                body(t, step)
            step.end(TURNS - 1)
            step = Steps(pool, p_steps)
            body(TURNS - 1, step, False)
            step.end()

        @block.vector
        def _(v):
            def first_moments(t, step):
                moments(nc, v, step, keep["spare"], [(m["stats"][s][:], m["mv"][:, s, :], tile_of_x(t, b, h)) for s, b, h in slots], var)

            def first_norm(t):
                v.wait_ge(rstd.sem, rstd.now(t))
                for s, b, h in slots:
                    nc.vector.tensor_scalar(m["xn"][s][:], tile_of_x(t, b, h), m["mv"][:, s, 0:1], m["rstd"][:, s:s + 1],
                                            ALU.subtract, ALU.mult).then_inc(xn.sem, 1)

            def high(t, s, full, pair, got, gone):
                v.wait_ge(got.sem, got.now(t, s))
                nc.vector.tensor_copy(pair[s][0][:], full[s][:]).then_inc(gone.sem, 1)

            def weights_low(t, i):
                w, _ = experts[i]
                v.wait_ge(raw_hi.sem, raw_hi.now(t, i))
                nc.vector.tensor_tensor(piece(w[1], t), m["raw"][i][:], f32(piece(w[0], t)), ALU.subtract).then_inc(raw_lo.sem, 1)

            def body(t, step, ahead=True):
                if ahead:
                    first_moments(t + 1, step)
                moments(nc, v, step, keep["spare"], [(m["mstats"][s][:], m["mmv"][s][:], bank[4 + s][:, 0:D]) for s, b, h in slots],
                        mvar, lambda s: v.wait_ge(mixed.sem, mixed.now(t, s)))
                for s, _, _ in slots:
                    v.wait_ge(mrstd.sem, mrstd.now(t, s))
                    nc.vector.tensor_scalar(m["mn"][s][:], bank[4 + s][:, 0:D], m["mmv"][s][:, 0:1], m["mrstd"][s][:],
                                            ALU.subtract, ALU.mult).then_inc(mn.sem, 1)
                if ahead:
                    first_norm(t + 1)
                for s, _, _ in slots:
                    high(t, s, m["mfeat"], m["mf"], mfeat, mf_hi)
                for s, _, _ in slots:
                    if s < len(experts):
                        weights_low(t, s)
                    if ahead:
                        high(t + 1, s, m["feat"], m["f"], feat, f_hi)
                for s, _, _ in slots:
                    v.wait_ge(kth.sem, kth.now(t, s))
                    nc.vector.scalar_tensor_tensor(m["karg"][s][:], m["kth"][s][:], 1.0, lay0["neg_u"][:], ALU.add,
                                                   ALU.mult).then_inc(karg.sem, 1)
                for s, b, h in slots:
                    v.wait_ge(kexp.sem, kexp.now(t, s))
                    o = lay0["wkv_tok"][:, bass.ds(t + h * TURNS, 1), b, :].rearrange("p a s -> p (a s)")
                    nc.vector.tensor_tensor(o, bank[4 + s][:, S:2 * S], m["kexp"][s][:], ALU.mult).then_inc(wkv.sem, 1)
            v.wait_ge(x_loaded, 16)
            step = Steps(v, v_steps)
            first_moments(0, step)
            step.end()
            first_norm(0)
            for s, _, _ in slots:
                high(0, s, m["feat"], m["f"], feat, f_hi)
            with nc.vector.Fori(0, TURNS - 1) as t:
                step = Steps(v, v_steps, t)
                body(t, step)
            step.end(TURNS - 1)
            step = Steps(v, v_steps)
            body(TURNS - 1, step, False)
            step.end()

        @block.scalar
        def _(act):
            def affine(t, bk, full, got, gone, columns):
                for s, b, _ in slots:
                    act.wait_ge(got.sem, got.now(t, s))
                    for c in range(KC):
                        scale, shift = columns(b, c)
                        last = nc.scalar.activation(full[s][:, c, :], bank[bk + s][:, c * P:(c + 1) * P], ACT.Identity, bias=shift, scale=scale)
                    last.then_inc(gone.sem, 1)

            def modulated(t):
                affine(t, 0, m["feat"], xT, feat, lambda b, c: (keep["mod_col0"][:, KC + c, b:b + 1], keep["mod_col0"][:, c, b:b + 1]))

            def body(t, ahead=True):
                for i, (w, _) in enumerate(experts):
                    act.wait_ge(raw_in[i], t * 16 + 16)
                    nc.scalar.copy(piece(w[0], t), m["raw"][i][:]).then_inc(raw_hi.sem, 1)
                affine(t, 4, m["mfeat"], mT, mfeat, lambda b, c: (lay0["ln_col"][:, 0, c:c + 1], lay0["ln_col"][:, 1, c:c + 1]))
                if ahead:
                    modulated(t + 1)
                for s, _, _ in slots:
                    act.wait_ge(kv.sem, kv.now(t, s))
                    nc.scalar.activation(m["kth"][s][:], bank[4 + s][:, 0:S], ACT.Tanh, scale=0.5).then_inc(kth.sem, 1)
                for s, _, _ in slots:
                    act.wait_ge(karg.sem, karg.now(t, s))
                    nc.scalar.activation(m["kexp"][s][:], m["karg"][s][:], ACT.Exp).then_inc(kexp.sem, 1)
            modulated(0)
            with nc.scalar.Fori(0, TURNS - 1) as t:
                body(t)
            body(TURNS - 1, False)

        @block.tensor
        def _(pe):
            def w0(first, n):
                return [w[:, first:first + n] for w in lay0["w0"]]

            def chunk(pair, c):
                return [x[:, c, :] for x in pair]

            def transposes(t, bk, src, got, gone):
                for s, _, _ in slots:
                    pe.wait_ge(got.sem, got.now(t, s))
                    for c in range(KC):
                        last = nc.tensor.transpose(bank[bk + s][:, c * P:(c + 1) * P], src[s][:, c * P:(c + 1) * P], keep["ident"][:])
                    last.then_inc(gone.sem, 1)

            def body(t, ahead=True):
                pe.wait_ge(f_lo.sem, f_lo.now(t, NS - 1))
                for s, b, h in slots:
                    partner = 2 * b + 1 - h
                    pe.wait_ge(wkv.sem, wkv.before(t, s))
                    product3(nc, bank[4 + s][:, 0:D], [(chunk(m["f"][partner], c), w0(MIX + c * D, D)) for c in range(KC)],
                             last=False)
                    for c in range(KC):
                        last = product3(nc, bank[4 + s][:, c * P:(c + 1) * P], [(chunk(m["f"][s], c), w0(DIAG + c * P, P))],
                                        first=False)
                    last.then_inc(mixed.sem, 1)
                transposes(t, 4, m["mn"], mn, mT)
                if ahead:
                    transposes(t + 1, 0, m["xn"], xn, xT)
                for s, _, _ in slots:
                    pe.wait_ge(mf_lo.sem, mf_lo.now(t, s))
                    product3(nc, bank[4 + s][:, 0:2 * S], [(chunk(m["mf"][s], c), w0(KV + c * P, P)) for c in range(KC)]
                             ).then_inc(kv.sem, 1)
            transposes(0, 0, m["xn"], xn, xT)
            with nc.tensor.Fori(0, TURNS - 1) as t:
                body(t)
            body(TURNS - 1, False)


def recurrence(nc, sem, bank, keep, lay0):
    turned, scanned = sem("wkv_turned"), sem("scanned")
    with nc.Block() as block:
        @block.tensor
        def _(pe):
            for j in range(J):
                nc.tensor.transpose(bank[j // 4][:, (j % 4) * P:(j % 4 + 1) * P],
                                    flat(lay0["wkv_tok"][:, j]), keep["ident"][:]).then_inc(turned, 1)

        @block.vector
        def _(v):
            half = T // 2
            for k in range(2):
                v.wait_ge(turned, (k + 1) * J // 2)
                if k:
                    v.wait_ge(scanned, 1)
                nc.vector.tensor_tensor_scan(lay0["states"][:, k * half:(k + 1) * half], lay0["decay"][:].to_broadcast([P, half]),
                                             bank[k][:], lay0["states"][:, half - 1:half] if k else 0.0,
                                             ALU.mult, ALU.add).then_inc(scanned, 1)
            v.wait_ge(scanned, 2)


class Cut:

    def __init__(self, nc, sem, m, a, name, parts):
        self.nc, self.a, self.parts = nc, a, parts
        n = len(parts)
        self.loaded = [sem(f"{name}_loaded{i}") for i in range(n)]
        self.scaled = Signal(sem(f"{name}_scaled"), n, True)
        self.hi = Signal(sem(f"{name}_hi"), n)
        self.lo = Signal(sem(f"{name}_lo"), n, True)
        shapes = [[w[0].shape[1], w[0].shape[2] // J] for _, _, w, _ in parts]
        self.raw = [m.add(f"{name}_raw{i}", shape, parts[i][1]) for i, shape in enumerate(shapes)]
        self.full = [m.add(f"{name}_full{i}", shape) for i, shape in enumerate(shapes)]

    def piece(self, w, t):
        n = w.shape[2] // J
        return w[:, :, bass.ds(t * n, n)]

    def start(self, sp):
        for sig in (self.scaled, self.lo):
            sp.sem_inc(sig.sem, sig.per_turn)

    def load(self, sp, t):
        for i, (name, _, _, _) in enumerate(self.parts):
            sp.wait_ge(self.scaled.sem, self.scaled.before(t, i))
            sp.dma_start(self.raw[i][:], self.a[name][bass.ds(t, 1)].rearrange("a p k n -> p (a k) n")).then_inc(self.loaded[i], 16)

    def scale(self, v, t):
        for i, (_, _, _, scaling) in enumerate(self.parts):
            v.wait_ge(self.loaded[i], t * 16 + 16)
            v.wait_ge(self.lo.sem, self.lo.before(t, i))
            scaling(self.full[i], self.raw[i], t).then_inc(self.scaled.sem, 1)

    def take_hi(self, act, t):
        for i, (_, _, w, _) in enumerate(self.parts):
            act.wait_ge(self.scaled.sem, self.scaled.now(t, i))
            self.nc.scalar.copy(self.piece(w[0], t), self.full[i][:]).then_inc(self.hi.sem, 1)

    def take_lo(self, v, t):
        for i, (_, _, w, _) in enumerate(self.parts):
            v.wait_ge(self.hi.sem, self.hi.now(t, i))
            self.nc.vector.tensor_tensor(self.piece(w[1], t), self.full[i][:], f32(self.piece(w[0], t)),
                                         ALU.subtract).then_inc(self.lo.sem, 1)


def by_column(nc, columns):
    def scaling(out, raw, t):
        for k in range(out.shape[1]):
            last = nc.vector.tensor_scalar(out[:, k, :], raw[:, k, :], columns(k), None, ALU.mult)
        return last
    return scaling


def by_constant(nc, value):
    return lambda out, raw, t: nc.vector.tensor_scalar(out[:], raw[:], value, None, ALU.mult)


def from_codes(nc, scales):
    def scaling(out, raw, t):
        k, n = out.shape[1], out.shape[2]
        return nc.vector.scalar_tensor_tensor(out[:], raw[:], ZERO_POINT, scales[:, bass.ds(t * n, n)].unsqueeze(1)
                                              .to_broadcast([P, k, n]), ALU.subtract, ALU.mult)
    return scaling


def gated_mlp(nc, sem, a, bank, keep, m, kind, lay0, out, signals):
    experts, mlp, ffn = kind == "experts", kind == "mlp", kind == "ffn"
    NS = B
    G, W = (EG, GW) if experts else (IG, IW)
    mod_col, gate_row = (keep["mod_col0"], keep["gate_row0"]) if experts else (keep["mod_col1"], keep["gate_row1"])
    which_gate = 0 if mlp else 1
    if experts:
        w_down = lay0["w_down"]
    else:
        w_in, w_down = (keep["w_mlp"], keep["w_mlp_down"]) if mlp else (keep["w_ffn"], keep["w_ffn_down"])

    m.slots(["xn", "tmp"], [D], NS)
    m.slots(["feat"], [KC, P], NS)
    m.pair_slots(["f"], [KC, P], NS)
    m.slots(["th", "silu", "prod"], [W], NS)
    m.slots(["hid"], [3 * P], NS)
    m.pair_slots(["h"], [3, P], NS)
    m.slots(["stats"], [6], NS)
    m.slots(["mv"], [2], NS)
    m.slots(["ve", "rstd"], [1], NS)
    if experts:
        m.pair("st", [P])
        m.slots(["best"], [8], NS)
        m.slots(["first", "second", "share"], [E], NS)
        m.slots(["lead", "lead_th"], [1], NS)
        m.slots(["weight"], [2], NS)
        m.slots(["index"], [8], NS, U32)
        m.slots(["place"], [2], NS)
        m.add("iota", [E])
        cut = Cut(nc, sem, m, a, "cut1", [
            ("w_qkvg", F32, keep["w_qkvg"], by_column(nc, lambda k: keep["norm16"][:, 0, k:k + 1])),
            ("w_o", F32, keep["w_o"], by_column(nc, lambda k: keep["gnorm4"][:]))])
    elif mlp:
        m.add("s_in", [IG * 2 * IW])
        m.add("s_down", [D])
        m.add("s_down_half", [D])
        cut = Cut(nc, sem, m, a, "cut3", [("w_ffn", I32, keep["w_ffn"], from_codes(nc, m["s_in"])),
                                          ("w_ffn_down", I32, keep["w_ffn_down"], from_codes(nc, m["s_down_half"]))])
    else:
        cut = None

    def signal(name, per_turn=NS, ahead=False):
        if name in signals:
            return signals[name].again(per_turn)
        signals[name] = Signal(sem("gated_" + name), per_turn, ahead)
        return signals[name]
    moment, rstd, xn, xT, f_hi, f_lo = (signal(n) for n in ("moment", "rstd", "xn", "xT", "f_hi", "f_lo"))
    gu, th, hT, h_hi, h_lo = (signal(n, NS * G) for n in ("gate_up", "tanh", "hid_T", "h_hi", "h_lo"))
    prod = signal("prod", NS * G, True)
    down = signal("down")
    x_out = signal("x_out", NS, True)
    if experts:
        st_hi, st_lo = signal("st_hi", 1), signal("st_lo", 1)
        attn = signal("attn", NS, True)
        routed, lead, lead_tanh, share, attn_used = (signal(n) for n in ("routed", "lead", "lead_tanh", "share", "attn_used"))
        hid = signal("hid", NS * G)
    else:
        hid = prod
    v_steps = signal("v_steps", {"experts": 24, "mlp": 8, "ffn": 8}[kind])
    p_steps = signal("p_steps")
    if not ffn:
        ready = sem(f"{kind}_ready")
    if out is not None:
        stored = sem("stored")
    slots = range(NS)
    at = lambda gr, s: gr * NS + s

    def A(s): return bank[4 * s]
    def GATE(s): return bank[4 * s + 1]
    def UP(s): return bank[4 * s + 2]
    def TURN(s): return bank[4 * s + 3]

    with nc.Block() as block:
        @block.sync
        def _(sp):
            if experts:
                for sig in (x_out, prod, attn):
                    sp.sem_inc(sig.sem, sig.per_turn)
                sp.dma_start(m["iota"][:], a["iota"].partition_broadcast(P)).then_inc(ready, 16)
            if mlp:
                sp.dma_start(m["s_in"][:], a["s_ffn"].partition_broadcast(P)).then_inc(ready, 16)
                sp.dma_start(m["s_down"][:], a["s_ffn_down"].partition_broadcast(P)).then_inc(ready, 16)
            if cut:
                cut.start(sp)
                with nc.sync.Fori(0, J) as t:
                    cut.load(sp, t)
            if out is not None:
                with nc.sync.Fori(0, J) as t:
                    for s in slots:
                        sp.wait_ge(x_out.sem, x_out.now(t, s))
                        sp.dma_start(out[s].rearrange("(j p) d -> j p d", p=P)[bass.ds(t, 1)].rearrange("a p d -> p (a d)"),
                                     row(keep["x"], s, t)).then_inc(stored, 16)
                sp.wait_ge(stored, 16 * NS * J)

        @block.gpsimd
        def _(pool):
            def states_low(t):
                if experts:
                    pool.wait_ge(st_hi.sem, st_hi.now(t))
                    nc.gpsimd.tensor_tensor(m["st"][1][:], lay0["states"][:, bass.ds(t * P, P)], f32(m["st"][0][:]),
                                            ALU.subtract).then_inc(st_lo.sem, 1)

            def rsqrt(t, step):
                for s in slots:
                    pool.wait_ge(moment.sem, moment.now(t, s))
                    if mlp:
                        step(nc.gpsimd.tensor_tensor(m["ve"][s][:], m["mv"][s][:, 0:1], keep["rms_eps"][:], ALU.add))
                    else:
                        step(nc.gpsimd.tensor_tensor(m["ve"][s][:], m["mv"][s][:, 1:2], keep["ln_eps"][:], ALU.add))
                    nc.gpsimd.tensor_tensor(m["rstd"][s][:], m["ve"][s][:], keep["neg_half"][:, 0:1], ALU.pow).then_inc(rstd.sem, 1)

            def lows(t):
                if not mlp:
                    for s in slots:
                        pool.wait_ge(f_hi.sem, f_hi.now(t, s))
                        nc.gpsimd.tensor_tensor(m["f"][s][1][:], m["feat"][s][:], f32(m["f"][s][0][:]), ALU.subtract).then_inc(f_lo.sem, 1)

            def weigh(t, gr):
                for s in slots:
                    if gr == 0:
                        pool.wait_ge(share.sem, share.now(t, s))
                    pool.wait_ge(prod.sem, prod.now(t, at(gr, s)))
                    nc.gpsimd.tensor_tensor(
                        m["hid"][s][:].rearrange("p (e f) -> p e f", f=FE), m["prod"][s][:].rearrange("p (e f) -> p e f", f=FE),
                        m["share"][s][:, gr * (E // G):(gr + 1) * (E // G)].unsqueeze(2).to_broadcast([P, E // G, FE]),
                        ALU.mult).then_inc(hid.sem, 1)

            def body(t, step, ahead=True):
                if ahead:
                    states_low(t + 1)
                for gr in range(1, G):
                    if experts:
                        weigh(t, gr)
                    if gr == 1 and ahead:
                        rsqrt(t + 1, step)
                if ahead:
                    lows(t + 1)
                    if experts:
                        weigh(t + 1, 0)
            step = Steps(pool, p_steps)
            states_low(0)
            rsqrt(0, step)
            step.end()
            lows(0)
            if experts:
                weigh(0, 0)
            with nc.gpsimd.Fori(0, J - 1) as t:
                step = Steps(pool, p_steps, t)
                body(t, step)
            step.end(J - 1)
            body(J - 1, None, False)

        @block.vector
        def _(v):
            def add_attention(t, step):
                if experts:
                    for s in slots:
                        v.wait_ge(attn.sem, attn.now(t, s))
                        nc.vector.tensor_tensor(m["tmp"][s][:], A(s)[:, 0:D], gate_row[:, s, 0, :], ALU.mult).then_inc(attn_used.sem, 1)
                        v.wait_ge(attn_used.sem, attn_used.now(t, s))
                        step(nc.vector.tensor_tensor(row(keep["x"], s, t), row(keep["x"], s, t), m["tmp"][s][:], ALU.add))

            def moments_of_x(t, step):
                if not mlp:
                    moments(nc, v, step, keep["spare"], [(m["stats"][s][:], m["mv"][s][:], row(keep["x"], s, t)) for s in slots], moment)

            def norm(t):
                for s in slots:
                    v.wait_ge(rstd.sem, rstd.now(t, s))
                    if mlp:
                        nc.vector.tensor_scalar(m["xn"][s][:], row(keep["r2"], s, t), m["rstd"][s][:], None, ALU.mult).then_inc(xn.sem, 1)
                    else:
                        nc.vector.tensor_scalar(m["xn"][s][:], row(keep["x"], s, t), m["mv"][s][:, 0:1], m["rstd"][s][:],
                                                ALU.subtract, ALU.mult).then_inc(xn.sem, 1)

            def mlp_low(t, s):
                if mlp:
                    v.wait_ge(f_hi.sem, f_hi.now(t, s))
                    nc.vector.tensor_tensor(flat(m["f"][s][1][:]), GATE(s)[:, 0:D], f32(flat(m["f"][s][0][:])),
                                            ALU.subtract).then_inc(f_lo.sem, 1)

            def routing(t, s, step):
                v.wait_ge(routed.sem, routed.now(t, s))
                nc.vector.memset(keep["spare"][:], 0.0)
                step(nc.vector.max(m["best"][s][:], TURN(s)[:, 0:E]))
                nc.vector.tensor_tensor(m["lead"][s][:], m["best"][s][:, 0:1], m["best"][s][:, 1:2], ALU.subtract).then_inc(lead.sem, 1)
                found = nc.vector.max_index(m["index"][s][:], m["best"][s][:], TURN(s)[:, 0:E])
                step(found)
                step(nc.vector.tensor_copy(m["place"][s][:], m["index"][s][:, 0:2]))
                v.wait_ge(lead_tanh.sem, lead_tanh.now(t, s))
                nc.vector.tensor_scalar(m["weight"][s][:, 0:1], m["lead_th"][s][:], 0.25, 0.25, ALU.mult, ALU.add)
                step(nc.vector.tensor_scalar(m["weight"][s][:, 1:2], m["lead_th"][s][:], -0.25, 0.25, ALU.mult, ALU.add))
                nc.vector.tensor_scalar(m["first"][s][:], m["iota"][:], m["place"][s][:, 0:1], m["weight"][s][:, 0:1], ALU.is_equal, ALU.mult)
                step(nc.vector.tensor_scalar(m["second"][s][:], m["iota"][:], m["place"][s][:, 1:2], m["weight"][s][:, 1:2], ALU.is_equal, ALU.mult))
                nc.vector.tensor_tensor(m["share"][s][:], m["first"][s][:], m["second"][s][:], ALU.add).then_inc(share.sem, 1)

            def product(t, gr, s, step):
                v.wait_ge(th.sem, th.now(t, at(gr, s)))
                step(nc.vector.scalar_tensor_tensor(m["silu"][s][:], m["th"][s][:], 1.0, GATE(s)[:, 0:W], ALU.add, ALU.mult))
                o = m["prod"][s][:] if experts else m["hid"][s][:, 0:W]
                nc.vector.tensor_tensor(o, m["silu"][s][:], UP(s)[:, 0:W], ALU.mult).then_inc(prod.sem, 1)

            def add_to_x(t, s, step):
                v.wait_ge(down.sem, down.now(t, s))
                gate = gate_row[:, s, which_gate, :]
                if mlp:
                    step(nc.vector.tensor_tensor(m["tmp"][s][:], A(s)[:, 0:D], row(keep["r2"], s, t), ALU.add))
                    step(nc.vector.tensor_tensor(m["tmp"][s][:], m["tmp"][s][:], gate, ALU.mult))
                else:
                    step(nc.vector.tensor_tensor(m["tmp"][s][:], A(s)[:, 0:D], gate, ALU.mult))
                nc.vector.tensor_tensor(row(keep["x"], s, t), row(keep["x"], s, t), m["tmp"][s][:], ALU.add).then_inc(x_out.sem, 1)

            def body(t, step, ahead=True):
                for gr in range(G):
                    if gr == G - 1 and ahead:
                        for s in slots:
                            mlp_low(t + 1, s)
                    for s in slots:
                        v.wait_ge(h_hi.sem, h_hi.now(t, at(gr, s)))
                        nc.vector.tensor_tensor(flat(m["h"][s][1][:]), TURN(s)[:, 0:3 * P], f32(flat(m["h"][s][0][:])),
                                                ALU.subtract).then_inc(h_lo.sem, 1)
                        if ahead and gr == 0 and s == 0:
                            add_attention(t + 1, step)
                            if not experts:
                                moments_of_x(t + 1, step)
                        if ahead and gr == G - 2 and s == 1:
                            norm(t + 1)
                        if gr + 1 < G:
                            product(t, gr + 1, s, step)
                    if ahead and experts and gr == 0:
                        moments_of_x(t + 1, step)
                    if cut and gr == 0:
                        cut.scale(v, t)
                if cut:
                    cut.take_lo(v, t)
                for s in slots:
                    if ahead:
                        if experts:
                            routing(t + 1, s, step)
                        product(t + 1, 0, s, step)
                    add_to_x(t, s, step)
            if experts:
                v.wait_ge(ready, 16)
            if mlp:
                v.wait_ge(ready, 32)
                nc.vector.tensor_scalar(m["s_down_half"][:], m["s_down"][:], 0.5, None, ALU.mult)
            if not experts:
                for s in slots:
                    nc.vector.memset(m["hid"][s][:, W:3 * P], 0.0)
            step = Steps(v, v_steps)
            add_attention(0, step)
            moments_of_x(0, step)
            norm(0)
            for s in slots:
                mlp_low(0, s)
                if experts:
                    routing(0, s, step)
                product(0, 0, s, step)
            step.end()
            with nc.vector.Fori(0, J - 1) as t:
                step = Steps(v, v_steps, t)
                body(t, step)
            step.end(J - 1)
            step = Steps(v, v_steps)
            body(J - 1, step, False)
            step.end()

        @block.scalar
        def _(act):
            def front(t):
                if experts:
                    act.wait_ge(attn.sem, attn.before(t, NS - 1))
                    nc.scalar.copy(m["st"][0][:], lay0["states"][:, bass.ds(t * P, P)]).then_inc(st_hi.sem, 1)
                if mlp:
                    for s in slots:
                        nc.scalar.activation(m["feat"][s][:].rearrange("p k n -> p (k n)"), row(keep["r2"], s, t), ACT.Square,
                                             accum_out=m["mv"][s][:, 0:1]).then_inc(moment.sem, 1)

            def features(t, s):
                act.wait_ge(xT.sem, xT.now(t, s))
                if mlp:
                    nc.scalar.copy(flat(m["f"][s][0][:]), GATE(s)[:, 0:D]).then_inc(f_hi.sem, 1)
                    return
                for c in range(KC):
                    scale, shift = mod_col[:, 4 * KC + c, s:s + 1], mod_col[:, 3 * KC + c, s:s + 1]
                    ps = GATE(s)[:, c * P:(c + 1) * P]
                    nc.scalar.activation(m["feat"][s][:, c, :], ps, ACT.Identity, bias=shift, scale=scale)
                    last = nc.scalar.activation(m["f"][s][0][:, c, :], ps, ACT.Identity, bias=shift, scale=scale)
                last.then_inc(f_hi.sem, 1)

            def lead_of(t, s):
                act.wait_ge(lead.sem, lead.now(t, s))
                nc.scalar.activation(m["lead_th"][s][:], m["lead"][s][:], ACT.Tanh, scale=0.5).then_inc(lead_tanh.sem, 1)

            def tanh(t, gr, s):
                act.wait_ge(gu.sem, gu.now(t, at(gr, s)))
                nc.scalar.activation(m["th"][s][:], GATE(s)[:, 0:W], ACT.Tanh, scale=0.5).then_inc(th.sem, 1)

            def body(t, ahead=True):
                if ahead:
                    front(t + 1)
                for gr in range(G):
                    if gr == G - 1 and ahead:
                        for s in slots:
                            features(t + 1, s)
                    for s in slots:
                        act.wait_ge(hT.sem, hT.now(t, at(gr, s)))
                        nc.scalar.copy(flat(m["h"][s][0][:]), TURN(s)[:, 0:3 * P]).then_inc(h_hi.sem, 1)
                        if gr + 1 < G:
                            tanh(t, gr + 1, s)
                    if cut and gr == 1:
                        cut.take_hi(act, t)
                if ahead:
                    for s in slots:
                        if experts:
                            lead_of(t + 1, s)
                        tanh(t + 1, 0, s)
            front(0)
            for s in slots:
                features(0, s)
            for s in slots:
                if experts:
                    lead_of(0, s)
                tanh(0, 0, s)
            with nc.scalar.Fori(0, J - 1) as t:
                body(t)
            body(J - 1, False)

        @block.tensor
        def _(pe):
            def attention(t):
                pe.wait_ge(st_lo.sem, st_lo.now(t))
                for s in slots:
                    product3(nc, A(s)[:, 0:D], [([w[:] for w in m["st"]], [w[:, OUT0 + s * D:OUT0 + (s + 1) * D] for w in lay0["w0"]])]
                             ).then_inc(attn.sem, 1)

            def normed(t, s):
                pe.wait_ge(xn.sem, xn.now(t, s))
                pe.wait_ge(prod.sem, prod.before(t, at(G - 1, s)))
                for c in range(KC):
                    last = nc.tensor.transpose(GATE(s)[:, c * P:(c + 1) * P], m["xn"][s][:, c * P:(c + 1) * P], keep["ident"][:])
                last.then_inc(xT.sem, 1)

            def gate_up(t, gr, s):
                if gr == 0:
                    pe.wait_ge(f_lo.sem, f_lo.now(t, s))
                for which, ps in enumerate((GATE(s), UP(s))):
                    terms = []
                    for c in range(KC):
                        if experts:
                            w = [x[:, c, gr * W:(gr + 1) * W] for x in (lay0["w_up"] if which else lay0["w_gate"])]
                        else:
                            w = [x[:, c, (2 * gr + which) * W:(2 * gr + which + 1) * W] for x in w_in]
                        terms.append(([x[:, c, :] for x in m["f"][s]], w))
                    last = product3(nc, ps[:, 0:W], terms)
                last.then_inc(gu.sem, 1)

            def turn(t, gr, s):
                pe.wait_ge(hid.sem, hid.now(t, at(gr, s)))
                for c in range(3):
                    last = nc.tensor.transpose(TURN(s)[:, c * P:(c + 1) * P], m["hid"][s][:, c * P:(c + 1) * P], keep["ident"][:])
                last.then_inc(hT.sem, 1)

            def route(t, s):
                pe.wait_ge(f_lo.sem, f_lo.now(t, s))
                product3(nc, TURN(s)[:, 0:E], [([x[:, c, :] for x in m["f"][s]], [w[:, ROUT + c * E:ROUT + (c + 1) * E] for w in lay0["w0"]])
                                               for c in range(KC)]).then_inc(routed.sem, 1)

            def down_from(t, gr, s):
                last = product3(nc, A(s)[:, 0:D], [([x[:, c, :] for x in m["h"][s]], [w[:, gr * 3 + c, :] for w in w_down])
                                                   for c in range(3)], first=gr == 0, last=gr == G - 1)
                if gr == G - 1:
                    last.then_inc(down.sem, 1)

            def body(t, ahead=True):
                for gr in range(G):
                    for s in slots:
                        turn(t, gr, s)
                        if gr + 1 < G:
                            gate_up(t, gr + 1, s)
                        if gr == 0 and s == 0:
                            for n in slots:
                                pe.wait_ge(x_out.sem, x_out.before(t, n))
                            if experts and ahead:
                                attention(t + 1)
                    for s in slots:
                        if gr == G - 1 and ahead:
                            gate_up(t + 1, 0, s)
                        pe.wait_ge(h_lo.sem, h_lo.now(t, at(gr, s)))
                        if experts and gr == 0 and ahead:
                            pe.wait_ge(attn_used.sem, attn_used.now(t + 1, s))
                        if experts and gr == G - 1 and ahead:
                            route(t + 1, s)
                        down_from(t, gr, s)
                        if gr == G - 2 and ahead:
                            normed(t + 1, s)
            if experts:
                attention(0)
            for s in slots:
                normed(0, s)
            for s in slots:
                if experts:
                    route(0, s)
                gate_up(0, 0, s)
            with nc.tensor.Fori(0, J - 1) as t:
                body(t)
            body(J - 1, False)
    for sig in signals.values():
        if sig is not v_steps and sig is not p_steps:
            sig.pass_turns(J)


def retention(nc, sem, a, bank, keep, m):
    NS, HG = B, H // 4
    QK = 2 * H * DK
    m.slots(["xn", "hn"], [D], NS)
    m.pair_slots(["f"], [KC, P], NS)
    m.slots(["work"], [2, QK], NS)
    m.slots(["rot"], [QK], NS)
    m.slots(["on"], [HV], NS)
    m.slots(["sgate"], [HV], NS)
    m.pair_slots(["k"], [H * DK], NS)
    m.pair_slots(["v"], [HV], NS)
    m.pair_slots(["qkT"], [4, P], NS)
    m.pair_slots(["score"], [HG, 4, P], NS)
    m["oT"] = [[x[:, 0] for x in pair] for pair in m["score"]]
    m.slots(["state"], [HG, 4 * DV], NS)
    m.pair_slots(["S"], [HG, 4 * DV], NS)
    m.slots(["stats"], [6], NS)
    m.slots(["mv"], [2], NS)
    m.slots(["ve", "rstd", "sumsq", "hve", "hrstd"], [1], NS)
    m.slots(["hsum", "heps", "hrms"], [H], NS)
    m.add("rope", [2, QK])
    m.add("state_mask", [HG, 4 * DV])
    m.add("state_gain", [HG])
    m.add("pool_spare", [NS])
    cut = Cut(nc, sem, m, a, "cut2", [
        ("w_mlp", F32, keep["w_mlp"], by_column(nc, lambda k: keep["norm16"][:, 1, k:k + 1])),
        ("w_mlp_down", F32, keep["w_mlp_down"], by_constant(nc, 0.5))])

    def signal(name, per_turn=NS, ahead=False):
        return Signal(sem("ret_" + name), per_turn, ahead)
    (moment, rstd, h_ready, sumsq, hrstd, hn, hT, f_hi, f_lo, qk, val, gate) = (signal(n) for n in (
        "moment", "rstd", "h", "sumsq", "hrstd", "hn", "hT", "f_hi", "f_lo", "qk", "val", "gate"))
    terms, rot, k_lo, v_hi, v_lo, tanh, sgate, qkT, qkT_hi, qkT_lo = (signal(n) for n in (
        "rope_terms", "rot", "k_lo", "v_hi", "v_lo", "tanh", "sgate", "qkT", "qkT_hi", "qkT_lo"))
    scores, copied_a, copied_v, masked, s_hi, s_lo = (signal(n) for n in (
        "scores", "copied_act", "copied_dve", "masked", "score_hi", "score_lo"))
    o_done, st_done, st_sum, S_hi = (signal(n) for n in ("o", "state_product", "state_sum", "S_hi"))
    S_lo = signal("S_lo", NS, True)
    square, hsum, hrms, on, oT, oT_hi, oT_lo, proj = (signal(n) for n in (
        "square", "head_sum", "head_rms", "out_norm", "oT", "oT_hi", "oT_lo", "proj"))
    r2_out = signal("r2", NS, True)
    k_hi = signal("k_hi")
    rope_in, ready, zeroed = (sem(f"ret_{n}") for n in ("rope_in", "ready", "zeroed"))
    v_steps, p_steps = signal("v_steps", 5 * NS), signal("p_steps", 3 * NS)
    slots = range(NS)

    def bk(s, i): return bank[4 * s + i]

    with nc.Block() as block:
        @block.sync
        def _(sp):
            cut.start(sp)
            for sig in (S_lo, r2_out):
                sp.sem_inc(sig.sem, sig.per_turn)
            sp.dma_start(m["state_mask"][:], a["state_mask"]).then_inc(ready, 16)
            sp.dma_start(m["state_gain"][:], a["state_gain"]).then_inc(ready, 16)
            sp.dma_start(m["rope"][:], a["rope"][0]).then_inc(rope_in, 16)
            with nc.sync.Fori(0, J - 1) as t:
                cut.load(sp, t)
                sp.wait_ge(terms.sem, terms.now(t, NS - 1))
                sp.dma_start(m["rope"][:], a["rope"][bass.ds(t + 1, 1)].rearrange("a p c n -> p (a c) n")).then_inc(rope_in, 16)
            cut.load(sp, J - 1)

        @block.gpsimd
        def _(pool):
            for s in slots:
                for x in (*m["S"][s], m["state"][s]):
                    nc.gpsimd.memset(x[:] if x is m["state"][s] else f32(x[:]), 0.0).then_inc(zeroed, 1)

            def rsqrt(t, s, step, got, out, tmp, x, eps, gone):
                pool.wait_ge(got.sem, got.now(t, s))
                step(nc.gpsimd.tensor_tensor(tmp[s][:], x, eps[:], ALU.add))
                nc.gpsimd.tensor_tensor(out[s][:], tmp[s][:], keep["neg_half"][:, 0:out[s].shape[1]], ALU.pow).then_inc(gone.sem, 1)

            def layer_norm(t, step):
                for s in slots:
                    rsqrt(t, s, step, moment, m["rstd"], m["ve"], m["mv"][s][:, 1:2], keep["ln_eps"], rstd)

            def rms_norm(t, step):
                for s in slots:
                    rsqrt(t, s, step, sumsq, m["hrstd"], m["hve"], m["sumsq"][s][:], keep["rms_eps"], hrstd)

            def rotated(t, s):
                pool.wait_ge(terms.sem, terms.now(t, s))
                nc.gpsimd.tensor_tensor(m["rot"][s][:], m["work"][s][:, 0, :], m["work"][s][:, 1, :], ALU.add).then_inc(rot.sem, 1)

            def keys_low(t):
                for s in slots:
                    pool.wait_ge(k_hi.sem, k_hi.now(t, s))
                    nc.gpsimd.tensor_tensor(m["k"][s][1][:], m["rot"][s][:, H * DK:QK], f32(m["k"][s][0][:]), ALU.subtract).then_inc(k_lo.sem, 1)

            def body(t, step, ahead=True, norms=True):
                for s in slots:
                    pool.wait_ge(copied_a.sem, copied_a.now(t, s))
                    pool.wait_ge(copied_v.sem, copied_v.now(t, s))
                    nc.gpsimd.tensor_tensor(m["pool_spare"][:, s:s + 1], keep["ln_eps"][:], keep["ln_eps"][:], ALU.add)
                    w = m["work"][s][:].rearrange("p a n -> p (a n)").rearrange("p (h i) -> p h i", i=P)
                    nc.gpsimd.affine_select(out=w, in_=w, pattern=[[0, H], [1, P]], compare_op=ALU.is_ge, fill=0.0,
                                            base=0, channel_multiplier=-1).then_inc(masked.sem, 1)
                if norms:
                    layer_norm(t + 2, step)
                for s in slots:
                    rsqrt(t, s, step, hsum, m["hrms"], m["heps"], m["hsum"][s][:], keep["head_eps"], hrms)
                if ahead:
                    for s in slots:
                        rotated(t + 1, s)
                        pool.wait_ge(S_hi.sem, S_hi.now(t, s))
                        nc.gpsimd.tensor_tensor(flat(m["S"][s][1][:]), flat(m["state"][s][:]), f32(flat(m["S"][s][0][:])),
                                                ALU.subtract).then_inc(S_lo.sem, 1)
                    keys_low(t + 1)
                if norms:
                    rms_norm(t + 2, step)
            step = Steps(pool, p_steps)
            for t in range(2):
                layer_norm(t, step)
                rms_norm(t, step)
            step.end()
            for s in slots:
                rotated(0, s)
            keys_low(0)
            with nc.gpsimd.Fori(0, J - 2) as t:
                step = Steps(pool, p_steps, t)
                body(t, step)
            step.end(J - 2)
            step = Steps(pool, p_steps)
            body(J - 2, step, True, False)
            body(J - 1, step, False, False)
            step.end()

        @block.vector
        def _(v):
            def moments_of_x(t, step):
                moments(nc, v, step, keep["spare"], [(m["stats"][s][:], m["mv"][s][:], row(keep["x"], s, t)) for s in slots], moment)

            def modulated(t, step):
                for s in slots:
                    v.wait_ge(rstd.sem, rstd.now(t, s))
                    step(nc.vector.tensor_scalar(m["xn"][s][:], row(keep["x"], s, t), m["mv"][s][:, 0:1], m["rstd"][s][:],
                                                 ALU.subtract, ALU.mult))
                    step(nc.vector.tensor_tensor(m["xn"][s][:], m["xn"][s][:], keep["shift_scale"][:, s, 1, :], ALU.mult))
                    nc.vector.tensor_tensor(row(keep["r2"], s, t), m["xn"][s][:], keep["shift_scale"][:, s, 0, :], ALU.add).then_inc(h_ready.sem, 1)

            def normed(t):
                for s in slots:
                    v.wait_ge(hrstd.sem, hrstd.now(t, s))
                    nc.vector.tensor_scalar(m["hn"][s][:], row(keep["r2"], s, t), m["hrstd"][s][:], None, ALU.mult).then_inc(hn.sem, 1)

            def low(t, s, pair, ps, got, gone):
                v.wait_ge(got.sem, got.now(t, s))
                nc.vector.tensor_tensor(pair[1], ps, f32(pair[0]), ALU.subtract).then_inc(gone.sem, 1)

            def features_low(t, s):
                low(t, s, flats(m["f"][s]), bk(s, 2)[:, 0:D], f_hi, f_lo)

            def rope(t, s):
                if s == 0:
                    v.wait_ge(rope_in, t * 16 + 16)
                v.wait_ge(qk.sem, qk.now(t, s))
                nc.vector.tensor_tensor(m["work"][s][:, 0, :], bk(s, 1)[:], m["rope"][:, 0, :], ALU.mult)
                split = [x.rearrange("p (h c d) -> p h c d", c=2, d=DK // 2) for x in (m["work"][s][:, 1, :], bk(s, 1)[:], m["rope"][:, 1, :])]
                for c in range(2):
                    last = nc.vector.tensor_tensor(split[0][:, :, c, :], split[1][:, :, 1 - c, :], split[2][:, :, c, :], ALU.mult)
                last.then_inc(terms.sem, 1)

            def gates_and_values(t, s):
                v.wait_ge(tanh.sem, tanh.now(t, s))
                nc.vector.scalar_tensor_tensor(m["sgate"][s][:], m["sgate"][s][:], 1.0, bk(s, 3)[:], ALU.add, ALU.mult).then_inc(sgate.sem, 1)
                low(t, s, [x[:] for x in m["v"][s]], bk(s, 2)[:], v_hi, v_lo)

            def turned_low(t, s):
                low(t, s, flats(m["qkT"][s]), bk(s, 0)[:], qkT_hi, qkT_lo)

            def scores_low(t, s):
                v.wait_ge(s_hi.sem, s_hi.now(t, s))
                nc.vector.tensor_tensor(m["score"][s][1][:].rearrange("p g h i -> p (g h i)"), flat(m["work"][s][:]),
                                        f32(m["score"][s][0][:]).rearrange("p g h i -> p (g h i)"), ALU.subtract).then_inc(s_lo.sem, 1)

            def add_to_state(t, s, step):
                v.wait_ge(st_done.sem, st_done.now(t, s))
                v.wait_ge(s_lo.sem, s_lo.now(t, s))
                step(nc.vector.tensor_tensor(m["work"][s][:, 1, :], bk(s, 1)[:], flat(m["state_mask"][:]), ALU.mult))
                for g in range(HG):
                    last = nc.vector.scalar_tensor_tensor(m["state"][s][:, g, :], m["state"][s][:, g, :], m["state_gain"][:, g:g + 1],
                                                          m["work"][s][:, 1, g * 4 * DV:(g + 1) * 4 * DV], ALU.mult, ALU.add)
                last.then_inc(st_sum.sem, 1)

            def add_to_h(t, s):
                v.wait_ge(proj.sem, proj.now(t, s))
                nc.vector.tensor_tensor(row(keep["r2"], s, t), bk(s, 1)[:, 0:D], row(keep["r2"], s, t), ALU.add).then_inc(r2_out.sem, 1)

            def body(t, step, ahead=True, norms=True):
                cut.scale(v, t)
                for s in slots:
                    v.wait_ge(scores.sem, scores.now(t, s))
                    for h in (2, 3):
                        last = nc.vector.tensor_copy(score_view(m["work"][s])[:, :, h, :], by_head(bk(s, h)))
                    last.then_inc(copied_v.sem, 1)
                for s in slots:
                    if ahead:
                        features_low(t + 1, s)
                    scores_low(t, s)
                for s in slots:
                    add_to_state(t, s, step)
                if norms:
                    moments_of_x(t + 2, step)
                for s in slots:
                    v.wait_ge(square.sem, square.now(t, s))
                    nc.vector.tensor_reduce(m["hsum"][s][:], m["work"][s][:, 0, :].rearrange("p (h d) -> p h d", d=DV), AX.X,
                                            ALU.add).then_inc(hsum.sem, 1)
                    if norms and s == 0:
                        modulated(t + 2, step)
                for s in slots:
                    v.wait_ge(hrms.sem, hrms.now(t, s))
                    heads = lambda x: x.rearrange("p (h d) -> p h d", d=DV)
                    step(nc.vector.tensor_tensor(heads(m["on"][s][:]), heads(bk(s, 0)[:]),
                                                 m["hrms"][s][:].unsqueeze(2).to_broadcast([P, H, DV]), ALU.mult))
                    nc.vector.tensor_tensor(m["on"][s][:], m["on"][s][:], m["sgate"][s][:], ALU.mult).then_inc(on.sem, 1)
                    if ahead:
                        rope(t + 1, s)
                for s in slots:
                    low(t, s, flats(m["oT"][s]), bk(s, 1)[:], oT_hi, oT_lo)
                    if ahead:
                        gates_and_values(t + 1, s)
                    if s == 1:
                        add_to_h(t, 0)
                    if ahead:
                        turned_low(t + 1, s)
                add_to_h(t, 1)
                if norms:
                    normed(t + 2)
                cut.take_lo(v, t)
            v.wait_ge(ready, 32)
            v.wait_ge(zeroed, 3 * NS)
            step = Steps(v, v_steps)
            for t in range(2):
                moments_of_x(t, step)
                modulated(t, step)
                if t:
                    v.wait_ge(hT.sem, hT.now(0, NS - 1))
                normed(t)
                if t == 0:
                    for s in slots:
                        features_low(0, s)
            step.end()
            for s in slots:
                rope(0, s)
            for s in slots:
                gates_and_values(0, s)
            for s in slots:
                turned_low(0, s)
            with nc.vector.Fori(0, J - 2) as t:
                step = Steps(v, v_steps, t)
                body(t, step)
            step.end(J - 2)
            step = Steps(v, v_steps)
            body(J - 2, step, True, False)
            body(J - 1, step, False, False)
            step.end()

        @block.scalar
        def _(act):
            def front(t):
                for s in slots:
                    act.wait_ge(h_ready.sem, h_ready.now(t, s))
                    nc.scalar.activation(m["hn"][s][:], row(keep["r2"], s, t), ACT.Square, accum_out=m["sumsq"][s][:]).then_inc(sumsq.sem, 1)

            def high(t, s, hi, src, got, gone):
                act.wait_ge(got.sem, got.now(t, s))
                nc.scalar.copy(hi, src).then_inc(gone.sem, 1)

            def features_high(t, s):
                high(t, s, flat(m["f"][s][0][:]), bk(s, 2)[:, 0:D], hT, f_hi)

            def gates_and_values(t, s, used):
                act.wait_ge(gate.sem, gate.now(t, s))
                if used:
                    act.wait_ge(on.sem, on.now(t - 1, s))
                nc.scalar.activation(m["sgate"][s][:], bk(s, 3)[:], ACT.Tanh, scale=0.5).then_inc(tanh.sem, 1)
                high(t, s, m["v"][s][0][:], bk(s, 2)[:], val, v_hi)

            def keys_high(t, s):
                high(t, s, m["k"][s][0][:], m["rot"][s][:, H * DK:QK], rot, k_hi)

            def turned_high(t, s):
                high(t, s, flat(m["qkT"][s][0][:]), bk(s, 0)[:], qkT, qkT_hi)

            def scores_high(t, s):
                act.wait_ge(masked.sem, masked.now(t, s))
                nc.scalar.copy(m["score"][s][0][:].rearrange("p g h i -> p (g h i)"), flat(m["work"][s][:])).then_inc(s_hi.sem, 1)

            def body(t, ahead=True, norms=True):
                for s in slots:
                    act.wait_ge(scores.sem, scores.now(t, s))
                    for h in (0, 1):
                        last = nc.scalar.copy(score_view(m["work"][s])[:, :, h, :], by_head(bk(s, h)))
                    last.then_inc(copied_a.sem, 1)
                for s in slots:
                    if ahead:
                        features_high(t + 1, s)
                    scores_high(t, s)
                cut.take_hi(act, t)
                for s in slots:
                    act.wait_ge(o_done.sem, o_done.now(t, s))
                    nc.scalar.activation(m["work"][s][:, 0, :], bk(s, 0)[:], ACT.Square).then_inc(square.sem, 1)
                if ahead:
                    for s in slots:
                        act.wait_ge(st_sum.sem, st_sum.now(t, s))
                        nc.scalar.copy(flat(m["S"][s][0][:]), flat(m["state"][s][:])).then_inc(S_hi.sem, 1)
                if norms:
                    front(t + 2)
                for s in slots:
                    if ahead:
                        gates_and_values(t + 1, s, True)
                        keys_high(t + 1, s)
                    high(t, s, flat(m["oT"][s][0]), bk(s, 1)[:], oT, oT_hi)
                    if ahead:
                        turned_high(t + 1, s)
            front(0)
            for s in slots:
                features_high(0, s)
            front(1)
            for s in slots:
                gates_and_values(0, s, False)
                keys_high(0, s)
            for s in slots:
                turned_high(0, s)
            with nc.scalar.Fori(0, J - 2) as t:
                body(t)
            body(J - 2, True, False)
            body(J - 1, False, False)

        @block.tensor
        def _(pe):
            def transposes(t, s, ps, src, n, got, gone):
                pe.wait_ge(got.sem, got.now(t, s))
                for c in range(n):
                    last = nc.tensor.transpose(ps[:, c * P:(c + 1) * P], src[s][:, c * P:(c + 1) * P], keep["ident"][:])
                last.then_inc(gone.sem, 1)

            def features(t, s):
                transposes(t, s, bk(s, 2), m["hn"], KC, hn, hT)

            def inward(t, s, which):
                sig = (qk, val, gate)[which]
                product3(nc, bk(s, 1 + which)[:], [([x[:, c, :] for x in m["f"][s]], [w[:, c, which * 512:(which + 1) * 512] for w in keep["w_qkvg"]])
                                                   for c in range(KC)]).then_inc(sig.sem, 1)

            def gates(t, s):
                pe.wait_ge(f_lo.sem, f_lo.now(t, s))
                inward(t, s, 2)

            def turned(t, s):
                transposes(t, s, bk(s, 0), m["rot"], 4, rot, qkT)

            def scores_of(t, s):
                pe.wait_ge(qkT_lo.sem, qkT_lo.now(t, s))
                pe.wait_ge(v_lo.sem, v_lo.now(t, s))
                pe.wait_ge(sgate.sem, sgate.now(t, s))
                pe.wait_ge(r2_out.sem, r2_out.before(t, s))
                for g in range(HG):
                    for h in range(4):
                        part = slice(h * DK, (h + 1) * DK)
                        last = product3(nc, bk(s, h)[:, g * P:(g + 1) * P],
                                        [([x[part, 2 + g, :] for x in m["qkT"][s]], [x[part, g, :] for x in m["qkT"][s]])])
                last.then_inc(scores.sem, 1)

            def state_product(t, s):
                pe.wait_ge(k_lo.sem, k_lo.now(t, s))
                pe.wait_ge(copied_a.sem, copied_a.now(t, s))
                for g in range(HG):
                    cols = slice(g * 4 * DV, (g + 1) * 4 * DV)
                    last = product3(nc, bk(s, 1)[:, cols], [([x[:, g * P:(g + 1) * P] for x in m["k"][s]], [x[:, cols] for x in m["v"][s]])])
                last.then_inc(st_done.sem, 1)

            def outward(t, s):
                pe.wait_ge(S_lo.sem, S_lo.before(t, s))
                pe.wait_ge(s_lo.sem, s_lo.now(t, s))
                for g in range(HG):
                    product3(nc, bk(s, 0)[:, g * 4 * DV:(g + 1) * 4 * DV], [([x[:, g, :] for x in m["qkT"][s]], [x[:, g, :] for x in m["S"][s]])],
                             first=g == 0, last=False)
                for n in range(H):
                    g, h = n // 4, n % 4
                    last = product3(nc, bk(s, 0)[:, n * DV:(n + 1) * DV],
                                    [([x[:, g, h, :] for x in m["score"][s]], [x[:, n * DV:(n + 1) * DV] for x in m["v"][s]])],
                                    first=False, last=n == H - 1)
                last.then_inc(o_done.sem, 1)

            def projected(t, s):
                pe.wait_ge(oT_lo.sem, oT_lo.now(t, s))
                product3(nc, bk(s, 1)[:, 0:D], [([x[:, c, :] for x in m["oT"][s]], [w[:, c, :] for w in keep["w_o"]])
                                                for c in range(HV // P)]).then_inc(proj.sem, 1)

            def body(t, ahead=True):
                for s in slots:
                    scores_of(t, s)
                for s in slots:
                    state_product(t, s)
                    if ahead:
                        pe.wait_ge(copied_v.sem, copied_v.now(t, s))
                        features(t + 1, s)
                for s in slots:
                    if ahead:
                        gates(t + 1, s)
                    outward(t, s)
                for s in slots:
                    pe.wait_ge(st_sum.sem, st_sum.now(t, s))
                    if ahead:
                        inward(t + 1, s, 0)
                        inward(t + 1, s, 1)
                for s in slots:
                    if ahead:
                        pe.wait_ge(terms.sem, terms.now(t + 1, s))
                    transposes(t, s, bk(s, 1), m["on"], 4, on, oT)
                    if ahead and s == 0:
                        turned(t + 1, s)
                projected(t, 0)
                if ahead:
                    turned(t + 1, 1)
                projected(t, 1)
            pe.wait_ge(zeroed, 3 * NS)
            for s in slots:
                features(0, s)
            for s in slots:
                gates(0, s)
            for s in slots:
                inward(0, s, 0)
                inward(0, s, 1)
            for s in slots:
                turned(0, s)
            with nc.tensor.Fori(0, J - 1) as t:
                body(t)
            body(J - 1, False)


def flats(pair):
    return [flat(x if isinstance(x, bass.AP) else x[:]) for x in pair]


def score_view(work):
    return work[:].rearrange("p a n -> p (a n)").rearrange("p (g h i) -> p g h i", g=H // 4, h=4)


def by_head(bank):
    return bank[:, 0:2 * P].rearrange("p (g i) -> p g i", i=P)




def kernel(**inputs):
    import concourse.bacc as _bacc
    from concourse.bass_utils import run_bass_kernel_spmd as _run

    def col(v):
        return np.asarray(v).reshape(KC, P).T

    def rows(w):
        w = np.asarray(w)
        return w.reshape(-1, P, w.shape[-1]).transpose(1, 0, 2)

    def pieces(w, n):
        return w.reshape(P, n, -1).transpose(1, 0, 2)

    def column_pieces(w, n):
        return w.reshape(P, w.shape[1], n, -1).transpose(2, 0, 1, 3)

    def by_group(gate, up):
        return np.concatenate([w[:, g * IW:(g + 1) * IW] for g in range(IG) for w in (gate, up)], axis=1)

    def down_rows(w):
        o = np.zeros((IG, 3 * P, w.shape[-1]), w.dtype)
        o[:, :IW] = w.reshape(IG, IW, -1)
        return rows(o.reshape(IG * 3 * P, -1))

    g = {k: np.asarray(v) for k, v in inputs.items()}
    a = {}
    a["x"] = g["L0_attn_x"]
    a["c"] = np.stack([rows(g[f"L{l}_c"].T) for l in range(2)], axis=1)
    a["wmod"] = np.stack([rows(g[f"L{l}_wmod"]) for l in range(2)])
    a["gate"], a["time_first"] = g["L0_attn_gate"], g["L0_attn_time_first"]
    a["time_decay"] = g["L0_attn_time_decay"].reshape(S, 1)
    a["ln_cols"] = np.stack([col(g["L0_attn_ln_gamma"]), col(g["L0_attn_ln_beta"])], axis=1)
    a["ident"] = np.eye(P, dtype=np.float32)
    a["w_mix"] = rows(g["L0_attn_W_shift"].T).reshape(P, -1)
    a["w_kv"] = rows(np.concatenate([g["L0_attn_W_key"], g["L0_attn_W_value"]], axis=0).T).reshape(P, -1)
    a["w_out0"] = g["L0_attn_W_output"].T
    a["router"] = rows(g["L0_ffn_router_w"]).reshape(P, -1)
    for name, key in (("w_gate", "gate_w"), ("w_up", "up_w")):
        a[name] = pieces(rows(g["L0_ffn_" + key].transpose(1, 0, 2).reshape(D, E * FE)), J // 2)
    a["w_down"] = pieces(rows(g["L0_ffn_down_w"].reshape(E * FE, D)), J // 2)

    qkvg = np.concatenate([g["L1_attn_" + n] for n in ("q_w", "k_w", "v_w", "g_w")], axis=1)
    a["w_qkvg"] = column_pieces(rows(qkvg), J)
    a["w_o"] = column_pieces(rows(g["L1_attn_o_w"]), J)
    a["norm_cols"] = np.stack([col(g["L1_attn_attn_norm_w"]), col(g["L1_attn_mlp_norm_w"])], axis=1)
    a["gnorm_col"] = np.tile(g["L1_attn_gnorm_w"], 2).reshape(P, 1)
    mlp = g["L1_attn_gate_w"]
    a["w_mlp"] = column_pieces(rows(by_group(mlp[:, :INTER], mlp[:, INTER:])), J)
    a["w_mlp_down"] = column_pieces(down_rows(g["L1_attn_down_w"]), J)
    a["w_ffn"] = column_pieces(rows(by_group(g["L1_ffn_wq_gate"].T, g["L1_ffn_wq_up"].T)), J)
    a["w_ffn_down"] = column_pieces(down_rows(g["L1_ffn_wq_down"].T), J)
    a["s_ffn"] = by_group(g["L1_ffn_s_gate"][None], g["L1_ffn_s_up"][None])[0]
    a["s_ffn_down"] = g["L1_ffn_s_down"]
    a.update(shape_tables())

    nc = _bacc.Bacc("TRN2", target_bir_lowering=False, num_devices=1)
    a = {k: np.ascontiguousarray(v) for k, v in a.items()}
    aps = {k: nc.dram_tensor("in_" + k, v.shape, mybir.dt.from_np(v.dtype), kind="ExternalInput").ap() for k, v in a.items()}
    out = nc.dram_tensor("out_0", (B, T, D), F32, kind="ExternalOutput").ap()
    build(nc, aps, out)
    r = _run(nc, [{"in_" + k: v for k, v in a.items()}], core_ids=[0])
    return r.results[0]["out_0"]


def shape_tables():
    gamma = 1.0 - np.exp2(-5.0 - np.arange(H, dtype=np.float64))
    i = np.arange(P, dtype=np.float64)[:, None]
    q_gain = gamma ** (i + 1) * DK ** -0.5
    k_gain = gamma ** -(i + 1)
    inv_freq = (np.float32(1.0) / np.float32(10000.0) ** (np.arange(0, DK, 2, dtype=np.float32) / np.float32(DK))).astype(np.float32)
    angle = np.arange(T, dtype=np.float32)[:, None] * inv_freq
    cos = np.cos(angle.astype(np.float64)).reshape(J, P, 1, DK // 2)
    sin = np.sin(angle.astype(np.float64)).reshape(J, P, 1, DK // 2)
    full_cos = np.concatenate([cos, cos], axis=-1)
    full_sin = np.concatenate([-sin, sin], axis=-1)
    table = np.stack([np.concatenate([f * q_gain[None, :, :, None], f * k_gain[None, :, :, None]], axis=2)
                      for f in (full_cos, full_sin)], axis=2)
    tile_decay = gamma ** P
    state_mask = np.zeros((4, DK, 2, 4, DV))
    state_gain = np.zeros((4, DK, 2))
    for grp in range(2):
        for h in range(4):
            state_mask[h, :, grp, h, :] = tile_decay[grp * 4 + h]
            state_gain[h, :, grp] = tile_decay[grp * 4 + h]
    return {"iota": np.arange(E, dtype=np.float32), "rope": table.reshape(J, P, 2, 2 * H * DK).astype(np.float32),
            "state_mask": state_mask.reshape(P, 2, 4 * DV).astype(np.float32),
            "state_gain": state_gain.reshape(P, 2).astype(np.float32)}
```

```python
from contextlib import ExitStack

import numpy as np
import concourse.bass as bass
from concourse import mybir

F32 = mybir.dt.float32
F32R = mybir.dt.float32r
I32 = mybir.dt.int32
U32 = mybir.dt.uint32
ALU = mybir.AluOpType
ACT = mybir.ActivationFunctionType
AX = mybir.AxisListType

P = 128
B, T, D = 2, 1024, 256
J = T // P
KC = D // P
S = 64
E, FE = 16, 96
EG = 4
GW = E * FE // EG
H, DK, DV = 8, 32, 64
HV = H * DV
INTER = 704
IG = 2
IW = INTER // IG
MODS = 6
LN_EPS = 1e-5
RMS_EPS = 1e-6
MIN_GATE = 0.25
ZERO_POINT = 128.0


class Signal:

    def __init__(self, sem, per_turn, ahead=False):
        self.sem, self.per_turn, self.ahead = sem, per_turn, ahead
        self.base = per_turn if ahead else 0

    def now(self, turn, k=0):
        return turn * self.per_turn + (self.base + k + 1)

    def before(self, turn, k=0):
        assert self.ahead
        return turn * self.per_turn + (self.base + k + 1 - self.per_turn)

    def pass_turns(self, turns):
        self.base += turns * self.per_turn

    def again(self, per_turn):
        self.per_turn = per_turn
        return self


class Steps:

    def __init__(self, eng, counts, turn=None):
        self.eng, self.counts, self.turn, self.k = eng, counts, turn, 0

    def __call__(self, instruction):
        instruction.then_inc(self.counts.sem, 1)
        self.eng.wait_ge(self.counts.sem, self.counts.now(0 if self.turn is None else self.turn, self.k))
        self.k += 1

    def end(self, turns=1):
        assert self.turn is None or self.k == self.counts.per_turn, (self.k, self.counts.per_turn)
        self.counts.base += turns * self.k


def f32(ap):
    return ap.bitcast(F32)


def product3(nc, out, terms, first=True, last=True):
    n = len(terms)
    for i, (lhs, rhs) in enumerate(terms):
        for k, (x, y) in enumerate(((0, 0), (0, 1), (1, 0))):
            done = nc.tensor.matmul(out, lhs[x], rhs[y], start=(first and i == 0 and k == 0),
                                    stop=(last and i == n - 1 and k == 2), skip_group_check=True)
    return done


class Memory(dict):

    def __init__(self, nc, stack, phase=""):
        self.nc, self.stack, self.phase = nc, stack, phase

    def add(self, name, shape, dt=F32):
        tile = self.stack.enter_context(self.nc.sbuf_tensor(self.phase + name, [P] + list(shape), dt))
        self[name] = tile
        return tile

    def pair(self, name, shape):
        both = [self.stack.enter_context(self.nc.sbuf_tensor(f"{self.phase}{name}_{x}", [P] + list(shape), F32R)) for x in ("hi", "lo")]
        self[name] = both
        return both

    def slots(self, names, shape, n, dt=F32):
        for name in names:
            self[name] = [self.stack.enter_context(self.nc.sbuf_tensor(f"{self.phase}{name}{s}", [P] + list(shape), dt))
                                   for s in range(n)]

    def pair_slots(self, names, shape, n):
        for name in names:
            self[name] = [[self.stack.enter_context(self.nc.sbuf_tensor(f"{self.phase}{name}{s}_{x}", [P] + list(shape), F32R))
                                    for x in ("hi", "lo")] for s in range(n)]


def flat(ap):
    return ap.rearrange("p a b -> p (a b)")


def row(tile, *index):
    *first, last = index
    ap = tile
    for i in first:
        ap = ap[:, i]
    return ap[:, bass.ds(last, 1), :].rearrange("p a d -> p (a d)")


MIX, DIAG = 0, KC * D
KV = DIAG + KC * P
OUT0 = KV + KC * P
ROUT = OUT0 + B * D
W0N = ROUT + KC * E


def build(nc, a, out):
    with ExitStack() as ctx:
        bank = [ctx.enter_context(nc.psum_tensor(f"bank{i}", [P, 512], F32)) for i in range(8)]

        def sem(name):
            return ctx.enter_context(nc.semaphore(name))

        keep = Memory(nc, ctx)
        keep.add("x", [B, J, D])
        keep.add("ident", [P])
        keep.add("neg_half", [H])
        keep.add("ln_eps", [1])
        keep.add("rms_eps", [1])
        keep.add("head_eps", [H])
        keep.add("norm_cols", [2, KC])
        keep.add("norm16", [2, KC])
        keep.add("gnorm_col", [1])
        keep.add("gnorm4", [1])
        keep.add("spare", [2 * B + 1])
        for l in range(2):
            keep.add(f"mod_col{l}", [MODS * KC, B])
            keep.add(f"gate_row{l}", [B, 2, D])
        keep.add("shift_scale", [B, 2, D])
        keep.pair("w_qkvg", [KC, 2 * D + 2 * HV])
        keep.pair("w_o", [HV // P, D])
        x_loaded = sem("x_loaded")
        with ExitStack() as early:
            lay0 = Memory(nc, early)
            lay0.pair("w0", [ROUT])
            lay0.add("wkv_tok", [J, B, S])
            lay0.add("states", [T])
            lay0.add("decay", [1])
            lay0.add("ln_col", [2, KC])
            lay0.add("neg_u", [S])
            lay0.pair("w_gate", [KC, E + E * FE])
            lay0.pair("w_up", [KC, E * FE])
            lay0.pair("w_down", [E * FE // P, D])
            with ExitStack() as first:
                norm = FirstNorm(nc, sem, keep, Memory(nc, first, "first_"))
                with ExitStack() as tmp:
                    setup(nc, sem, a, bank, keep, lay0, Memory(nc, tmp, "setup_"), x_loaded, norm)
                with ExitStack() as tmp:
                    mix_and_key_value(nc, sem, a, bank, keep, lay0, Memory(nc, tmp, "mix_"), norm)
            signals = {}
            with ExitStack() as tmp:
                gated_mlp(nc, sem, a, bank, keep, Memory(nc, tmp, "experts_"), ("experts",), lay0, None, signals)
        keep.pair("w_mlp", [KC, IG * 2 * IW])
        keep.pair("w_mlp_down", [IG * 3, D])
        keep.add("r2", [B, J, D])
        with ExitStack() as tmp:
            retention(nc, sem, a, bank, keep, Memory(nc, tmp, "ret_"))
        keep.pair("w_ffn", [KC, IG * 2 * IW])
        keep.pair("w_ffn_down", [IG * 3, D])
        with ExitStack() as tmp:
            gated_mlp(nc, sem, a, bank, keep, Memory(nc, tmp, "mlp_"), ("mlp", "ffn"), None, out, signals)


def moments(nc, v, step, spare, tiles, gone):
    for s, (stats, mv, x) in enumerate(tiles):
        nc.vector.memset(spare[:], 0.0)
        statistics = nc.vector.bn_stats(stats, x)
        if s:
            nc.vector.bn_aggr(tiles[s - 1][1], tiles[s - 1][0]).then_inc(gone.sem, 1)
        step(statistics)
    nc.vector.memset(spare[:], 0.0)
    nc.vector.bn_aggr(tiles[-1][1], tiles[-1][0]).then_inc(gone.sem, 1)


class FirstNorm:
    SLOTS = [(s, s // 2, s % 2) for s in range(2 * B)]

    def __init__(self, nc, sem, keep, m):
        n = len(self.SLOTS)
        self.nc, self.keep, self.m = nc, keep, m
        m.slots(["xn"], [D], n)
        m.slots(["stats"], [6], n)
        m.add("mv", [n, 2])
        m.add("ve", [n])
        m.add("rstd", [n])
        self.var, self.rstd, self.xn = Signal(sem("first_var"), n), Signal(sem("first_rstd"), 1), Signal(sem("first_xn"), n)

    def tile(self, t, b, h):
        return row(self.keep["x"], b, t + h * (J // 2))

    def moments(self, v, step, t):
        m, n = self.m, len(self.SLOTS)
        moments(self.nc, v, step, self.keep["spare"][:, n:n + 1], [(m["stats"][s][:], m["mv"][:, s, :], self.tile(t, b, h))
                                                       for s, b, h in self.SLOTS], self.var)

    def rsqrt(self, pool, step, t):
        m, n = self.m, len(self.SLOTS)
        pool.wait_ge(self.var.sem, self.var.now(t, n - 1))
        step(self.nc.gpsimd.tensor_tensor(m["ve"][:], m["mv"][:, :, 1:2].rearrange("p s a -> p (s a)"),
                                          self.keep["ln_eps"][:].to_broadcast([P, n]), ALU.add))
        self.nc.gpsimd.tensor_tensor(m["rstd"][:], m["ve"][:], self.keep["neg_half"][:, 0:n], ALU.pow).then_inc(self.rstd.sem, 1)

    def norm(self, v, t):
        m = self.m
        v.wait_ge(self.rstd.sem, self.rstd.now(t))
        for s, b, h in self.SLOTS:
            self.nc.vector.tensor_scalar(m["xn"][s][:], self.tile(t, b, h), m["mv"][:, s, 0:1], m["rstd"][:, s:s + 1],
                                         ALU.subtract, ALU.mult).then_inc(self.xn.sem, 1)


def setup(nc, sem, a, bank, keep, lay0, m, x_loaded, first):
    m.add("w_raw", [W0N])
    m.slots(["wmod"], [KC, MODS * D], 2)
    for name in ("c_col", "c_th", "c_sum", "c_silu"):
        m.add(name, [2, KC, B])
    m.slots(["rows"], [MODS, D], 2)
    m.add("pick", [B, P])
    for name in ("gate_bc", "gate_th", "mix_gain", "keep_gain"):
        m.add(name, [D])
    m.add("u_bc", [S])
    m.add("u_exp", [S])
    m.add("dec_raw", [1])
    m.add("sign", [2, D])
    N = 2 * D
    c_in, small, loaded, zeroed, c_tanh, gate_tanh, exps, silu, raw_ready, hi_ready, steps, pool_steps = (
        sem(n) for n in ("c_loaded", "small_loaded", "weights_loaded", "padding_zeroed", "c_tanh_done", "gate_tanh_done",
                         "exps_done", "silu_ready", "w0_raw_ready", "w0_hi_ready", "setup_steps", "setup_pool_steps"))
    wmod_in = [sem(f"wmod_loaded{l}") for l in range(2)]
    ident_in, rows_done, rows_copied, rows_ready, cols_done, wide_done = (sem(n) for n in (
        "ident_loaded", "rows_product", "rows_copied", "rows_ready", "columns_turned", "rows_repeated"))
    router = m["w_raw"][:, ROUT:W0N].rearrange("p (k e) -> p k e", k=KC)
    wide = [(flat(keep[f"gate_row{l}"][:, b]), l, b, 3 * l + b) for l in range(2) for b in range(B)]
    wide += [(flat(keep["shift_scale"][:, b]), 1, b, 2 + 3 * b) for b in range(B)]

    with nc.Block() as block:
        @block.sync
        def _(sp):
            sp.dma_start(m["c_col"][:], a["c"]).then_inc(c_in, 16)
            sp.dma_start(keep["ident"][:], a["ident"]).then_inc(ident_in, 16)
            for l in range(2):
                sp.dma_start(m["wmod"][l][:], a["wmod"][l]).then_inc(wmod_in[l], 16)
            sp.dma_start(keep["x"][:], a["x"].rearrange("b (j p) d -> p b j d", p=P)).then_inc(x_loaded, 16)

        @block.gpsimd
        def _(pool):
            nc.gpsimd.memset(m["w_raw"][:, OUT0:ROUT], 0.0).then_inc(zeroed, 1)
            nc.gpsimd.memset(keep["neg_half"][:], -0.5).then_inc(zeroed, 1)
            nc.gpsimd.memset(keep["ln_eps"][:], LN_EPS).then_inc(zeroed, 1)
            nc.gpsimd.memset(keep["rms_eps"][:], RMS_EPS * D)
            nc.gpsimd.memset(keep["head_eps"][:], RMS_EPS * DV)
            pool.wait_ge(zeroed, 3)
            first.rsqrt(pool, Steps(pool, Signal(pool_steps, 0)), 0)

        @block.scalar
        def _(act):
            act.wait_ge(c_in, 16)
            nc.scalar.activation(m["c_th"][:], m["c_col"][:], ACT.Tanh, scale=0.5).then_inc(c_tanh, 1)
            act.dma_start(m["gate_bc"][:], a["gate"].partition_broadcast(P)).then_inc(small, 16)
            act.dma_start(m["u_bc"][:], a["time_first"].partition_broadcast(P)).then_inc(small, 16)
            act.dma_start(lay0["ln_col"][:], a["ln_cols"]).then_inc(small, 16)
            act.dma_start(keep["norm_cols"][:], a["norm_cols"]).then_inc(small, 16)
            act.dma_start(keep["gnorm_col"][:], a["gnorm_col"]).then_inc(small, 16)
            for b in range(B):
                act.dma_start(m["dec_raw"][S * b:S * b + S, :], a["time_decay"]).then_inc(small, 16)
            act.dma_start(m["w_raw"][:, MIX:DIAG], a["w_mix"]).then_inc(loaded, 16)
            act.dma_start(m["w_raw"][:, KV:OUT0], a["w_kv"]).then_inc(loaded, 16)
            act.dma_start(m["w_raw"][:, ROUT:W0N], a["router"]).then_inc(loaded, 16)
            act.wait_ge(zeroed, 2)
            for b in range(B):
                act.dma_start(m["w_raw"][S * b:S * b + S, OUT0 + b * D:OUT0 + (b + 1) * D], a["w_out0"]).then_inc(loaded, 16)
            def copy_rows(l):
                for n in range(3):
                    act.wait_ge(rows_done, 3 * l + n + 1)
                    nc.scalar.copy(flat(m["rows"][l][0:B, 2 * n:2 * n + 2, :]), bank[3 * l + n][0:B, :]).then_inc(rows_copied, 1)
            copy_rows(0)
            act.wait_ge(small, 16 * 7)
            nc.scalar.activation(m["gate_th"][:], m["gate_bc"][:], ACT.Tanh, scale=0.5).then_inc(gate_tanh, 1)
            nc.scalar.activation(m["u_exp"][:], m["u_bc"][:], ACT.Exp).then_inc(exps, 1)
            nc.scalar.activation(lay0["decay"][:], m["dec_raw"][:], ACT.Exp).then_inc(exps, 1)
            copy_rows(1)
            act.wait_ge(raw_ready, 1)
            nc.scalar.copy(lay0["w0"][0][:], m["w_raw"][:, 0:ROUT]).then_inc(hi_ready, 1)
            nc.scalar.copy(lay0["w_gate"][0][:, :, 0:E], router).then_inc(hi_ready, 1)
            for n, (target, _, _, i) in enumerate(wide):
                if n % 2 == 0:
                    act.wait_ge(wide_done, n + 1)
                    nc.scalar.copy(target, bank[i][:])

        @block.vector
        def _(v):
            step = Steps(v, Signal(steps, 0))
            v.wait_ge(c_tanh, 1)
            step(nc.vector.scalar_tensor_tensor(m["c_sum"][:], m["c_th"][:], 1.0, m["c_col"][:], ALU.add, ALU.mult))
            nc.vector.tensor_scalar(m["c_silu"][:], m["c_sum"][:], 0.5, None, ALU.mult).then_inc(silu, 1)
            v.wait_ge(ident_in, 16)
            for b in range(B):
                step(nc.vector.tensor_copy(m["pick"][0:B, b, :], keep["ident"][0:B, b:b + 1].to_broadcast([B, P])))
            def finish_rows(l):
                v.wait_ge(rows_copied, 3 * l + 3)
                rows = m["rows"][l][0:B].rearrange("p (h i) d -> p h i d", i=3)
                scale, gate = rows[:, :, 1, :], rows[:, :, 2, :]
                sign = m["sign"][0:B]
                step(nc.vector.tensor_scalar(scale, scale, 1.0, None, ALU.add))
                step(nc.vector.tensor_scalar(sign, gate, 0.0, 2.0, ALU.is_ge, ALU.mult))
                step(nc.vector.tensor_scalar(sign, sign, 1.0, None, ALU.subtract))
                step(nc.vector.tensor_tensor(gate, gate, sign, ALU.mult))
                nc.vector.scalar_tensor_tensor(gate, gate, MIN_GATE, sign, ALU.max, ALU.mult).then_inc(rows_ready, 1)
            finish_rows(0)
            v.wait_ge(gate_tanh, 1)
            step(nc.vector.tensor_scalar(m["mix_gain"][:], m["gate_th"][:], 0.5, 0.5, ALU.mult, ALU.add))
            step(nc.vector.tensor_scalar(m["keep_gain"][:], m["gate_th"][:], -0.5, 0.5, ALU.mult, ALU.add))
            v.wait_ge(exps, 1)
            nc.vector.tensor_scalar(lay0["neg_u"][:], m["u_exp"][:], -0.5, None, ALU.mult)
            nc.vector.tensor_scalar(keep["norm16"][:], keep["norm_cols"][:], float(D) ** 0.5, None, ALU.mult)
            nc.vector.tensor_scalar(keep["gnorm4"][:], keep["gnorm_col"][:], float(DV) ** 0.5 / 2, None, ALU.mult)
            v.wait_ge(loaded, 16 * 5)
            for k in range(KC):
                w = m["w_raw"][:, MIX + k * D:MIX + (k + 1) * D]
                step(nc.vector.tensor_tensor(w, w, m["mix_gain"][:], ALU.mult))
                step(nc.vector.tensor_tensor(m["w_raw"][:, DIAG + k * P:DIAG + (k + 1) * P], keep["ident"][:],
                                             m["keep_gain"][:, k * P:(k + 1) * P], ALU.mult))
            v.sem_inc(raw_ready, 1)
            finish_rows(1)
            v.wait_ge(x_loaded, 16)
            first.moments(v, step, 0)
            v.wait_ge(hi_ready, 2)
            nc.vector.tensor_tensor(lay0["w0"][1][:], m["w_raw"][:, 0:ROUT], f32(lay0["w0"][0][:]), ALU.subtract)
            nc.vector.tensor_tensor(lay0["w_gate"][1][:, :, 0:E], router, f32(lay0["w_gate"][0][:, :, 0:E]), ALU.subtract)
            for l in range(2):
                v.wait_ge(cols_done, l + 1)
                nc.vector.tensor_copy(keep[f"mod_col{l}"][:].rearrange("p m b -> p (m b)"), bank[6 + l][:, 0:MODS * KC * B])
            first.norm(v, 0)
            for n, (target, _, _, i) in enumerate(wide):
                if n % 2:
                    v.wait_ge(wide_done, n + 1)
                    nc.vector.tensor_copy(target, bank[i][:])

        @block.tensor
        def _(pe):
            pe.wait_ge(silu, 1)
            for l in range(2):
                pe.wait_ge(wmod_in[l], 16)
                for n in range(3):
                    for k in range(KC):
                        last = nc.tensor.matmul(bank[3 * l + n][0:B, :], m["c_silu"][:, l, k, :], m["wmod"][l][:, k, n * N:(n + 1) * N],
                                                start=(k == 0), stop=(k == KC - 1))
                    last.then_inc(rows_done, 1)
            for l in range(2):
                pe.wait_ge(rows_ready, l + 1)
                for i in range(MODS * KC):
                    last = nc.tensor.transpose(bank[6 + l][:, i * B:(i + 1) * B], flat(m["rows"][l][0:B])[:, i * P:(i + 1) * P],
                                               keep["ident"][0:B, 0:B])
                last.then_inc(cols_done, 1)
                for n, (_, layer, b, i) in enumerate(wide):
                    if layer != l:
                        continue
                    if n < 4:
                        for k, which in enumerate((2, 5)):
                            last = nc.tensor.matmul(bank[i][:, k * D:(k + 1) * D], m["pick"][0:B, b, :], m["rows"][l][0:B, which, :],
                                                    start=True, stop=True)
                    else:
                        last = nc.tensor.matmul(bank[i][:], m["pick"][0:B, b, :], flat(m["rows"][l][0:B, 0:2, :]), start=True, stop=True)
                    last.then_inc(wide_done, 1)


def mix_and_key_value(nc, sem, a, bank, keep, lay0, m, first):
    NS, TURNS = 2 * B, J // 2
    slots = first.SLOTS
    m.slots(["mn"], [D], NS)
    m.slots(["feat", "mfeat"], [KC, P], NS)
    m.pair_slots(["f", "mf"], [KC, P], NS)
    m.slots(["mstats"], [6], NS)
    m.slots(["mmv"], [2], NS)
    m.slots(["mve", "mrstd"], [1], NS)
    m.slots(["kth", "karg", "kexp"], [S], NS)
    experts = ((lay0["w_gate"], "w_gate", E), (lay0["w_up"], "w_up", 0), (lay0["w_down"], "w_down", 0))
    m["raw"] = [m.add("raw_" + name, [w[0].shape[1], (w[0].shape[2] - first_col) // TURNS]) for w, name, first_col in experts]

    def signal(name, per_turn=NS, ahead=False):
        return Signal(sem("mix_" + name), per_turn, ahead)
    xT, feat, f_hi, f_lo = (signal(n) for n in ("xT", "feat", "f_hi", "f_lo"))
    mixed, mvar, mrstd, mn, mT, mfeat, mf_hi, mf_lo = (signal(n) for n in (
        "mixed", "mvar", "mrstd", "mn", "mT", "mfeat", "mf_hi", "mf_lo"))
    kv, kth, karg, kexp = (signal(n) for n in ("kv", "ktanh", "karg", "kexp"))
    wkv = signal("wkv", ahead=True)
    raw_in = [sem(f"mix_raw_in{i}") for i in range(3)]
    raw_hi, raw_lo = signal("raw_hi", 3), signal("raw_lo", 3, True)
    v_steps, p_steps = signal("v_steps", 2 * NS), signal("p_steps", 1 + NS)

    def piece(i, part, t):
        w, _, first_col = experts[i]
        n = m["raw"][i].shape[2]
        return w[part][:, :, bass.ds(t * n + first_col, n)]

    with nc.Block() as block:
        @block.sync
        def _(sp):
            for sig in (wkv, raw_lo):
                sp.sem_inc(sig.sem, sig.per_turn)
            with nc.sync.Fori(0, TURNS) as t:
                for i, (_, name, _) in enumerate(experts):
                    sp.wait_ge(raw_lo.sem, raw_lo.before(t, i))
                    sp.dma_start(m["raw"][i][:], a[name][bass.ds(t, 1)].rearrange("a p k n -> p (a k) n")).then_inc(raw_in[i], 16)

        @block.gpsimd
        def _(pool):
            def low(t, full, pair, got, gone):
                for s, _, _ in slots:
                    pool.wait_ge(got.sem, got.now(t, s))
                    nc.gpsimd.tensor_tensor(pair[s][1][:], full[s][:], f32(pair[s][0][:]), ALU.subtract).then_inc(gone.sem, 1)

            def body(t, step, ahead=True):
                for s, _, _ in slots:
                    if s == 2 and ahead:
                        first.rsqrt(pool, step, t + 1)
                    pool.wait_ge(mvar.sem, mvar.now(t, s))
                    step(nc.gpsimd.tensor_tensor(m["mve"][s][:], m["mmv"][s][:, 1:2], keep["ln_eps"][:], ALU.add))
                    nc.gpsimd.tensor_tensor(m["mrstd"][s][:], m["mve"][s][:], keep["neg_half"][:, 0:1], ALU.pow).then_inc(mrstd.sem, 1)
                low(t, m["mfeat"], m["mf"], mf_hi, mf_lo)
                if ahead:
                    low(t + 1, m["feat"], m["f"], f_hi, f_lo)
            low(0, m["feat"], m["f"], f_hi, f_lo)
            with nc.gpsimd.Fori(0, TURNS - 1) as t:
                step = Steps(pool, p_steps, t)
                body(t, step)
            step.end(TURNS - 1)
            step = Steps(pool, p_steps)
            body(TURNS - 1, step, False)
            step.end()

        @block.vector
        def _(v):
            def high(t, s, full, pair, got, gone):
                v.wait_ge(got.sem, got.now(t, s))
                nc.vector.tensor_copy(pair[s][0][:], full[s][:]).then_inc(gone.sem, 1)

            def weights_low(t, i):
                v.wait_ge(raw_hi.sem, raw_hi.now(t, i))
                nc.vector.tensor_tensor(piece(i, 1, t), m["raw"][i][:], f32(piece(i, 0, t)), ALU.subtract).then_inc(raw_lo.sem, 1)

            def body(t, step, ahead=True):
                if ahead:
                    first.moments(v, step, t + 1)
                def second_norm(s):
                    if s < 0:
                        return
                    v.wait_ge(mrstd.sem, mrstd.now(t, s))
                    nc.vector.tensor_scalar(m["mn"][s][:], bank[4 + s][:, 0:D], m["mmv"][s][:, 0:1], m["mrstd"][s][:],
                                            ALU.subtract, ALU.mult).then_inc(mn.sem, 1)
                for s, _, _ in slots:
                    v.wait_ge(mixed.sem, mixed.now(t, s))
                    moments(nc, v, step, keep["spare"][:, s:s + 1], [(m["mstats"][s][:], m["mmv"][s][:], bank[4 + s][:, 0:D])], mvar)
                    second_norm(s - 1)
                second_norm(NS - 1)
                if ahead:
                    first.norm(v, t + 1)
                for s, _, _ in slots:
                    high(t, s, m["mfeat"], m["mf"], mfeat, mf_hi)
                for s, _, _ in slots:
                    if s < len(experts):
                        weights_low(t, s)
                    if ahead:
                        high(t + 1, s, m["feat"], m["f"], feat, f_hi)
                for s, _, _ in slots:
                    v.wait_ge(kth.sem, kth.now(t, s))
                    nc.vector.scalar_tensor_tensor(m["karg"][s][:], m["kth"][s][:], 1.0, lay0["neg_u"][:], ALU.add,
                                                   ALU.mult).then_inc(karg.sem, 1)
                for s, b, h in slots:
                    v.wait_ge(kexp.sem, kexp.now(t, s))
                    o = lay0["wkv_tok"][:, bass.ds(t + h * TURNS, 1), b, :].rearrange("p a s -> p (a s)")
                    nc.vector.tensor_tensor(o, bank[4 + s][:, S:2 * S], m["kexp"][s][:], ALU.mult).then_inc(wkv.sem, 1)
            for s, _, _ in slots:
                high(0, s, m["feat"], m["f"], feat, f_hi)
            with nc.vector.Fori(0, TURNS - 1) as t:
                step = Steps(v, v_steps, t)
                body(t, step)
            step.end(TURNS - 1)
            step = Steps(v, v_steps)
            body(TURNS - 1, step, False)
            step.end()

        @block.scalar
        def _(act):
            def affine(t, bk, full, got, gone, columns):
                for s, b, _ in slots:
                    act.wait_ge(got.sem, got.now(t, s))
                    for c in range(KC):
                        scale, shift = columns(b, c)
                        last = nc.scalar.activation(full[s][:, c, :], bank[bk + s][:, c * P:(c + 1) * P], ACT.Identity, bias=shift, scale=scale)
                    last.then_inc(gone.sem, 1)

            def modulated(t):
                affine(t, 0, m["feat"], xT, feat, lambda b, c: (keep["mod_col0"][:, KC + c, b:b + 1], keep["mod_col0"][:, c, b:b + 1]))

            def body(t, ahead=True):
                for i in range(len(experts)):
                    act.wait_ge(raw_in[i], t * 16 + 16)
                    nc.scalar.copy(piece(i, 0, t), m["raw"][i][:]).then_inc(raw_hi.sem, 1)
                affine(t, 4, m["mfeat"], mT, mfeat, lambda b, c: (lay0["ln_col"][:, 0, c:c + 1], lay0["ln_col"][:, 1, c:c + 1]))
                if ahead:
                    modulated(t + 1)
                for s, _, _ in slots:
                    act.wait_ge(kv.sem, kv.now(t, s))
                    nc.scalar.activation(m["kth"][s][:], bank[4 + s][:, 0:S], ACT.Tanh, scale=0.5).then_inc(kth.sem, 1)
                for s, _, _ in slots:
                    act.wait_ge(karg.sem, karg.now(t, s))
                    nc.scalar.activation(m["kexp"][s][:], m["karg"][s][:], ACT.Exp).then_inc(kexp.sem, 1)
            modulated(0)
            with nc.scalar.Fori(0, TURNS - 1) as t:
                body(t)
            body(TURNS - 1, False)

        @block.tensor
        def _(pe):
            def w0(first, n):
                return [w[:, first:first + n] for w in lay0["w0"]]

            def chunk(pair, c):
                return [x[:, c, :] for x in pair]

            def transposes(t, bk, src, got, gone):
                for s, _, _ in slots:
                    pe.wait_ge(got.sem, got.now(t, s))
                    for c in range(KC):
                        last = nc.tensor.transpose(bank[bk + s][:, c * P:(c + 1) * P], src[s][:, c * P:(c + 1) * P], keep["ident"][:])
                    last.then_inc(gone.sem, 1)

            def body(t, ahead=True):
                pe.wait_ge(f_lo.sem, f_lo.now(t, NS - 1))
                for s, b, h in slots:
                    partner = 2 * b + 1 - h
                    pe.wait_ge(wkv.sem, wkv.before(t, s))
                    product3(nc, bank[4 + s][:, 0:D], [(chunk(m["f"][partner], c), w0(MIX + c * D, D)) for c in range(KC)],
                             last=False)
                    for c in range(KC):
                        last = product3(nc, bank[4 + s][:, c * P:(c + 1) * P], [(chunk(m["f"][s], c), w0(DIAG + c * P, P))],
                                        first=False)
                    last.then_inc(mixed.sem, 1)
                transposes(t, 4, m["mn"], mn, mT)
                if ahead:
                    transposes(t + 1, 0, first.m["xn"], first.xn, xT)
                for s, _, _ in slots:
                    pe.wait_ge(mf_lo.sem, mf_lo.now(t, s))
                    product3(nc, bank[4 + s][:, 0:2 * S], [(chunk(m["mf"][s], c), w0(KV + c * P, P)) for c in range(KC)]
                             ).then_inc(kv.sem, 1)
            transposes(0, 0, first.m["xn"], first.xn, xT)
            with nc.tensor.Fori(0, TURNS - 1) as t:
                body(t)
            body(TURNS - 1, False)


class Recurrence:

    def __init__(self, nc, sem, bank, keep, lay0):
        self.nc, self.bank, self.keep, self.lay0 = nc, bank, keep, lay0
        self.turned, self.scanned = sem("wkv_turned"), sem("scanned")

    def turn(self):
        for j in range(J):
            self.nc.tensor.transpose(self.bank[j // 4][:, (j % 4) * P:(j % 4 + 1) * P],
                                     flat(self.lay0["wkv_tok"][:, j]), self.keep["ident"][:]).then_inc(self.turned, 1)

    def scan(self, v):
        states, half = self.lay0["states"], T // 2
        for k in range(2):
            v.wait_ge(self.turned, (k + 1) * J // 2)
            if k:
                v.wait_ge(self.scanned, 1)
            self.nc.vector.tensor_tensor_scan(states[:, k * half:(k + 1) * half], self.lay0["decay"][:].to_broadcast([P, half]),
                                              self.bank[k][:], states[:, half - 1:half] if k else 0.0, ALU.mult, ALU.add
                                              ).then_inc(self.scanned, 1)


class Cut:

    def __init__(self, nc, sem, m, a, name, parts):
        self.nc, self.a, self.parts = nc, a, parts
        n = len(parts)
        self.loaded = [sem(f"{name}_loaded{i}") for i in range(n)]
        self.scaled = Signal(sem(f"{name}_scaled"), n, True)
        self.hi = Signal(sem(f"{name}_hi"), n)
        self.lo = Signal(sem(f"{name}_lo"), n, True)
        shapes = [[w[0].shape[1], w[0].shape[2] // J] for _, _, w, _ in parts]
        self.raw = [m.add(f"{name}_raw{i}", shape, parts[i][1]) for i, shape in enumerate(shapes)]
        self.full = [m.add(f"{name}_full{i}", shape) for i, shape in enumerate(shapes)]

    def piece(self, w, t):
        n = w.shape[2] // J
        return w[:, :, bass.ds(t * n, n)]

    def start(self, sp):
        for sig in (self.scaled, self.lo):
            sp.sem_inc(sig.sem, sig.per_turn)

    def load(self, sp, t):
        for i, (name, _, _, _) in enumerate(self.parts):
            sp.wait_ge(self.scaled.sem, self.scaled.before(t, i))
            sp.dma_start(self.raw[i][:], self.a[name][bass.ds(t, 1)].rearrange("a p k n -> p (a k) n")).then_inc(self.loaded[i], 16)

    def scale(self, v, t):
        for i, (_, _, _, scaling) in enumerate(self.parts):
            v.wait_ge(self.loaded[i], t * 16 + 16)
            v.wait_ge(self.lo.sem, self.lo.before(t, i))
            scaling(self.full[i], self.raw[i], t).then_inc(self.scaled.sem, 1)

    def take_hi(self, act, t):
        for i, (_, _, w, _) in enumerate(self.parts):
            act.wait_ge(self.scaled.sem, self.scaled.now(t, i))
            self.nc.scalar.copy(self.piece(w[0], t), self.full[i][:]).then_inc(self.hi.sem, 1)

    def take_lo(self, v, t):
        for i, (_, _, w, _) in enumerate(self.parts):
            v.wait_ge(self.hi.sem, self.hi.now(t, i))
            self.nc.vector.tensor_tensor(self.piece(w[1], t), self.full[i][:], f32(self.piece(w[0], t)),
                                         ALU.subtract).then_inc(self.lo.sem, 1)


def by_column(nc, columns):
    def scaling(out, raw, t):
        for k in range(out.shape[1]):
            last = nc.vector.tensor_scalar(out[:, k, :], raw[:, k, :], columns(k), None, ALU.mult)
        return last
    return scaling


def by_constant(nc, value):
    return lambda out, raw, t: nc.vector.tensor_scalar(out[:], raw[:], value, None, ALU.mult)


def from_codes(nc, scales):
    def scaling(out, raw, t):
        k, n = out.shape[1], out.shape[2]
        return nc.vector.scalar_tensor_tensor(out[:], raw[:], ZERO_POINT, scales[:, bass.ds(t * n, n)].unsqueeze(1)
                                              .to_broadcast([P, k, n]), ALU.subtract, ALU.mult)
    return scaling


def gated_mlp(nc, sem, a, bank, keep, m, kinds, lay0, out, signals):
    experts = kinds[0] == "experts"
    NS = B
    G, W = (EG, GW) if experts else (IG, IW)
    mod_col, gate_row = (keep["mod_col0"], keep["gate_row0"]) if experts else (keep["mod_col1"], keep["gate_row1"])
    w_down = {k: lay0["w_down"] if experts else keep[f"w_{k}_down"] for k in kinds}

    m.slots(["xn", "tmp"], [D], NS)
    m.slots(["feat"], [KC, P], NS)
    m.pair_slots(["f"], [KC, P], NS)
    m.slots(["th", "silu", "prod"], [W], NS)
    m.slots(["hid"], [3 * P], NS)
    m.pair_slots(["h"], [3, P], NS)
    m.slots(["stats"], [6], NS)
    m.slots(["mv"], [2], NS)
    m.slots(["ve", "rstd"], [1], NS)
    if experts:
        m.pair("st", [P])
        m.slots(["best"], [8], NS)
        m.slots(["first", "second", "share"], [E], NS)
        m.slots(["lead", "lead_th"], [1], NS)
        m.slots(["weight"], [2], NS)
        m.slots(["index"], [8], NS, U32)
        m.slots(["place"], [2], NS)
        m.add("iota", [E])
        cut = Cut(nc, sem, m, a, "cut1", [
            ("w_qkvg", F32, keep["w_qkvg"], by_column(nc, lambda k: keep["norm16"][:, 0, k:k + 1])),
            ("w_o", F32, keep["w_o"], by_column(nc, lambda k: keep["gnorm4"][:]))])
    else:
        m.add("s_in", [IG * 2 * IW])
        m.add("s_down", [D])
        m.add("s_down_half", [D])
        cut = Cut(nc, sem, m, a, "cut3", [("w_ffn", I32, keep["w_ffn"], from_codes(nc, m["s_in"])),
                                          ("w_ffn_down", I32, keep["w_ffn_down"], from_codes(nc, m["s_down_half"]))])

    def signal(name, per_turn=NS, ahead=False):
        if name in signals:
            return signals[name].again(per_turn)
        signals[name] = Signal(sem("gated_" + name), per_turn, ahead)
        return signals[name]
    moment, rstd, xn, xT, f_hi, f_lo = (signal(n) for n in ("moment", "rstd", "xn", "xT", "f_hi", "f_lo"))
    gu, th, hT, h_hi, h_lo = (signal(n, NS * G) for n in ("gate_up", "tanh", "hid_T", "h_hi", "h_lo"))
    prod = signal("prod", NS * G, True)
    down = signal("down")
    x_out = signal("x_out", NS, True)
    if experts:
        states = Recurrence(nc, sem, bank, keep, lay0)
        st_hi, st_lo = signal("st_hi", 1), signal("st_lo", 1)
        attn = signal("attn", NS, True)
        placed, lead, lead_tanh, share, attn_used = (signal(n) for n in ("placed", "lead", "lead_tanh", "share", "attn_used"))
        hid = signal("hid", NS * G)
    else:
        hid = prod
    v_steps = signal("v_steps", 22 if experts else 8)
    p_steps = signal("p_steps")
    ready = sem(f"{kinds[0]}_ready")
    if out is not None:
        stored = sem("stored")
    slots = range(NS)

    def tile(k, t):
        return t - kinds.index(k) * J

    def turns(engine, body, steps=None):
        for i, k in enumerate(kinds):
            with engine.Fori(0, J - 1) as t:
                step = Steps(engine, steps, t) if steps else None
                body(t + i * J, k, k, step)
            if steps:
                step.end(J - 1)
            step = Steps(engine, steps) if steps else None
            body(i * J + J - 1, k, kinds[i + 1] if i + 1 < len(kinds) else None, step)
            if steps:
                step.end()
    at = lambda gr, s: gr * NS + s

    def gate_of(s, gr):
        first = E if experts and gr == 0 else 0
        return GATE(s)[:, first:first + W]

    def A(s): return bank[4 * s]
    def GATE(s): return bank[4 * s + 1]
    def UP(s): return bank[4 * s + 2]
    def TURN(s): return bank[4 * s + 3]

    with nc.Block() as block:
        @block.sync
        def _(sp):
            if experts:
                for sig in (x_out, prod, attn):
                    sp.sem_inc(sig.sem, sig.per_turn)
                sp.dma_start(m["iota"][:], a["iota"].partition_broadcast(P)).then_inc(ready, 16)
            else:
                sp.dma_start(m["s_in"][:], a["s_ffn"].partition_broadcast(P)).then_inc(ready, 16)
                sp.dma_start(m["s_down"][:], a["s_ffn_down"].partition_broadcast(P)).then_inc(ready, 16)
            cut.start(sp)
            with nc.sync.Fori(0, J) as t:
                cut.load(sp, t)
            if out is not None:
                with nc.sync.Fori(0, J) as t:
                    for s in slots:
                        sp.wait_ge(x_out.sem, x_out.now(t + J * (len(kinds) - 1), s))
                        sp.dma_start(out[s].rearrange("(j p) d -> j p d", p=P)[bass.ds(t, 1)].rearrange("a p d -> p (a d)"),
                                     row(keep["x"], s, t)).then_inc(stored, 16)
                sp.wait_ge(stored, 16 * NS * J)

        @block.gpsimd
        def _(pool):
            def states_low(t):
                if experts:
                    pool.wait_ge(st_hi.sem, st_hi.now(t))
                    nc.gpsimd.tensor_tensor(m["st"][1][:], lay0["states"][:, bass.ds(t * P, P)], f32(m["st"][0][:]),
                                            ALU.subtract).then_inc(st_lo.sem, 1)

            def rsqrt(t, k, step):
                for s in slots:
                    pool.wait_ge(moment.sem, moment.now(t, s))
                    if k == "mlp":
                        step(nc.gpsimd.tensor_tensor(m["ve"][s][:], m["mv"][s][:, 0:1], keep["rms_eps"][:], ALU.add))
                    else:
                        step(nc.gpsimd.tensor_tensor(m["ve"][s][:], m["mv"][s][:, 1:2], keep["ln_eps"][:], ALU.add))
                    nc.gpsimd.tensor_tensor(m["rstd"][s][:], m["ve"][s][:], keep["neg_half"][:, 0:1], ALU.pow).then_inc(rstd.sem, 1)

            def weigh(t, gr):
                for s in slots:
                    if gr == 0:
                        pool.wait_ge(share.sem, share.now(t, s))
                    pool.wait_ge(prod.sem, prod.now(t, at(gr, s)))
                    nc.gpsimd.tensor_tensor(
                        m["hid"][s][:].rearrange("p (e f) -> p e f", f=FE), m["prod"][s][:].rearrange("p (e f) -> p e f", f=FE),
                        m["share"][s][:, gr * (E // G):(gr + 1) * (E // G)].unsqueeze(2).to_broadcast([P, E // G, FE]),
                        ALU.mult).then_inc(hid.sem, 1)

            def body(t, k, following, step):
                if following:
                    states_low(t + 1)
                for gr in range(1, G):
                    if experts:
                        weigh(t, gr)
                    if gr == 1 and following:
                        rsqrt(t + 1, following, step)
                if experts and following:
                    weigh(t + 1, 0)
            step = Steps(pool, p_steps)
            states_low(0)
            rsqrt(0, kinds[0], step)
            step.end()
            if experts:
                weigh(0, 0)
            turns(nc.gpsimd, body, p_steps)

        @block.vector
        def _(v):
            def gate_attention(t, s):
                if experts:
                    v.wait_ge(attn.sem, attn.now(t, s))
                    nc.vector.tensor_tensor(m["tmp"][s][:], A(s)[:, 0:D], gate_row[:, s, 0, :], ALU.mult).then_inc(attn_used.sem, 1)

            def add_attention(t, s, step):
                if experts:
                    v.wait_ge(attn_used.sem, attn_used.now(t, s))
                    step(nc.vector.tensor_tensor(row(keep["x"], s, t), row(keep["x"], s, t), m["tmp"][s][:], ALU.add))

            def moments_of_x(t, k, step):
                if k != "mlp":
                    moments(nc, v, step, keep["spare"], [(m["stats"][s][:], m["mv"][s][:], row(keep["x"], s, tile(k, t)))
                                                         for s in slots], moment)

            def norm(t, k, s):
                v.wait_ge(rstd.sem, rstd.now(t, s))
                if k == "mlp":
                    nc.vector.tensor_scalar(m["xn"][s][:], row(keep["r2"], s, t), m["rstd"][s][:], None, ALU.mult).then_inc(xn.sem, 1)
                else:
                    nc.vector.tensor_scalar(m["xn"][s][:], row(keep["x"], s, tile(k, t)), m["mv"][s][:, 0:1], m["rstd"][s][:],
                                            ALU.subtract, ALU.mult).then_inc(xn.sem, 1)

            def features_low(t, k, s):
                v.wait_ge(f_hi.sem, f_hi.now(t, s))
                full = GATE(s)[:, 0:D] if k == "mlp" else flat(m["feat"][s][:])
                nc.vector.tensor_tensor(flat(m["f"][s][1][:]), full, f32(flat(m["f"][s][0][:])), ALU.subtract).then_inc(f_lo.sem, 1)

            def routing(t, s, step):
                v.wait_ge(gu.sem, gu.now(t, at(0, s)))
                nc.vector.memset(keep["spare"][:], 0.0)
                step(nc.vector.max(m["best"][s][:], GATE(s)[:, 0:E]))
                nc.vector.tensor_tensor(m["lead"][s][:], m["best"][s][:, 0:1], m["best"][s][:, 1:2], ALU.subtract).then_inc(lead.sem, 1)
                nc.vector.max_index(m["index"][s][:], m["best"][s][:], GATE(s)[:, 0:E]).then_inc(placed.sem, 1)
                v.wait_ge(placed.sem, placed.now(t, s))
                step(nc.vector.tensor_copy(m["place"][s][:], m["index"][s][:, 0:2]))
                v.wait_ge(lead_tanh.sem, lead_tanh.now(t, s))
                nc.vector.tensor_scalar(m["weight"][s][:, 0:1], m["lead_th"][s][:], 0.25, 0.25, ALU.mult, ALU.add)
                step(nc.vector.tensor_scalar(m["weight"][s][:, 1:2], m["lead_th"][s][:], -0.25, 0.25, ALU.mult, ALU.add))
                nc.vector.tensor_scalar(m["first"][s][:], m["iota"][:], m["place"][s][:, 0:1], m["weight"][s][:, 0:1], ALU.is_equal, ALU.mult)
                step(nc.vector.tensor_scalar(m["second"][s][:], m["iota"][:], m["place"][s][:, 1:2], m["weight"][s][:, 1:2], ALU.is_equal, ALU.mult))
                nc.vector.tensor_tensor(m["share"][s][:], m["first"][s][:], m["second"][s][:], ALU.add).then_inc(share.sem, 1)

            def product(t, gr, s, step):
                v.wait_ge(th.sem, th.now(t, at(gr, s)))
                step(nc.vector.scalar_tensor_tensor(m["silu"][s][:], m["th"][s][:], 1.0, gate_of(s, gr), ALU.add, ALU.mult))
                o = m["prod"][s][:] if experts else m["hid"][s][:, 0:W]
                nc.vector.tensor_tensor(o, m["silu"][s][:], UP(s)[:, 0:W], ALU.mult).then_inc(prod.sem, 1)

            def add_to_x(t, k, s, step):
                v.wait_ge(down.sem, down.now(t, s))
                gate = gate_row[:, s, 0 if k == "mlp" else 1, :]
                if k == "mlp":
                    step(nc.vector.tensor_tensor(m["tmp"][s][:], A(s)[:, 0:D], row(keep["r2"], s, t), ALU.add))
                    step(nc.vector.tensor_tensor(m["tmp"][s][:], m["tmp"][s][:], gate, ALU.mult))
                else:
                    step(nc.vector.tensor_tensor(m["tmp"][s][:], A(s)[:, 0:D], gate, ALU.mult))
                x = row(keep["x"], s, tile(k, t))
                nc.vector.tensor_tensor(x, x, m["tmp"][s][:], ALU.add).then_inc(x_out.sem, 1)

            def body(t, k, following, step):
                for gr in range(G):
                    if gr == G - 1 and following:
                        for s in slots:
                            features_low(t + 1, following, s)
                    for s in slots:
                        if following and gr == G - 2 and s == 1:
                            norm(t + 1, following, 0)
                        if following and gr == 0 and s == 1:
                            gate_attention(t + 1, 0)
                        v.wait_ge(h_hi.sem, h_hi.now(t, at(gr, s)))
                        nc.vector.tensor_tensor(flat(m["h"][s][1][:]), TURN(s)[:, 0:3 * P], f32(flat(m["h"][s][0][:])),
                                                ALU.subtract).then_inc(h_lo.sem, 1)
                        if following and gr == 0 and s == 0 and not experts:
                            moments_of_x(t + 1, following, step)
                        if following and gr == 0 and s == 1:
                            gate_attention(t + 1, 1)
                            for n in slots:
                                add_attention(t + 1, n, step)
                        if following and gr == G - 2 and s == 1:
                            norm(t + 1, following, 1)
                        if gr + 1 < G:
                            product(t, gr + 1, s, step)
                    if following and experts and gr == 0:
                        moments_of_x(t + 1, following, step)
                    if k == kinds[0] and gr == 0:
                        cut.scale(v, t)
                if k == kinds[0]:
                    cut.take_lo(v, t)
                for s in slots:
                    if following:
                        if experts:
                            routing(t + 1, s, step)
                        product(t + 1, 0, s, step)
                    if not experts:
                        add_to_x(t, k, s, step)
                if experts:
                    for s in slots:
                        add_to_x(t, k, s, step)
            if not experts:
                for s in slots:
                    nc.vector.memset(m["hid"][s][:, W:3 * P], 0.0)
            if experts:
                states.scan(v)
            step = Steps(v, v_steps)
            for s in slots:
                gate_attention(0, s)
            for s in slots:
                add_attention(0, s, step)
            moments_of_x(0, kinds[0], step)
            for s in slots:
                norm(0, kinds[0], s)
            if experts:
                v.wait_ge(ready, 16)
            for s in slots:
                features_low(0, kinds[0], s)
            for s in slots:
                if experts:
                    routing(0, s, step)
                product(0, 0, s, step)
            step.end()
            if not experts:
                v.wait_ge(ready, 32)
                nc.vector.tensor_scalar(m["s_down_half"][:], m["s_down"][:], 0.5, None, ALU.mult)
            turns(nc.vector, body, v_steps)

        @block.scalar
        def _(act):
            def front(t, k):
                if experts:
                    act.wait_ge(attn.sem, attn.before(t, NS - 1))
                    nc.scalar.copy(m["st"][0][:], lay0["states"][:, bass.ds(t * P, P)]).then_inc(st_hi.sem, 1)
                if k == "mlp":
                    for s in slots:
                        nc.scalar.activation(m["feat"][s][:].rearrange("p k n -> p (k n)"), row(keep["r2"], s, t), ACT.Square,
                                             accum_out=m["mv"][s][:, 0:1]).then_inc(moment.sem, 1)

            def features(t, k, s):
                act.wait_ge(xT.sem, xT.now(t, s))
                if k == "mlp":
                    nc.scalar.copy(flat(m["f"][s][0][:]), GATE(s)[:, 0:D]).then_inc(f_hi.sem, 1)
                    return
                for c in range(KC):
                    scale, shift = mod_col[:, 4 * KC + c, s:s + 1], mod_col[:, 3 * KC + c, s:s + 1]
                    ps = GATE(s)[:, c * P:(c + 1) * P]
                    nc.scalar.activation(m["feat"][s][:, c, :], ps, ACT.Identity, bias=shift, scale=scale)
                    last = nc.scalar.activation(m["f"][s][0][:, c, :], ps, ACT.Identity, bias=shift, scale=scale)
                last.then_inc(f_hi.sem, 1)

            def lead_of(t, s):
                act.wait_ge(lead.sem, lead.now(t, s))
                nc.scalar.activation(m["lead_th"][s][:], m["lead"][s][:], ACT.Tanh, scale=0.5).then_inc(lead_tanh.sem, 1)

            def tanh(t, gr, s):
                act.wait_ge(gu.sem, gu.now(t, at(gr, s)))
                if experts and gr == 0:
                    act.wait_ge(placed.sem, placed.now(t, s))
                nc.scalar.activation(m["th"][s][:], gate_of(s, gr), ACT.Tanh, scale=0.5).then_inc(th.sem, 1)

            def body(t, k, following, step):
                if following:
                    front(t + 1, following)
                for gr in range(G):
                    if gr == G - 1 and following:
                        for s in slots:
                            features(t + 1, following, s)
                    for s in slots:
                        act.wait_ge(hT.sem, hT.now(t, at(gr, s)))
                        nc.scalar.copy(flat(m["h"][s][0][:]), TURN(s)[:, 0:3 * P]).then_inc(h_hi.sem, 1)
                        if gr + 1 < G:
                            tanh(t, gr + 1, s)
                    if k == kinds[0] and gr == 1:
                        cut.take_hi(act, t)
                if following:
                    for s in slots:
                        if experts:
                            lead_of(t + 1, s)
                        tanh(t + 1, 0, s)
            if experts:
                act.wait_ge(states.scanned, 1)
            front(0, kinds[0])
            if experts:
                act.wait_ge(states.scanned, 2)
            for s in slots:
                features(0, kinds[0], s)
            for s in slots:
                if experts:
                    lead_of(0, s)
                tanh(0, 0, s)
            turns(nc.scalar, body)

        @block.tensor
        def _(pe):
            def attention(t):
                pe.wait_ge(st_lo.sem, st_lo.now(t))
                for s in slots:
                    product3(nc, A(s)[:, 0:D], [([w[:] for w in m["st"]], [w[:, OUT0 + s * D:OUT0 + (s + 1) * D] for w in lay0["w0"]])]
                             ).then_inc(attn.sem, 1)

            def normed(t, s):
                pe.wait_ge(xn.sem, xn.now(t, s))
                pe.wait_ge(prod.sem, prod.before(t, at(G - 1, s)))
                for c in range(KC):
                    last = nc.tensor.transpose(GATE(s)[:, c * P:(c + 1) * P], m["xn"][s][:, c * P:(c + 1) * P], keep["ident"][:])
                last.then_inc(xT.sem, 1)

            def gate_up(t, k, gr, s):
                if gr == 0:
                    pe.wait_ge(f_lo.sem, f_lo.now(t, s))
                for which, ps in enumerate((GATE(s), UP(s))):
                    terms = []
                    router = E if experts and gr == 0 and which == 0 else 0
                    first = E if experts and which == 0 and gr else 0
                    for c in range(KC):
                        if experts:
                            w = [x[:, c, first + gr * W:first + router + (gr + 1) * W] for x in (lay0["w_up"] if which else lay0["w_gate"])]
                        else:
                            w = [x[:, c, (2 * gr + which) * W:(2 * gr + which + 1) * W] for x in keep["w_" + k]]
                        terms.append(([x[:, c, :] for x in m["f"][s]], w))
                    last = product3(nc, ps[:, 0:router + W], terms)
                last.then_inc(gu.sem, 1)

            def turn(t, gr, s):
                pe.wait_ge(hid.sem, hid.now(t, at(gr, s)))
                for c in range(3):
                    last = nc.tensor.transpose(TURN(s)[:, c * P:(c + 1) * P], m["hid"][s][:, c * P:(c + 1) * P], keep["ident"][:])
                last.then_inc(hT.sem, 1)

            def down_from(t, k, gr, s):
                last = product3(nc, A(s)[:, 0:D], [([x[:, c, :] for x in m["h"][s]], [w[:, gr * 3 + c, :] for w in w_down[k]])
                                                   for c in range(3)], first=gr == 0, last=gr == G - 1)
                if gr == G - 1:
                    last.then_inc(down.sem, 1)

            def body(t, k, following, step):
                if k != kinds[0]:
                    pe.wait_ge(cut.lo.sem, cut.lo.now(J - 1, 1))
                for gr in range(G):
                    for s in slots:
                        turn(t, gr, s)
                        if gr + 1 < G:
                            gate_up(t, k, gr + 1, s)
                    if gr == 0:
                        for s in slots:
                            pe.wait_ge(x_out.sem, x_out.before(t, s))
                        if experts and following:
                            attention(t + 1)
                    for s in slots:
                        if gr == G - 1 and following:
                            if k != following and s == 0:
                                pe.wait_ge(cut.lo.sem, cut.lo.now(J - 2, 1))
                            gate_up(t + 1, following, 0, s)
                        pe.wait_ge(h_lo.sem, h_lo.now(t, at(gr, s)))
                        if experts and gr == 0 and following:
                            pe.wait_ge(attn_used.sem, attn_used.now(t + 1, s))
                        down_from(t, k, gr, s)
                        if gr == G - 2 and following:
                            normed(t + 1, s)
            if experts:
                states.turn()
                attention(0)
            for s in slots:
                normed(0, s)
            for s in slots:
                gate_up(0, kinds[0], 0, s)
            turns(nc.tensor, body)
    for sig in signals.values():
        if sig is not v_steps and sig is not p_steps:
            sig.pass_turns(J * len(kinds))


def retention(nc, sem, a, bank, keep, m):
    NS, HG = B, H // 4
    QK = 2 * H * DK
    m.slots(["xn", "hn"], [D], NS)
    m.pair_slots(["f"], [KC, P], NS)
    m.slots(["work"], [2, QK], NS)
    m.slots(["rot"], [QK], NS)
    m.slots(["on"], [HV], NS)
    m.slots(["sgate"], [HV], NS)
    m.pair_slots(["k"], [H * DK], NS)
    m.pair_slots(["v"], [HV], NS)
    m.pair_slots(["qkT"], [4, P], NS)
    m.pair_slots(["score"], [HG, 4, P], NS)
    m["oT"] = [[x[:, 0] for x in pair] for pair in m["score"]]
    m.slots(["state"], [HG, 4 * DV], NS)
    m.pair_slots(["S"], [HG, 4 * DV], NS)
    m.slots(["stats"], [6], NS)
    m.slots(["mv"], [2], NS)
    m.slots(["ve", "rstd", "sumsq", "hve", "hrstd"], [1], NS)
    m.slots(["hsum", "heps", "hrms"], [H], NS)
    m.add("rope", [2, QK])
    m.add("state_mask", [HG, 4 * DV])
    m.add("state_gain", [HG])
    m.add("pool_spare", [NS])
    cut = Cut(nc, sem, m, a, "cut2", [
        ("w_mlp", F32, keep["w_mlp"], by_column(nc, lambda k: keep["norm16"][:, 1, k:k + 1])),
        ("w_mlp_down", F32, keep["w_mlp_down"], by_constant(nc, 0.5))])

    def signal(name, per_turn=NS, ahead=False):
        return Signal(sem("ret_" + name), per_turn, ahead)
    (moment, rstd, h_ready, sumsq, hrstd, hn, hT, f_hi, f_lo, qk, val, gate) = (signal(n) for n in (
        "moment", "rstd", "h", "sumsq", "hrstd", "hn", "hT", "f_hi", "f_lo", "qk", "val", "gate"))
    terms, rot, k_lo, v_hi, v_lo, tanh, sgate, qkT, qkT_hi, qkT_lo = (signal(n) for n in (
        "rope_terms", "rot", "k_lo", "v_hi", "v_lo", "tanh", "sgate", "qkT", "qkT_hi", "qkT_lo"))
    scores, copied_a, copied_v, masked, s_hi, s_lo = (signal(n) for n in (
        "scores", "copied_act", "copied_dve", "masked", "score_hi", "score_lo"))
    o_done, st_done, st_sum, S_hi = (signal(n) for n in ("o", "state_product", "state_sum", "S_hi"))
    S_lo = signal("S_lo", NS, True)
    square, hsum, hrms, on, oT, oT_hi, oT_lo, proj = (signal(n) for n in (
        "square", "head_sum", "head_rms", "out_norm", "oT", "oT_hi", "oT_lo", "proj"))
    r2_out = signal("r2", NS, True)
    k_hi = signal("k_hi")
    rope_in, ready, zeroed = (sem(f"ret_{n}") for n in ("rope_in", "ready", "zeroed"))
    v_steps, p_steps = signal("v_steps", 5 * NS), signal("p_steps", 3 * NS)
    slots = range(NS)

    def bk(s, i): return bank[4 * s + i]

    with nc.Block() as block:
        @block.sync
        def _(sp):
            cut.start(sp)
            for sig in (S_lo, r2_out):
                sp.sem_inc(sig.sem, sig.per_turn)
            sp.dma_start(m["state_mask"][:], a["state_mask"]).then_inc(ready, 16)
            sp.dma_start(m["state_gain"][:], a["state_gain"]).then_inc(ready, 16)
            sp.dma_start(m["rope"][:], a["rope"][0]).then_inc(rope_in, 16)
            with nc.sync.Fori(0, J - 1) as t:
                cut.load(sp, t)
                sp.wait_ge(terms.sem, terms.now(t, NS - 1))
                sp.dma_start(m["rope"][:], a["rope"][bass.ds(t + 1, 1)].rearrange("a p c n -> p (a c) n")).then_inc(rope_in, 16)
            cut.load(sp, J - 1)

        @block.gpsimd
        def _(pool):
            def rsqrt(t, s, step, got, out, tmp, x, eps, gone):
                pool.wait_ge(got.sem, got.now(t, s))
                step(nc.gpsimd.tensor_tensor(tmp[s][:], x, eps[:], ALU.add))
                nc.gpsimd.tensor_tensor(out[s][:], tmp[s][:], keep["neg_half"][:, 0:out[s].shape[1]], ALU.pow).then_inc(gone.sem, 1)

            def layer_norm(t, step):
                for s in slots:
                    rsqrt(t, s, step, moment, m["rstd"], m["ve"], m["mv"][s][:, 1:2], keep["ln_eps"], rstd)

            def rms_norm(t, step):
                for s in slots:
                    rsqrt(t, s, step, sumsq, m["hrstd"], m["hve"], m["sumsq"][s][:], keep["rms_eps"], hrstd)

            def rotated(t, s):
                pool.wait_ge(terms.sem, terms.now(t, s))
                nc.gpsimd.tensor_tensor(m["rot"][s][:], m["work"][s][:, 0, :], m["work"][s][:, 1, :], ALU.add).then_inc(rot.sem, 1)

            def keys_low(t):
                for s in slots:
                    pool.wait_ge(k_hi.sem, k_hi.now(t, s))
                    nc.gpsimd.tensor_tensor(m["k"][s][1][:], m["rot"][s][:, H * DK:QK], f32(m["k"][s][0][:]), ALU.subtract).then_inc(k_lo.sem, 1)

            def body(t, step, ahead=True, norms=True):
                for s in slots:
                    pool.wait_ge(copied_a.sem, copied_a.now(t, s))
                    pool.wait_ge(copied_v.sem, copied_v.now(t, s))
                    nc.gpsimd.tensor_tensor(m["pool_spare"][:, s:s + 1], keep["ln_eps"][:], keep["ln_eps"][:], ALU.add)
                    w = m["work"][s][:].rearrange("p a n -> p (a n)").rearrange("p (h i) -> p h i", i=P)
                    nc.gpsimd.affine_select(out=w, in_=w, pattern=[[0, H], [1, P]], compare_op=ALU.is_ge, fill=0.0,
                                            base=0, channel_multiplier=-1).then_inc(masked.sem, 1)
                if norms:
                    layer_norm(t + 2, step)
                for s in slots:
                    rsqrt(t, s, step, hsum, m["hrms"], m["heps"], m["hsum"][s][:], keep["head_eps"], hrms)
                if ahead:
                    for s in slots:
                        rotated(t + 1, s)
                        pool.wait_ge(S_hi.sem, S_hi.now(t, s))
                        nc.gpsimd.tensor_tensor(flat(m["S"][s][1][:]), flat(m["state"][s][:]), f32(flat(m["S"][s][0][:])),
                                                ALU.subtract).then_inc(S_lo.sem, 1)
                    keys_low(t + 1)
                if norms:
                    rms_norm(t + 2, step)
            step = Steps(pool, p_steps)
            layer_norm(0, step)
            rms_norm(0, step)
            for s in slots:
                for x in (*m["S"][s], m["state"][s]):
                    nc.gpsimd.memset(x[:] if x is m["state"][s] else f32(x[:]), 0.0).then_inc(zeroed, 1)
            for s in slots:
                rotated(0, s)
            keys_low(0)
            layer_norm(1, step)
            rms_norm(1, step)
            step.end()
            with nc.gpsimd.Fori(0, J - 2) as t:
                step = Steps(pool, p_steps, t)
                body(t, step)
            step.end(J - 2)
            step = Steps(pool, p_steps)
            body(J - 2, step, True, False)
            body(J - 1, step, False, False)
            step.end()

        @block.vector
        def _(v):
            def moments_of_x(t, step):
                moments(nc, v, step, keep["spare"], [(m["stats"][s][:], m["mv"][s][:], row(keep["x"], s, t)) for s in slots], moment)

            def modulated(t, step):
                for s in slots:
                    v.wait_ge(rstd.sem, rstd.now(t, s))
                    step(nc.vector.tensor_scalar(m["xn"][s][:], row(keep["x"], s, t), m["mv"][s][:, 0:1], m["rstd"][s][:],
                                                 ALU.subtract, ALU.mult))
                    step(nc.vector.tensor_tensor(m["xn"][s][:], m["xn"][s][:], keep["shift_scale"][:, s, 1, :], ALU.mult))
                    nc.vector.tensor_tensor(row(keep["r2"], s, t), m["xn"][s][:], keep["shift_scale"][:, s, 0, :], ALU.add).then_inc(h_ready.sem, 1)

            def normed(t):
                for s in slots:
                    v.wait_ge(hrstd.sem, hrstd.now(t, s))
                    nc.vector.tensor_scalar(m["hn"][s][:], row(keep["r2"], s, t), m["hrstd"][s][:], None, ALU.mult).then_inc(hn.sem, 1)

            def low(t, s, pair, ps, got, gone):
                v.wait_ge(got.sem, got.now(t, s))
                nc.vector.tensor_tensor(pair[1], ps, f32(pair[0]), ALU.subtract).then_inc(gone.sem, 1)

            def features_low(t, s):
                low(t, s, flats(m["f"][s]), bk(s, 2)[:, 0:D], f_hi, f_lo)

            def rope(t, s):
                if s == 0:
                    v.wait_ge(rope_in, t * 16 + 16)
                v.wait_ge(qk.sem, qk.now(t, s))
                nc.vector.tensor_tensor(m["work"][s][:, 0, :], bk(s, 1)[:], m["rope"][:, 0, :], ALU.mult)
                split = [x.rearrange("p (h c d) -> p h c d", c=2, d=DK // 2) for x in (m["work"][s][:, 1, :], bk(s, 1)[:], m["rope"][:, 1, :])]
                for c in range(2):
                    last = nc.vector.tensor_tensor(split[0][:, :, c, :], split[1][:, :, 1 - c, :], split[2][:, :, c, :], ALU.mult)
                last.then_inc(terms.sem, 1)

            def gates_and_values(t, s):
                v.wait_ge(tanh.sem, tanh.now(t, s))
                nc.vector.scalar_tensor_tensor(m["sgate"][s][:], m["sgate"][s][:], 1.0, bk(s, 3)[:], ALU.add, ALU.mult).then_inc(sgate.sem, 1)
                low(t, s, [x[:] for x in m["v"][s]], bk(s, 2)[:], v_hi, v_lo)

            def turned_low(t, s):
                low(t, s, flats(m["qkT"][s]), bk(s, 0)[:], qkT_hi, qkT_lo)

            def scores_low(t, s):
                v.wait_ge(s_hi.sem, s_hi.now(t, s))
                nc.vector.tensor_tensor(m["score"][s][1][:].rearrange("p g h i -> p (g h i)"), flat(m["work"][s][:]),
                                        f32(m["score"][s][0][:]).rearrange("p g h i -> p (g h i)"), ALU.subtract).then_inc(s_lo.sem, 1)

            def add_to_state(t, s, step):
                v.wait_ge(st_done.sem, st_done.now(t, s))
                v.wait_ge(s_lo.sem, s_lo.now(t, s))
                step(nc.vector.tensor_tensor(m["work"][s][:, 1, :], bk(s, 1)[:], flat(m["state_mask"][:]), ALU.mult))
                for g in range(HG):
                    last = nc.vector.scalar_tensor_tensor(m["state"][s][:, g, :], m["state"][s][:, g, :], m["state_gain"][:, g:g + 1],
                                                          m["work"][s][:, 1, g * 4 * DV:(g + 1) * 4 * DV], ALU.mult, ALU.add)
                last.then_inc(st_sum.sem, 1)

            def add_to_h(t, s):
                v.wait_ge(proj.sem, proj.now(t, s))
                nc.vector.tensor_tensor(row(keep["r2"], s, t), bk(s, 1)[:, 0:D], row(keep["r2"], s, t), ALU.add).then_inc(r2_out.sem, 1)

            def body(t, step, ahead=True, norms=True):
                cut.scale(v, t)
                for s in slots:
                    v.wait_ge(scores.sem, scores.now(t, s))
                    for h in (2, 3):
                        last = nc.vector.tensor_copy(score_view(m["work"][s])[:, :, h, :], by_head(bk(s, h)))
                    last.then_inc(copied_v.sem, 1)
                for s in slots:
                    if ahead:
                        features_low(t + 1, s)
                    scores_low(t, s)
                for s in slots:
                    add_to_state(t, s, step)
                if norms:
                    moments_of_x(t + 2, step)
                for s in slots:
                    v.wait_ge(square.sem, square.now(t, s))
                    nc.vector.tensor_reduce(m["hsum"][s][:], m["work"][s][:, 0, :].rearrange("p (h d) -> p h d", d=DV), AX.X,
                                            ALU.add).then_inc(hsum.sem, 1)
                    if norms and s == 0:
                        modulated(t + 2, step)
                for s in slots:
                    v.wait_ge(hrms.sem, hrms.now(t, s))
                    heads = lambda x: x.rearrange("p (h d) -> p h d", d=DV)
                    step(nc.vector.tensor_tensor(heads(m["on"][s][:]), heads(bk(s, 0)[:]),
                                                 m["hrms"][s][:].unsqueeze(2).to_broadcast([P, H, DV]), ALU.mult))
                    nc.vector.tensor_tensor(m["on"][s][:], m["on"][s][:], m["sgate"][s][:], ALU.mult).then_inc(on.sem, 1)
                    if ahead:
                        rope(t + 1, s)
                low(t, 0, flats(m["oT"][0]), bk(0, 1)[:], oT_hi, oT_lo)
                if ahead:
                    gates_and_values(t + 1, 0)
                low(t, 1, flats(m["oT"][1]), bk(1, 1)[:], oT_hi, oT_lo)
                if ahead:
                    turned_low(t + 1, 0)
                add_to_h(t, 0)
                if ahead:
                    gates_and_values(t + 1, 1)
                    turned_low(t + 1, 1)
                add_to_h(t, 1)
                if norms:
                    normed(t + 2)
                cut.take_lo(v, t)
            def norms_of(t, step):
                moments_of_x(t, step)
                modulated(t, step)
                normed(t)
            step = Steps(v, v_steps)
            norms_of(0, step)
            for s in slots:
                features_low(0, s)
            for s in slots:
                rope(0, s)
            for s in slots:
                gates_and_values(0, s)
            for s in slots:
                turned_low(0, s)
            norms_of(1, step)
            step.end()
            v.wait_ge(ready, 32)
            v.wait_ge(zeroed, 3 * NS)
            with nc.vector.Fori(0, J - 2) as t:
                step = Steps(v, v_steps, t)
                body(t, step)
            step.end(J - 2)
            step = Steps(v, v_steps)
            body(J - 2, step, True, False)
            body(J - 1, step, False, False)
            step.end()

        @block.scalar
        def _(act):
            def front(t):
                for s in slots:
                    act.wait_ge(h_ready.sem, h_ready.now(t, s))
                    nc.scalar.activation(m["hn"][s][:], row(keep["r2"], s, t), ACT.Square, accum_out=m["sumsq"][s][:]).then_inc(sumsq.sem, 1)

            def high(t, s, hi, src, got, gone):
                act.wait_ge(got.sem, got.now(t, s))
                nc.scalar.copy(hi, src).then_inc(gone.sem, 1)

            def features_high(t, s):
                high(t, s, flat(m["f"][s][0][:]), bk(s, 2)[:, 0:D], hT, f_hi)

            def gates_and_values(t, s, used):
                act.wait_ge(gate.sem, gate.now(t, s))
                if used:
                    act.wait_ge(on.sem, on.now(t - 1, s))
                nc.scalar.activation(m["sgate"][s][:], bk(s, 3)[:], ACT.Tanh, scale=0.5).then_inc(tanh.sem, 1)
                high(t, s, m["v"][s][0][:], bk(s, 2)[:], val, v_hi)

            def keys_high(t, s):
                high(t, s, m["k"][s][0][:], m["rot"][s][:, H * DK:QK], rot, k_hi)

            def turned_high(t, s):
                high(t, s, flat(m["qkT"][s][0][:]), bk(s, 0)[:], qkT, qkT_hi)

            def scores_high(t, s):
                act.wait_ge(masked.sem, masked.now(t, s))
                nc.scalar.copy(m["score"][s][0][:].rearrange("p g h i -> p (g h i)"), flat(m["work"][s][:])).then_inc(s_hi.sem, 1)

            def body(t, ahead=True, norms=True):
                for s in slots:
                    act.wait_ge(scores.sem, scores.now(t, s))
                    for h in (0, 1):
                        last = nc.scalar.copy(score_view(m["work"][s])[:, :, h, :], by_head(bk(s, h)))
                    last.then_inc(copied_a.sem, 1)
                for s in slots:
                    if ahead:
                        features_high(t + 1, s)
                    scores_high(t, s)
                cut.take_hi(act, t)
                for s in slots:
                    act.wait_ge(o_done.sem, o_done.now(t, s))
                    nc.scalar.activation(m["work"][s][:, 0, :], bk(s, 0)[:], ACT.Square).then_inc(square.sem, 1)
                if ahead:
                    for s in slots:
                        act.wait_ge(st_sum.sem, st_sum.now(t, s))
                        nc.scalar.copy(flat(m["S"][s][0][:]), flat(m["state"][s][:])).then_inc(S_hi.sem, 1)
                if norms:
                    front(t + 2)
                if ahead:
                    gates_and_values(t + 1, 0, True)
                    keys_high(t + 1, 0)
                high(t, 0, flat(m["oT"][0][0]), bk(0, 1)[:], oT, oT_hi)
                if ahead:
                    turned_high(t + 1, 0)
                high(t, 1, flat(m["oT"][1][0]), bk(1, 1)[:], oT, oT_hi)
                if ahead:
                    gates_and_values(t + 1, 1, True)
                    keys_high(t + 1, 1)
                    turned_high(t + 1, 1)
            front(0)
            for s in slots:
                features_high(0, s)
            for s in slots:
                gates_and_values(0, s, False)
                keys_high(0, s)
            for s in slots:
                turned_high(0, s)
            front(1)
            with nc.scalar.Fori(0, J - 2) as t:
                body(t)
            body(J - 2, True, False)
            body(J - 1, False, False)

        @block.tensor
        def _(pe):
            def transposes(t, s, ps, src, n, got, gone):
                pe.wait_ge(got.sem, got.now(t, s))
                for c in range(n):
                    last = nc.tensor.transpose(ps[:, c * P:(c + 1) * P], src[s][:, c * P:(c + 1) * P], keep["ident"][:])
                last.then_inc(gone.sem, 1)

            def features(t, s):
                transposes(t, s, bk(s, 2), m["hn"], KC, hn, hT)

            def inward(t, s, which):
                sig = (qk, val, gate)[which]
                product3(nc, bk(s, 1 + which)[:], [([x[:, c, :] for x in m["f"][s]], [w[:, c, which * 512:(which + 1) * 512] for w in keep["w_qkvg"]])
                                                   for c in range(KC)]).then_inc(sig.sem, 1)

            def turned(t, s):
                transposes(t, s, bk(s, 0), m["rot"], 4, rot, qkT)

            def scores_of(t, s):
                pe.wait_ge(qkT_lo.sem, qkT_lo.now(t, s))
                pe.wait_ge(v_lo.sem, v_lo.now(t, s))
                pe.wait_ge(sgate.sem, sgate.now(t, s))
                pe.wait_ge(r2_out.sem, r2_out.before(t, s))
                for g in range(HG):
                    for h in range(4):
                        part = slice(h * DK, (h + 1) * DK)
                        last = product3(nc, bk(s, h)[:, g * P:(g + 1) * P],
                                        [([x[part, 2 + g, :] for x in m["qkT"][s]], [x[part, g, :] for x in m["qkT"][s]])])
                last.then_inc(scores.sem, 1)

            def state_product(t, s):
                pe.wait_ge(k_lo.sem, k_lo.now(t, s))
                pe.wait_ge(copied_a.sem, copied_a.now(t, s))
                for g in range(HG):
                    cols = slice(g * 4 * DV, (g + 1) * 4 * DV)
                    last = product3(nc, bk(s, 1)[:, cols], [([x[:, g * P:(g + 1) * P] for x in m["k"][s]], [x[:, cols] for x in m["v"][s]])])
                last.then_inc(st_done.sem, 1)

            def outward(t, s):
                pe.wait_ge(S_lo.sem, S_lo.before(t, s))
                pe.wait_ge(s_lo.sem, s_lo.now(t, s))
                for g in range(HG):
                    product3(nc, bk(s, 0)[:, g * 4 * DV:(g + 1) * 4 * DV], [([x[:, g, :] for x in m["qkT"][s]], [x[:, g, :] for x in m["S"][s]])],
                             first=g == 0, last=False)
                for n in range(H):
                    g, h = n // 4, n % 4
                    last = product3(nc, bk(s, 0)[:, n * DV:(n + 1) * DV],
                                    [([x[:, g, h, :] for x in m["score"][s]], [x[:, n * DV:(n + 1) * DV] for x in m["v"][s]])],
                                    first=False, last=n == H - 1)
                last.then_inc(o_done.sem, 1)

            def projected(t, s):
                pe.wait_ge(oT_lo.sem, oT_lo.now(t, s))
                product3(nc, bk(s, 1)[:, 0:D], [([x[:, c, :] for x in m["oT"][s]], [w[:, c, :] for w in keep["w_o"]])
                                                for c in range(HV // P)]).then_inc(proj.sem, 1)

            def body(t, ahead=True):
                for s in slots:
                    scores_of(t, s)
                for s in slots:
                    state_product(t, s)
                    if ahead:
                        pe.wait_ge(copied_v.sem, copied_v.now(t, s))
                        features(t + 1, s)
                for s in slots:
                    if ahead:
                        pe.wait_ge(f_lo.sem, f_lo.now(t + 1, s))
                        inward(t + 1, s, 2)
                    outward(t, s)
                for s in slots:
                    pe.wait_ge(st_sum.sem, st_sum.now(t, s))
                    if ahead:
                        inward(t + 1, s, 0)
                        inward(t + 1, s, 1)
                for s in slots:
                    if ahead:
                        pe.wait_ge(terms.sem, terms.now(t + 1, s))
                    transposes(t, s, bk(s, 1), m["on"], 4, on, oT)
                    if ahead and s == 0:
                        turned(t + 1, s)
                projected(t, 0)
                if ahead:
                    turned(t + 1, 1)
                projected(t, 1)
            for s in slots:
                features(0, s)
            for s in slots:
                pe.wait_ge(f_lo.sem, f_lo.now(0, s))
                inward(0, s, 0)
            for s in slots:
                inward(0, s, 2)
                inward(0, s, 1)
            for s in slots:
                turned(0, s)
            pe.wait_ge(zeroed, 3 * NS)
            with nc.tensor.Fori(0, J - 1) as t:
                body(t)
            body(J - 1, False)


def flats(pair):
    return [flat(x if isinstance(x, bass.AP) else x[:]) for x in pair]


def score_view(work):
    return work[:].rearrange("p a n -> p (a n)").rearrange("p (g h i) -> p g h i", g=H // 4, h=4)


def by_head(bank):
    return bank[:, 0:2 * P].rearrange("p (g i) -> p g i", i=P)




def kernel(**inputs):
    import concourse.bacc as _bacc
    from concourse.bass_utils import run_bass_kernel_spmd as _run

    def col(v):
        return np.asarray(v).reshape(KC, P).T

    def rows(w):
        w = np.asarray(w)
        return w.reshape(-1, P, w.shape[-1]).transpose(1, 0, 2)

    def column_pieces(w, n):
        return w.reshape(P, w.shape[1], n, -1).transpose(2, 0, 1, 3)

    def by_group(gate, up):
        return np.concatenate([w[:, g * IW:(g + 1) * IW] for g in range(IG) for w in (gate, up)], axis=1)

    def down_rows(w):
        o = np.zeros((IG, 3 * P, w.shape[-1]), w.dtype)
        o[:, :IW] = w.reshape(IG, IW, -1)
        return rows(o.reshape(IG * 3 * P, -1))

    g = {k: np.asarray(v) for k, v in inputs.items()}
    a = {}
    a["x"] = g["L0_attn_x"]
    a["c"] = np.stack([rows(g[f"L{l}_c"].T) for l in range(2)], axis=1)
    a["wmod"] = np.stack([rows(g[f"L{l}_wmod"]) for l in range(2)])
    a["gate"], a["time_first"] = g["L0_attn_gate"], g["L0_attn_time_first"]
    a["time_decay"] = g["L0_attn_time_decay"].reshape(S, 1)
    a["ln_cols"] = np.stack([col(g["L0_attn_ln_gamma"]), col(g["L0_attn_ln_beta"])], axis=1)
    a["ident"] = np.eye(P, dtype=np.float32)
    a["w_mix"] = rows(g["L0_attn_W_shift"].T).reshape(P, -1)
    a["w_kv"] = rows(np.concatenate([g["L0_attn_W_key"], g["L0_attn_W_value"]], axis=0).T).reshape(P, -1)
    a["w_out0"] = g["L0_attn_W_output"].T
    a["router"] = rows(g["L0_ffn_router_w"]).reshape(P, -1)
    for name, key in (("w_gate", "gate_w"), ("w_up", "up_w")):
        a[name] = column_pieces(rows(g["L0_ffn_" + key].transpose(1, 0, 2).reshape(D, E * FE)), J // 2)
    a["w_down"] = column_pieces(rows(g["L0_ffn_down_w"].reshape(E * FE, D)), J // 2)

    qkvg = np.concatenate([g["L1_attn_" + n] for n in ("q_w", "k_w", "v_w", "g_w")], axis=1)
    a["w_qkvg"] = column_pieces(rows(qkvg), J)
    a["w_o"] = column_pieces(rows(g["L1_attn_o_w"]), J)
    a["norm_cols"] = np.stack([col(g["L1_attn_attn_norm_w"]), col(g["L1_attn_mlp_norm_w"])], axis=1)
    a["gnorm_col"] = np.tile(g["L1_attn_gnorm_w"], 2).reshape(P, 1)
    mlp = g["L1_attn_gate_w"]
    a["w_mlp"] = column_pieces(rows(by_group(mlp[:, :INTER], mlp[:, INTER:])), J)
    a["w_mlp_down"] = column_pieces(down_rows(g["L1_attn_down_w"]), J)
    a["w_ffn"] = column_pieces(rows(by_group(g["L1_ffn_wq_gate"].T, g["L1_ffn_wq_up"].T)), J)
    a["w_ffn_down"] = column_pieces(down_rows(g["L1_ffn_wq_down"].T), J)
    a["s_ffn"] = by_group(g["L1_ffn_s_gate"][None], g["L1_ffn_s_up"][None])[0]
    a["s_ffn_down"] = g["L1_ffn_s_down"]
    a.update(shape_tables())

    nc = _bacc.Bacc("TRN2", target_bir_lowering=False, num_devices=1)
    a = {k: np.ascontiguousarray(v) for k, v in a.items()}
    aps = {k: nc.dram_tensor("in_" + k, v.shape, mybir.dt.from_np(v.dtype), kind="ExternalInput").ap() for k, v in a.items()}
    out = nc.dram_tensor("out_0", (B, T, D), F32, kind="ExternalOutput").ap()
    build(nc, aps, out)
    r = _run(nc, [{"in_" + k: v for k, v in a.items()}], core_ids=[0])
    return r.results[0]["out_0"]


def shape_tables():
    gamma = 1.0 - np.exp2(-5.0 - np.arange(H, dtype=np.float64))
    i = np.arange(P, dtype=np.float64)[:, None]
    q_gain = gamma ** (i + 1) * DK ** -0.5
    k_gain = gamma ** -(i + 1)
    inv_freq = (np.float32(1.0) / np.float32(10000.0) ** (np.arange(0, DK, 2, dtype=np.float32) / np.float32(DK))).astype(np.float32)
    angle = np.arange(T, dtype=np.float32)[:, None] * inv_freq
    cos = np.cos(angle.astype(np.float64)).reshape(J, P, 1, DK // 2)
    sin = np.sin(angle.astype(np.float64)).reshape(J, P, 1, DK // 2)
    full_cos = np.concatenate([cos, cos], axis=-1)
    full_sin = np.concatenate([-sin, sin], axis=-1)
    table = np.stack([np.concatenate([f * q_gain[None, :, :, None], f * k_gain[None, :, :, None]], axis=2)
                      for f in (full_cos, full_sin)], axis=2)
    tile_decay = gamma ** P
    state_mask = np.zeros((4, DK, 2, 4, DV))
    state_gain = np.zeros((4, DK, 2))
    for grp in range(2):
        for h in range(4):
            state_mask[h, :, grp, h, :] = tile_decay[grp * 4 + h]
            state_gain[h, :, grp] = tile_decay[grp * 4 + h]
    return {"iota": np.arange(E, dtype=np.float32), "rope": table.reshape(J, P, 2, 2 * H * DK).astype(np.float32),
            "state_mask": state_mask.reshape(P, 2, 4 * DV).astype(np.float32),
            "state_gain": state_gain.reshape(P, 2).astype(np.float32)}
```
